# Optimizing a Trainium2 kernel written in Bass

```python
import numpy as np
import jax
import jax.numpy as jnp

def _softmax(x, axis=-1):
    return jax.nn.softmax(x, axis=axis)

def _gelu(x):
    return jax.nn.gelu(x, approximate=True)

def _silu(x):
    return jax.nn.silu(x)

def _sigmoid(x):
    return jax.nn.sigmoid(x)

def _layernorm(x, axis=-1, eps=1e-05):
    m = jnp.mean(x, axis=axis, keepdims=True)
    v = jnp.var(x, axis=axis, keepdims=True)
    return (x - m) / jnp.sqrt(v + eps)

def _scatter_add(tgt, idx, src, axis=0):
    return tgt.at[idx].add(src)

def _segment_sum(src, seg, n):
    return jax.ops.segment_sum(src, seg, n)
kernel_name = 'mk_perceiver_d1_seqx_r2_034023'

def setup_inputs(seed: int=0):
    np.random.seed(seed)
    _w = jnp.asarray

    def _rec_inputs():
        import jax
        import jax.numpy as jnp
        _rk = jax.random.key(seed)
        x = 7.22e-05 + 1 * jax.random.normal(jax.random.fold_in(_rk, 1), (32, 32, 512), jnp.float32)
        _lenS = 32 - jax.random.randint(jax.random.fold_in(_rk, 7), (32,), 0, max(1, 32 // 4) + 1, jnp.int32)
        _lenS2 = 257 - jax.random.randint(jax.random.fold_in(_rk, 8), (32,), 0, max(1, 257 // 4) + 1, jnp.int32)
        _ctx_1024P = jax.random.normal(jax.random.fold_in(_rk, 11), (32, 16, 512), jnp.float32)
        _ctx_1024c = jax.random.dirichlet(jax.random.fold_in(_rk, 511), 0.3 * jnp.ones((16,), jnp.float32), (32, 257))
        _ctx_1024t = jnp.einsum('bsk,bkd->bsd', _ctx_1024c, _ctx_1024P)
        _ctx_1024t = _ctx_1024t * jax.lax.rsqrt(jnp.mean(jnp.square(_ctx_1024t)) + 1e-12) * 0.953939
        ctx_1024 = 4.13588e-05 + 0.999923 * (_ctx_1024t + 0.3 * jax.random.normal(jax.random.fold_in(_rk, 611), (32, 257, 512), jnp.float32))
        return (x, ctx_1024)
    x, ctx_1024 = _rec_inputs()

    def _L0_xattn_setup():
        import jax, jax.numpy as jnp
        import numpy as np
        D = 512
        H = 16
        HD = D // H
        key = jax.random.key(seed)
        ks = jax.random.split(key, 11)
        B, T = (4, 1024)
        s = 1.0 / np.sqrt(D)
        inp = {'q': jax.random.normal(ks[0], (B, T, D), jnp.float32), 'k': jax.random.normal(ks[1], (B, T, D), jnp.float32), 'v': jax.random.normal(ks[2], (B, T, D), jnp.float32), 'Wq': jax.random.normal(ks[3], (D, D), jnp.float32) * s, 'bq': jnp.zeros((D,), jnp.float32), 'Wk': jax.random.normal(ks[4], (D, D), jnp.float32) * s, 'bk': jnp.zeros((D,), jnp.float32), 'Wv': jax.random.normal(ks[5], (D, D), jnp.float32) * s, 'bv': jnp.zeros((D,), jnp.float32), 'Wo': jax.random.normal(ks[6], (D, D), jnp.float32) * s, 'bo': jnp.zeros((D,), jnp.float32)}
        return inp
    _L0_xattn_all = _L0_xattn_setup()
    _L0_xattn_in = {k: v for k, v in _L0_xattn_all.items() if k in ('Wq', 'bq', 'Wk', 'bk', 'Wv', 'bv', 'Wo', 'bo')}
    del _L0_xattn_all

    def _L0_attn_setup():
        import jax, jax.numpy as jnp
        import numpy as np
        B, N, DIM, H = (8, 2048, 512, 16)
        D = DIM // H
        EPS_NORM = 1e-12
        EPS_PI = 1e-08
        key = jax.random.key(seed)
        k1, k2, k3 = jax.random.split(key, 3)
        x = jax.random.normal(k1, (B, N, DIM), dtype=jnp.float32)
        Wqkv = jax.random.normal(k2, (DIM, DIM), dtype=jnp.float32) * (1.0 / np.sqrt(DIM))
        temp = jnp.ones((H, 1), dtype=jnp.float32)
        Wout = jax.random.normal(k3, (DIM, DIM), dtype=jnp.float32) * (1.0 / np.sqrt(DIM))
        bout = jnp.zeros((DIM,), dtype=jnp.float32)
        return {'x': x, 'Wqkv': Wqkv, 'temp': temp, 'Wout': Wout, 'bout': bout}
    _L0_attn_all = _L0_attn_setup()
    _L0_attn_in = {k: v for k, v in _L0_attn_all.items() if k in ('Wqkv', 'temp', 'Wout', 'bout')}
    del _L0_attn_all

    def _L0_ffn_setup():
        import jax, jax.numpy as jnp
        import numpy as np
        B, S, D = (2, 1024, 512)
        H, E, P, K = (8, 8, 128, 2)
        SCALE = 1.0 / np.sqrt(P)

        def _get_sel_gate(x, w, route_scale):
            logits = jnp.einsum('bsd,ed->bse', x, w).astype(jnp.float32)
            raw = logits.reshape(x.shape[0], x.shape[1], H, E)
            probs = jax.nn.sigmoid(raw)
            vals, idx = jax.lax.top_k(probs, K)
            vals = vals / jnp.clip(vals.sum(-1, keepdims=True), 1e-09)
            vals = vals * route_scale
            gate = (jax.nn.one_hot(idx, E, dtype=vals.dtype) * vals[..., None]).sum(-2)
            return gate
        key = jax.random.key(seed)
        ks = jax.random.split(key, 8)
        std = 1.0 / np.sqrt(D)
        return {'x': jax.random.normal(ks[0], (B, S, D), jnp.float32), 'q_w': jax.random.normal(ks[1], (H * P, D), jnp.float32) * std, 'k_w': jax.random.normal(ks[2], (H * P, D), jnp.float32) * std, 'v_w': jax.random.normal(ks[3], (H * E, D, P), jnp.float32) * std, 'o_w': jax.random.normal(ks[4], (H * E, P, D), jnp.float32) * (1.0 / np.sqrt(H * P)), 'sel_v_w': jax.random.normal(ks[5], (H * E, D), jnp.float32) * std, 'sel_o_w': jax.random.normal(ks[6], (H * E, D), jnp.float32) * std, 'route_scale': jnp.ones((1,), jnp.float32)}
    _L0_ffn_all = _L0_ffn_setup()
    _L0_ffn_in = {k: v for k, v in _L0_ffn_all.items() if k in ('q_w', 'k_w', 'v_w', 'o_w', 'sel_v_w', 'sel_o_w', 'route_scale')}
    del _L0_ffn_all
    return {'x': x, 'ctx_1024': ctx_1024, 'L0_xattn_Wq': _L0_xattn_in['Wq'], 'L0_xattn_bq': _L0_xattn_in['bq'], 'L0_xattn_Wk': _L0_xattn_in['Wk'], 'L0_xattn_bk': _L0_xattn_in['bk'], 'L0_xattn_Wv': _L0_xattn_in['Wv'], 'L0_xattn_bv': _L0_xattn_in['bv'], 'L0_xattn_Wo': _L0_xattn_in['Wo'], 'L0_xattn_bo': _L0_xattn_in['bo'], 'L0_attn_Wqkv': _L0_attn_in['Wqkv'], 'L0_attn_temp': _L0_attn_in['temp'], 'L0_attn_Wout': _L0_attn_in['Wout'], 'L0_attn_bout': _L0_attn_in['bout'], 'L0_ffn_q_w': _L0_ffn_in['q_w'], 'L0_ffn_k_w': _L0_ffn_in['k_w'], 'L0_ffn_v_w': _L0_ffn_in['v_w'], 'L0_ffn_o_w': _L0_ffn_in['o_w'], 'L0_ffn_sel_v_w': _L0_ffn_in['sel_v_w'], 'L0_ffn_sel_o_w': _L0_ffn_in['sel_o_w'], 'L0_ffn_route_scale': _L0_ffn_in['route_scale']}

def reference(x, ctx_1024, L0_xattn_Wq, L0_xattn_bq, L0_xattn_Wk, L0_xattn_bk, L0_xattn_Wv, L0_xattn_bv, L0_xattn_Wo, L0_xattn_bo, L0_attn_Wqkv, L0_attn_temp, L0_attn_Wout, L0_attn_bout, L0_ffn_q_w, L0_ffn_k_w, L0_ffn_v_w, L0_ffn_o_w, L0_ffn_sel_v_w, L0_ffn_sel_o_w, L0_ffn_route_scale):
    import jax
    import jax.numpy as jnp

    def _L0_xattn_ref(q, k, v, Wq, bq, Wk, bk, Wv, bv, Wo, bo):
        import jax, jax.numpy as jnp
        import numpy as np
        D = 512
        H = 16
        HD = D // H
        B, Tq, _ = q.shape
        Tk = k.shape[1]
        qw = q @ Wq + bq
        kw = k @ Wk + bk
        vw = v @ Wv + bv
        qh = qw.reshape(B, Tq, H, HD)
        kh = kw.reshape(B, Tk, H, HD)
        vh = vw.reshape(B, Tk, H, HD)
        scale = 1.0 / np.sqrt(HD).astype(np.float32)
        logits = jnp.einsum('bqhd,bkhd->bhqk', qh, kh) * scale
        causal = jnp.tril(jnp.ones((Tq, Tk), bool))
        logits = jnp.where(causal, logits, -jnp.inf)
        attn = jax.nn.softmax(logits, axis=-1)
        out = jnp.einsum('bhqk,bkhd->bqhd', attn, vh).reshape(B, Tq, D)
        return out @ Wo + bo

    def _L0_attn_ref(x, Wqkv, temp, Wout, bout):
        import jax, jax.numpy as jnp
        import numpy as np
        B, N, DIM, H = (8, 2048, 512, 16)
        D = DIM // H
        EPS_NORM = 1e-12
        EPS_PI = 1e-08
        b, n, dim = x.shape
        h, d = (H, dim // H)
        w = (x @ Wqkv.T).reshape(b, n, h, d).transpose(0, 2, 1, 3)
        norm = jnp.sqrt(jnp.sum(w * w, axis=-2, keepdims=True))
        w_normed = w / jnp.maximum(norm, EPS_NORM)
        logits = jnp.sum(w_normed * w_normed, axis=-1) * temp[None, :, :]
        Pi = jax.nn.softmax(logits, axis=1)
        Pi_norm = Pi / (jnp.sum(Pi, axis=-1, keepdims=True) + EPS_PI)
        dots = jnp.einsum('bhn,bhnd->bhd', Pi_norm, w * w)
        attn = 1.0 / (1.0 + dots)
        out = -(w * Pi[..., None]) * attn[:, :, None, :]
        out = out.transpose(0, 2, 1, 3).reshape(b, n, dim)
        return out @ Wout.T + bout

    def _L0_ffn_ref(x, q_w, k_w, v_w, o_w, sel_v_w, sel_o_w, route_scale):
        import jax, jax.numpy as jnp
        import numpy as np
        B, S, D = (2, 1024, 512)
        H, E, P, K = (8, 8, 128, 2)
        SCALE = 1.0 / np.sqrt(P)

        def _get_sel_gate(x, w, route_scale):
            logits = jnp.einsum('bsd,ed->bse', x, w).astype(jnp.float32)
            raw = logits.reshape(x.shape[0], x.shape[1], H, E)
            probs = jax.nn.sigmoid(raw)
            vals, idx = jax.lax.top_k(probs, K)
            vals = vals / jnp.clip(vals.sum(-1, keepdims=True), 1e-09)
            vals = vals * route_scale
            gate = (jax.nn.one_hot(idx, E, dtype=vals.dtype) * vals[..., None]).sum(-2)
            return gate
        rs = route_scale[0]
        gate_v = _get_sel_gate(x, sel_v_w, rs)
        gate_o = _get_sel_gate(x, sel_o_w, rs)
        q = jnp.einsum('bsd,hpd->bhsp', x, q_w.reshape(H, P, D))
        k = jnp.einsum('bsd,hpd->bhsp', x, k_w.reshape(H, P, D))
        xv = jnp.einsum('bsd,hedp->bshep', x, v_w.reshape(H, E, D, P))
        v = jnp.einsum('bshep,bshe->bhsp', xv, gate_v)
        att = jax.nn.softmax(jnp.einsum('bhqp,bhkp->bhqk', q, k) * SCALE, axis=-1)
        ctx = jnp.einsum('bhqk,bhkp->bqhp', att, v)
        weighted = ctx[:, :, :, None, :] * gate_o[..., None]
        out = jnp.einsum('bshep,hepd->bsd', weighted, o_w.reshape(H, E, P, D))
        return out
    x = x + _L0_xattn_ref(_layernorm(x, axis=-1), ctx_1024, ctx_1024, L0_xattn_Wq, L0_xattn_bq, L0_xattn_Wk, L0_xattn_bk, L0_xattn_Wv, L0_xattn_bv, L0_xattn_Wo, L0_xattn_bo)
    x = x + _L0_attn_ref(_layernorm(x, axis=-1), L0_attn_Wqkv, L0_attn_temp, L0_attn_Wout, L0_attn_bout)
    x = x + _L0_ffn_ref(_layernorm(x, axis=-1), L0_ffn_q_w, L0_ffn_k_w, L0_ffn_v_w, L0_ffn_o_w, L0_ffn_sel_v_w, L0_ffn_sel_o_w, L0_ffn_route_scale)
    return x

_drawn_inputs = setup_inputs


def setup_inputs(seed=0):
    import zlib

    import numpy as np

    out = dict(_drawn_inputs(seed))
    spreads = {'L0_xattn_bq': (0.0, 0.1),
     'L0_xattn_bk': (0.0, 0.8),
     'L0_xattn_bv': (0.0, 0.1),
     'L0_xattn_bo': (0.0, 0.1),
     'L0_attn_temp': (1.0, 0.6),
     'L0_attn_bout': (0.0, 0.1)}
    factors = {}
    for name, (base, spread) in spreads.items():
        noise = np.random.default_rng([zlib.crc32(name.encode()), seed]).standard_normal(out[name].shape)
        drawn = base * np.exp(spread * noise) if base else spread * noise
        out[name] = jnp.asarray(drawn.astype(out[name].dtype))
    for name, factor in factors.items():
        out[name] = (out[name] * factor).astype(out[name].dtype)
    return out
```

```python
from contextlib import ExitStack

import concourse.bass as bass
from concourse import mybir

F32 = mybir.dt.float32
F16 = mybir.dt.float16
ALU = mybir.AluOpType
ACT = mybir.ActivationFunctionType
AX = mybir.AxisListType

P = 128
B, T, D = 32, 32, 512
N = B * T
KD = D // P
NT = N // P
HALF = N // 2
TH = NT // 2
BH = B // 2
XH, XD = 16, 32
HJ = XH // KD
FH, E = 8, 8
EC = E // 2
WSCALE = 64.0
ASCALE = 16.0
MASKED = -1.0e30
LN_EPS = 1e-5

ACC, SPLIT, TURN = 4, 2, 2
ACC_BODY = 4 + 2 * NT + NT


def front_order():
    acc, split, turn = [], [], []
    for f in range(2):
        acc += [("k", f, c) for c in range(KD)] + [("v", f, t) for t in range(TH)]
        split += [("x1", f, t) for t in range(TH)]
        acc += [("q", f, c) for c in range(KD)]
    for f in range(2):
        for kind, a in attention_order():
            if kind == "scores":
                acc.append(("s", f, a))
            elif kind == "turn":
                turn.append(("p", f, a))
            elif kind == "values":
                acc.append(("pv", f, a))
            elif kind == "turn_out":
                split.append(("at", f, a))
            else:
                acc.append(("wo", f, a))
    for f in range(2):
        split += [("x2", f, t) for t in range(TH)]
        acc += [("w", f, c) for c in range(KD)]
    for f in range(2):
        acc.append(("lg", f))
        turn.append(("pi", f))
        acc += [("pb", f, c) for c in range(KD)]
    for f in range(2):
        acc += [("wout", f, t) for t in range(TH)]
        split += [("x3", f, t) for t in range(TH)]
    for f in range(2):
        acc += [("gl", f, t) for t in range(TH)]
        turn.append(("go", f))
    return acc, split, turn


def attention_order():
    units = 4 * TH
    for n in range(units + 7):
        if n < units:
            yield "scores", n
        if n >= 4 and n % 2 == 0 and (n - 4) // 2 < units // 2:
            yield "values", (n - 4) // 2
        if 2 <= n < units + 2:
            yield "turn", n - 2
        if n >= 8 and n % 4 == 0 and (n - 8) // 4 < TH:
            yield "turn_out", (n - 8) // 4
        if n >= 10 and n % 4 == 2 and (n - 10) // 4 < TH:
            yield "project", (n - 10) // 4


_ACC, _SPLIT, _TURN = front_order()
ACC_AT = {k: n for n, k in enumerate(_ACC)}
SPLIT_AT = {k: n for n, k in enumerate(_SPLIT)}
TURN_AT = {k: n for n, k in enumerate(_TURN)}
assert len(_SPLIT) % SPLIT == 0 and len(_TURN) % TURN == 0 and ACC_BODY % ACC == 0


def acc_at(kind, h, n):
    off = {"qk": 0, "xv": 4, "out": 4 + 2 * NT}[kind] + n
    if kind == "out":
        h = h + 1
        if isinstance(h, int) and h == FH:
            return len(_ACC) + (4 + 2 * NT) + (FH - 1) * ACC_BODY + n
    if isinstance(h, int) and h == 0:
        return len(_ACC) + off
    return h * ACC_BODY + (len(_ACC) + (4 + 2 * NT) - ACC_BODY + off)


def acc_bank(kind, n):
    off = {"qk": 0, "xv": 4, "out": 4 + 2 * NT}[kind] + n
    return (len(_ACC) + off) % ACC


def split_at(h, f):
    return h * 2 + (len(_SPLIT) + f)


def turn_at(kind, h, f):
    return h * 4 + (len(_TURN) + {"p": 0, "ctx": 2}[kind] + f)


def perceiver_kernel(nc, x, ctx_t, wk, wv, wq, wo, wqkv_t, wout_t, sel_v_t, sel_o_t,
                     qk_t, v_w, o_w, bq, bk, bv, bo, bout, temp, route_scale, out, gate_dram):
    ctx = ExitStack()
    with ctx:
        def sb(name, shape, dt=F32):
            return ctx.enter_context(nc.sbuf_tensor(name, shape, dt))

        def sem(name):
            return ctx.enter_context(nc.semaphore(name))

        KB = 256
        r_stage = sb("r_stage", [P, 16 * KB])
        r_split = sb("r_split", [P, 16 * KB])
        r_qk = sb("r_qk", [P, 32 * KB])
        r_mid = sb("r_mid", [P, 32 * KB])
        r_w = sb("r_w", [P, 32 * KB])
        r_v = sb("r_v", [P, NT * XH * (XD + 1)])
        r_s = sb("r_s", [P, 4 * KB])
        r_p = sb("r_p", [P, 4 * KB])
        r_pt = sb("r_pt", [P, 4 * KB])
        r_att = sb("r_att", [P, 4 * KB])

        xres = sb("xres", [P, NT, D])
        xt_split = sb("xt_split", [P, 16 * KB])
        xn = sb("xn", [P, 2, D])
        bo_row = sb("bo_row", [P, D])
        ident = sb("ident", [P, P])
        mask_causal = sb("mask_causal", [P, P])
        mask_batch = sb("mask_batch", [P, P])
        head_sum = sb("head_sum", [P, KD, XH])
        bias_cols = sb("bias_cols", [P, 2, KD])
        temp_row = sb("temp_row", [P, XH])
        rs_col = sb("rs_col", [P, 1])
        ramp = sb("ramp", [P, E])
        stats = sb("stats", [P, TH, 6])
        mv = sb("mv", [P, TH, 2])
        var = sb("var", [P, TH])
        rstd = sb("rstd", [P, TH])
        nw = sb("nw", [P, TH])
        smax = sb("smax", [P, 2, 4])
        ssum = sb("ssum", [P, 2, 4])
        rinv = sb("rinv", [P, 8])
        gsm = sb("gsm", [P, 5, TH * 2 * FH])
        bsm = sb("bsm", [P, 4, KD, BH])
        gate_h = sb("gate_h", [P, NT, E])

        def half_view(region, off, shape, names, **kw):
            size = 1
            for s in shape:
                size *= s
            return region[:, off * KB:].bitcast(F16)[:, 0:size].rearrange(names, **kw)

        def words(region, off, size):
            return region[:, off:off + size]

        ctx_stage = r_stage[:, :].rearrange("p (k n) -> p k n", k=KD)
        ctx_hl = [half_view(r_split, 8 * s, (KD, N), "p (k n) -> p k n", k=KD) for s in range(2)]
        wstage4 = [words(r_mid, 8 * KB * s, 8 * KB).rearrange("p (k n) -> p k n", k=KD) for s in range(4)]
        wstage2 = [words(r_stage, 8 * KB * s, 8 * KB).rearrange("p (k n) -> p k n", k=KD) for s in range(2)]
        sel_stage = words(r_att, 0, KD * P).rearrange("p (k n) -> p k n", k=KD)
        w_hl = [[half_view(r_w, 8 * s + 4 * z, (KD, D), "p (k n) -> p k n", k=KD) for z in range(2)]
                for s in range(4)]
        sel_hl = [half_view(r_w, 16 + 4 * z, (KD, P), "p (k n) -> p k n", k=KD) for z in range(2)]
        xt_hl = [half_view(xt_split, 8 * s, (KD, N), "p (k n) -> p k n", k=KD) for s in range(2)]
        qT = words(r_qk, 0, 16 * KB).rearrange("p (c n) -> p c n", c=KD)
        kT = words(r_qk, 16 * KB, 16 * KB).rearrange("p (c n) -> p c n", c=KD)
        bv_row = words(r_s, 2 * KB, D)
        vones = r_v[:, :].rearrange("p (t h d) -> p t h d", t=NT, h=XH)
        sbuf = [words(r_s, 2 * KB * s, D) for s in range(2)]
        pbuf = [words(r_p, 2 * KB * s, D) for s in range(2)]
        ptbuf = [words(r_pt, 2 * KB * s, D) for s in range(2)]
        attn = [words(r_att, 2 * KB * s, D) for s in range(2)]
        wT = words(r_mid, 0, 16 * KB).rearrange("p (c n) -> p c n", c=KD)
        sqT = words(r_mid, 16 * KB, 16 * KB).rearrange("p (c n) -> p c n", c=KD)
        wn2 = words(r_qk, 0, 16 * KB).rearrange("p (c n) -> p c n", c=KD)
        head_spread = words(r_qk, 16 * KB, KD * P).rearrange("p (c j) -> p c j", c=KD)
        piT = [words(r_qk, (18 + 2 * f) * KB, D) for f in range(2)]
        pi = [words(r_qk, 22 * KB + 64 * f, TH * XH).rearrange("p (t h) -> p t h", t=TH) for f in range(2)]
        gates = words(r_att, 0, NT * 2 * FH * E).rearrange("p (t g) -> p t g", t=NT)
        goT = r_pt[0:FH * E, :]
        stage_v = r_stage[:, :].rearrange("p (c n) -> p c n", c=2)
        v_hl = [half_view(r_split, 8 * z, (2, KD, EC * P), "p (c k n) -> p c k n", c=2, k=KD) for z in range(2)]
        o_hl = [half_view(r_w, 8 * z, (E, D), "p (e n) -> p e n", e=E) for z in range(2)]
        o_hl_last = [half_view(r_split, 8 * z, (E, D), "p (e n) -> p e n", e=E) for z in range(2)]
        prod = [words(r_w, (16 + 4 * s) * KB, E * P).rearrange("p (e n) -> p e n", e=E) for s in range(2)]
        ctxT = words(r_w, 24 * KB, N)
        v_head = words(r_w, 28 * KB, NT * P).rearrange("p (t d) -> p t d", t=NT)
        stage_qk = words(r_v, 0, 4 * KB)
        qk_hl = [half_view(r_v, 4 + 2 * z, (2, KD, P), "p (m k n) -> p m k n", m=2, k=KD) for z in range(2)]
        qkT = words(r_v, 8 * KB, 8 * KB).rearrange("p (m n) -> p m n", m=2)
        gate_b = r_qk[:, :].rearrange("p (e n) -> p e n", e=E)
        gated = [half_view(r_mid, 16 * z, (NT, E, P), "p (t e n) -> p t e n", t=NT, e=E) for z in range(2)]

        psum = [ctx.enter_context(nc.psum_tensor(f"bank{i}", [P, 512], F32)) for i in range(8)]

        def accb(n):
            return psum[n % ACC]

        def splitb(n):
            return psum[ACC + n % SPLIT]

        def turnb(n):
            return psum[ACC + SPLIT + n % TURN]

        ld_ctx = [sem(f"ld_ctx{f}") for f in range(2)]
        ld_w = [sem(f"ld_w{i}") for i in range(7)]
        ld_x = [sem(f"ld_x{t}") for t in range(NT)]
        ld_bias, ld_bv, ld_bo, ld_bout = sem("ld_bias"), sem("ld_bv"), sem("ld_bo"), sem("ld_bout")
        ld_exp, ld_qk, ld_gate = sem("ld_exp"), sem("ld_qk"), sem("ld_gate")
        gate_stored, out_stored = sem("gate_stored"), sem("out_stored")
        cst, consts_ready, ones_ready, spread_ready = sem("cst"), sem("consts_ready"), sem("ones_ready"), sem("spread_ready")
        headsum_ready = sem("headsum_ready")
        acc_ready, acc_free = sem("acc_ready"), sem("acc_free")
        split_ready, split_hi, split_free = sem("split_ready"), sem("split_hi"), sem("split_free")
        turn_ready, turn_free = sem("turn_ready"), sem("turn_free")
        w_hi, w_lo = sem("w_hi"), sem("w_lo")
        var_ready, std_ready, xn_ready, bias_added = sem("var_ready"), sem("std_ready"), sem("xn_ready"), sem("bias_added")
        max_ready, sub_ready, exp_ready, att_ready = sem("max_ready"), sem("sub_ready"), sem("exp_ready"), sem("att_ready")
        rsum_ready, norm_ready = sem("rsum_ready"), sem("norm_ready")
        sq_ready, inv_ready, wn2_ready = sem("sq_ready"), sem("inv_ready"), sem("wn2_ready")
        lmax_ready, lexp_ready, pi_ready = sem("lmax_ready"), sem("lexp_ready"), sem("pi_ready")
        z_ready, z_hi, z_lo = sem("z_ready"), sem("z_hi"), sem("z_lo")
        rl_ready, prob_ready, gates_ready = sem("rl_ready"), sem("prob_ready"), sem("gates_ready")
        vw_hi, vw_lo, ow_hi, ow_lo = sem("vw_hi"), sem("vw_lo"), sem("ow_hi"), sem("ow_lo")
        vhead_ready = sem("vhead_ready")
        prod_ready, gated_hi, gated_lo = sem("prod_ready"), sem("gated_hi"), sem("gated_lo")
        dve_step, pool_step = sem("dve_step"), sem("pool_step")

        SPLITS = ["ctx0", "wk", "wv", "ctx1", "wq", "wo", "wqkv", "wout", "sel"]

        def split_count(name):
            return SPLITS.index(name) + 1

        def split_operands(name):
            if name == "ctx0" or name == "ctx1":
                f = int(name[3])
                n = slice(f * HALF, (f + 1) * HALF)
                return ctx_stage[:, :, n], [c[:, :, n] for c in ctx_hl], 1.0, ld_ctx[f], 16
            i = ["wk", "wv", "wq", "wo", "wqkv", "wout", "sel"].index(name)
            if name == "sel":
                return sel_stage, sel_hl, WSCALE, ld_w[6], 32
            src = wstage4[i] if i < 4 else wstage2[i - 4]
            slot = {"wk": 0, "wv": 1, "wq": 2, "wo": 3, "wqkv": 0, "wout": 1}[name]
            return src, w_hl[slot], WSCALE, ld_w[i], 16

        block = ctx.enter_context(nc.Block())

        @block.sync
        def _(sp):
            ctx_v = ctx_t.rearrange("(k p) n -> p k n", p=P)

            def weight(w):
                return w.rearrange("(k p) n -> p k n", p=P)

            sp.dma_start(ctx_stage[:, :, 0:HALF], ctx_v[:, :, 0:HALF]).then_inc(ld_ctx[0], 16)
            sp.dma_start(wstage4[0], weight(wk)).then_inc(ld_w[0], 16)
            sp.dma_start(wstage4[1], weight(wv)).then_inc(ld_w[1], 16)
            sp.dma_start(ctx_stage[:, :, HALF:N], ctx_v[:, :, HALF:N]).then_inc(ld_ctx[1], 16)
            sp.dma_start(wstage4[2], weight(wq)).then_inc(ld_w[2], 16)
            sp.dma_start(wstage4[3], weight(wo)).then_inc(ld_w[3], 16)
            sp.wait_ge(w_lo, split_count("ctx1"))
            sp.dma_start(wstage2[0], weight(wqkv_t)).then_inc(ld_w[4], 16)
            sp.dma_start(wstage2[1], weight(wout_t)).then_inc(ld_w[5], 16)
            sp.wait_ge(w_lo, split_count("wout"))
            sp.dma_start(r_stage[:, :], v_w[0]).then_inc(ld_exp, 16)
            sp.wait_ge(bias_added, NT)
            sp.dma_start(bo_row[:, :], bout.partition_broadcast(P)).then_inc(ld_bout, 16)
            sp.wait_ge(split_ready, SPLIT_AT["at", 1, TH - 1] + 1)
            sp.dma_start(sel_stage[:, :, 0:FH * E], weight(sel_v_t)).then_inc(ld_w[6], 16)
            sp.dma_start(sel_stage[:, :, FH * E:P], weight(sel_o_t)).then_inc(ld_w[6], 16)
            sp.wait_ge(acc_ready, ACC_AT["pv", 1, 2 * TH - 1] + 1)
            sp.dma_start(stage_qk, qk_t[0]).then_inc(ld_qk, 16)
            sp.wait_ge(turn_free, TURN_AT["go", 1] + 1)
            sp.dma_start(gate_dram, goT).then_inc(gate_stored, 16)
            sp.wait_ge(gate_stored, 16)
            sp.dma_start(gate_b, gate_dram[0:E, :].partition_broadcast(P)).then_inc(ld_gate, 16)
            sp.wait_ge(vw_lo, 3)
            sp.dma_start(r_stage[:, :], v_w[1]).then_inc(ld_exp, 16)
            sp.dma_start(stage_qk, qk_t[1]).then_inc(ld_qk, 16)

            def step(h, last=False):
                sp.wait_ge(vw_lo, 3 * (h + 1))
                sp.dma_start(r_stage[:, :], o_w[bass.ds(h - 1, 1)][0] if not isinstance(h, int) else o_w[h - 1])\
                    .then_inc(ld_exp, 16)
                sp.wait_ge(prod_ready, NT * h)
                g = gate_dram[bass.ds(h * E, E), :]
                sp.dma_start(gate_b, g.partition_broadcast(P)).then_inc(ld_gate, 16)
                sp.wait_ge(ow_lo, 2 * h)
                if not last:
                    sp.dma_start(r_stage[:, :], v_w[bass.ds(h + 1, 1)][0]).then_inc(ld_exp, 16)
                    sp.dma_start(stage_qk, qk_t[bass.ds(h + 1, 1)][0]).then_inc(ld_qk, 16)
                else:
                    sp.dma_start(r_stage[:, :], o_w[h]).then_inc(ld_exp, 16)

            with sp.Fori(1, FH - 1) as h:
                step(h)
            step(FH - 1, last=True)
            out_v = out.rearrange("(t p) d -> t p d", p=P)
            for t in range(NT):
                sp.wait_ge(acc_free, acc_at("out", FH - 1, t) + 1)
                sp.dma_start(out_v[t], xres[:, t, :]).then_inc(out_stored, 16)
            sp.wait_ge(out_stored, 16 * NT)

        @block.gpsimd
        def _(pool):
            steps = [0]

            def link(ins):
                steps[0] += 1
                ins.then_inc(pool_step, 1)
                pool.wait_ge(pool_step, steps[0])

            def select(view, pattern, base, mult, op, fill):
                return pool.affine_select(out=view, in_=view, pattern=pattern, compare_op=op, fill=fill,
                                          base=base, channel_multiplier=mult)

            link(pool.memset(ident[:, :], 0.0))
            link(pool.memset(mask_causal[:, :], 0.0))
            link(pool.memset(mask_batch[:, :], 0.0))
            link(select(ident[:, :], [[-1, P]], 0, 1, ALU.not_equal, 1.0))
            pool.memset(vones[:, :, :, XD:XD + 1], 1.0).then_inc(ones_ready, 1)
            blocks = [[0, P // T], [0, T]]
            mc = mask_causal[:, :].rearrange("p (b j) -> p b j", b=P // T)
            mb = mask_batch[:, :].rearrange("p (b j) -> p b j", b=P // T)
            link(select(mc, [[-T, P // T], [-1, T]], 0, 1, ALU.is_ge, MASKED))
            link(select(mc, [[T, P // T], [0, T]], T - 1, -1, ALU.is_ge, MASKED))
            link(select(mb, [[-T, P // T], [0, T]], 0, 1, ALU.is_ge, MASKED))
            link(select(mb, [[T, P // T], [0, T]], T - 1, -1, ALU.is_ge, MASKED))
            link(pool.memset(head_sum[:, :, :], 1.0))
            link(select(head_sum[:, :, :], [[P, KD], [-XD, XH]], 0, 1, ALU.is_ge, 0.0))
            link(select(head_sum[:, :, :], [[-P, KD], [XD, XH]], XD - 1, -1, ALU.is_ge, 0.0))
            for e in range(E):
                last = pool.memset(ramp[:, e:e + 1], float(E - e))
            link(last)
            pool.wait_ge(ld_bias, 16 * 4)
            pool.tensor_tensor(head_sum[:, :, :], head_sum[:, :, :],
                               temp_row[:, :].unsqueeze(1).broadcast_to([P, KD, XH]), ALU.mult)\
                .then_inc(consts_ready, 1)

            def add_bias(f, load, ln):
                pool.wait_ge(load, 16)
                for t in range(TH):
                    pool.wait_ge(xn_ready, ln * NT + f * TH + t + 1)
                    pool.tensor_tensor(xres[:, f * TH + t, :], xres[:, f * TH + t, :], bo_row[:, :], ALU.add)\
                        .then_inc(bias_added, 1)

            def subtract_max(n, slot):
                pool.wait_ge(max_ready, n)
                s = sbuf[slot].rearrange("p (c k) -> p c k", c=4)
                pool.tensor_tensor(s, s, smax[:, slot, :].unsqueeze(2).broadcast_to([P, 4, P]),
                                   ALU.subtract).then_inc(sub_ready, 1)

            add_bias(0, ld_bo, 0)
            add_bias(1, ld_bo, 0)
            units = 4 * TH
            for f in range(2):
                for n in range(units):
                    subtract_max(f * units + n + 1, n % 2)
            pool.wait_ge(acc_ready, ACC_AT["s", 1, units - 1] + 1)
            link(pool.memset(head_spread[0:XH], 1.0))
            link(select(head_spread[0:XH], [[P, KD], [1, P]], 0, -XD, ALU.is_ge, 0.0))
            select(head_spread[0:XH], [[-P, KD], [-1, P]], XD - 1, XD, ALU.is_ge, 0.0).then_inc(spread_ready, 1)
            add_bias(0, ld_bout, 1)
            add_bias(1, ld_bout, 1)
            for f in range(2):
                pool.wait_ge(inv_ready, f + 1)
                for c in range(KD):
                    n = slice(f * HALF, (f + 1) * HALF)
                    pool.tensor_tensor(wn2[:, c, n].rearrange("p (b n) -> p b n", b=BH),
                                       sqT[:, c, n].rearrange("p (b n) -> p b n", b=BH),
                                       bsm[:, 0, c, :].unsqueeze(2).broadcast_to([P, BH, T]),
                                       ALU.mult).then_inc(wn2_ready, 1)

            def step(h):
                for f in range(2):
                    subtract_max(2 * units + 2 * h + f + 1, f)
                for f in range(2):
                    pool.wait_ge(rsum_ready, 2 * h + f + 1)
                    p = pbuf[f].rearrange("p (c k) -> p c k", c=4)
                    pool.tensor_tensor(p, p, ssum[:, f, :].unsqueeze(2).broadcast_to([P, 4, P]),
                                       ALU.mult).then_inc(norm_ready, 1)

            with pool.Fori(0, FH) as h:
                step(h)

        @block.scalar
        def _(act):
            x_v = x.rearrange("(t p) d -> t p d", p=P)
            for t in range(NT):
                act.dma_start(xres[:, t, :], x_v[t]).then_inc(ld_x[t], 16)
            act.dma_start(bias_cols[:, 0, :], bq).then_inc(ld_bias, 16)
            act.dma_start(bias_cols[:, 1, :], bk).then_inc(ld_bias, 16)
            act.dma_start(temp_row[:, :], temp.partition_broadcast(P)).then_inc(ld_bias, 16)
            act.dma_start(rs_col[:, :], route_scale.partition_broadcast(P)).then_inc(ld_bias, 16)
            act.dma_start(bv_row, bv.partition_broadcast(P)).then_inc(ld_bv, 16)
            act.dma_start(bo_row[:, :], bo.partition_broadcast(P)).then_inc(ld_bo, 16)

            def high(name):
                src, hl, scale, load, count = split_operands(name)
                act.wait_ge(load, count)
                act.activation(hl[0], src, ACT.Copy, scale=scale).then_inc(w_hi, 1)

            def high_turned(key):
                g = SPLIT_AT[key]
                t = key[1] * TH + key[2]
                act.wait_ge(split_ready, g + 1)
                act.activation(xt_hl[0][:, :, t * P:(t + 1) * P],
                               splitb(g)[:, :].rearrange("p (k n) -> p k n", k=KD), ACT.Copy)\
                    .then_inc(split_hi, 1)

            def std(n):
                act.wait_ge(var_ready, n)
                act.activation(rstd[:, :], var[:, :], ACT.Sqrt).then_inc(std_ready, 1)

            units = 4 * TH

            def exp_scores(f, n):
                act.wait_ge(sub_ready, f * units + n + 1)
                m = f * units + n
                if m >= 2:
                    act.wait_ge(turn_ready, TURN_AT["p", (m - 2) // units, (m - 2) % units] + 1)
                act.activation(pbuf[n % 2], sbuf[n % 2], ACT.Exp, scale=float(XD) ** -0.5)\
                    .then_inc(exp_ready, 1)

            def take_turned(f, n):
                g = TURN_AT["p", f, n]
                m = f * units + n
                act.wait_ge(turn_ready, g + 1)
                if m >= 2:
                    u = (m - 2) // 2
                    act.wait_ge(acc_ready, ACC_AT["pv", u // (units // 2), u % (units // 2)] + 1)
                act.copy(ptbuf[n % 2], turnb(g)[:, :]).then_inc(turn_free, 1)

            high("ctx0")
            high("wk")
            high("wv")
            high("ctx1")
            high("wq")
            std(1)
            for t in range(TH):
                high_turned(("x1", 0, t))
            high("wo")
            std(2)
            for t in range(TH):
                high_turned(("x1", 1, t))
            act.wait_ge(acc_ready, ACC_AT["v", 1, TH - 1] + 1)
            high("wqkv")
            high("wout")
            for f in range(2):
                for kind, a in attention_order():
                    if kind == "scores":
                        exp_scores(f, a)
                    elif kind == "turn":
                        take_turned(f, a)
                    elif kind == "turn_out":
                        high_turned(("at", f, a))
            high("sel")
            for f in range(2):
                std(3 + f)
                for t in range(TH):
                    high_turned(("x2", f, t))
                for c in range(KD):
                    n = slice(f * HALF, (f + 1) * HALF)
                    act.wait_ge(acc_free, ACC_AT["w", f, c] + 1)
                    act.activation(sqT[:, c, n], wT[:, c, n], ACT.Square).then_inc(sq_ready, 1)
            for f in range(2):
                act.wait_ge(lmax_ready, f + 1)
                act.activation(pi[f], pi[f], ACT.Exp).then_inc(lexp_ready, 1)
                g = TURN_AT["pi", f]
                act.wait_ge(turn_ready, g + 1)
                act.copy(piT[f][0:XH], turnb(g)[0:XH, :]).then_inc(turn_free, 1)
                for c in range(KD):
                    n = slice(f * HALF, (f + 1) * HALF)
                    act.wait_ge(z_ready, f * KD + c + 1)
                    act.activation(xt_hl[0][:, c, n], wT[:, c, n], ACT.Copy).then_inc(z_hi, 1)

            def weights_high(h, o_last=False):
                act.wait_ge(ld_qk, 16 * (h + 1))
                act.activation(qk_hl[0], stage_qk.rearrange("p (m k n) -> p m k n", m=2, k=KD), ACT.Copy,
                               scale=WSCALE).then_inc(vw_hi, 1)
                act.wait_ge(ld_exp, 16 if isinstance(h, int) and h == 0 else h * 32)
                for c in range(2):
                    act.activation(v_hl[0][:, c], stage_v[:, c].rearrange("p (k n) -> p k n", k=KD), ACT.Copy,
                                   scale=WSCALE).then_inc(vw_hi, 1)

            def out_weights_high(h, hl):
                act.wait_ge(ld_exp, h * 32 + 48 if not (isinstance(h, int) and h == FH - 1) else 32 * FH)
                for c in range(2):
                    act.activation(hl[0][:, c * EC:(c + 1) * EC],
                                   stage_v[:, c].rearrange("p (e n) -> p e n", e=EC), ACT.Copy,
                                   scale=WSCALE).then_inc(ow_hi, 1)

            for f in range(2):
                std(5 + f)
                for t in range(TH):
                    high_turned(("x3", f, t))
            weights_high(0)
            for f in range(2):
                act.wait_ge(rl_ready, f + 1)
                act.activation(sbuf[1], sbuf[0], ACT.Sigmoid).then_inc(prob_ready, 1)
            for f in range(2):
                g = TURN_AT["go", f]
                act.wait_ge(turn_ready, g + 1)
                act.copy(goT[:, f * HALF:(f + 1) * HALF], turnb(g)[0:FH * E, :]).then_inc(turn_free, 1)
            act.wait_ge(gate_stored, 16)

            def step(h, first=False, last=False):
                if not first:
                    act.wait_ge(acc_ready, acc_at("out", h - 2, NT - 1) + 1)
                    out_weights_high(h - 1, o_hl)
                for f in range(2):
                    act.wait_ge(sub_ready, 2 * units + 2 * h + f + 1)
                    act.wait_ge(turn_ready, turn_at("p", h - 1, f) + 1 if not first else TURN_AT["p", 1, units - 1] + 1)
                    act.activation(pbuf[f], sbuf[f], ACT.Exp, scale=float(P) ** -0.5).then_inc(exp_ready, 1)
                for f in range(2):
                    act.wait_ge(turn_ready, turn_at("p", h, f) + 1)
                    act.copy(ptbuf[f], turnb(f)[:, :]).then_inc(turn_free, 1)
                if not last:
                    act.wait_ge(acc_ready, acc_at("xv", h, 2 * NT - 1) + 1)
                    weights_high(h + 1)
                else:
                    act.wait_ge(acc_ready, acc_at("xv", h, 2 * NT - 1) + 1)
                    out_weights_high(h, o_hl_last)
                for f in range(2):
                    act.wait_ge(turn_ready, turn_at("ctx", h, f) + 1)
                    if not first:
                        act.wait_ge(prod_ready, NT * h)
                    act.copy(ctxT[:, f * HALF:(f + 1) * HALF], turnb(f)[:, :]).then_inc(turn_free, 1)
                for t in range(NT):
                    act.wait_ge(prod_ready, NT * h + t + 1)
                    if not first:
                        act.wait_ge(acc_ready, acc_at("out", h - 1, t) + 1)
                    act.activation(gated[0][:, t], prod[t % 2], ACT.Copy).then_inc(gated_hi, 1)

            step(0, first=True)
            with act.Fori(1, FH - 1) as h:
                step(h)
            step(FH - 1, last=True)

        @block.vector
        def _(dve):
            steps = [0, None]

            def link(ins):
                steps[0] += 1
                ins.then_inc(dve_step, 1)
                dve.wait_ge(dve_step, steps[0] if steps[1] is None else steps[1] + steps[0])

            def low(name):
                src, hl, scale, load, count = split_operands(name)
                dve.wait_ge(w_hi, split_count(name))
                dve.scalar_tensor_tensor(out=hl[1], in0=src, scalar=scale, in1=hl[0], op0=ALU.mult,
                                         op1=ALU.subtract).then_inc(w_lo, 1)

            def low_turned(key):
                g = SPLIT_AT[key]
                t = key[1] * TH + key[2]
                dve.wait_ge(split_hi, g + 1)
                dve.tensor_tensor(xt_hl[1][:, :, t * P:(t + 1) * P],
                                  splitb(g)[:, :].rearrange("p (k n) -> p k n", k=KD),
                                  xt_hl[0][:, :, t * P:(t + 1) * P], ALU.subtract).then_inc(split_free, 1)

            def layernorm(f, ln, key):
                if ln or f:
                    dve.wait_ge(xn_ready, ln * NT + f * TH)
                for t in range(TH):
                    if ln == 0:
                        dve.wait_ge(ld_x[f * TH + t], 16)
                    last = dve.bn_stats(stats[:, t, :], xres[:, f * TH + t, :])
                link(last)
                for t in range(TH):
                    last = dve.bn_aggr(mv[:, t, :], stats[:, t, :])
                link(last)
                dve.tensor_scalar(var[:, :], mv[:, :, 1], LN_EPS, None, ALU.add).then_inc(var_ready, 1)
                dve.wait_ge(std_ready, 2 * ln + f + 1)
                link(dve.reciprocal(rstd[:, :], rstd[:, :]))
                link(dve.tensor_tensor(nw[:, :], rstd[:, :], rstd[:, :], ALU.mult))
                link(dve.tensor_tensor(nw[:, :], nw[:, :], var[:, :], ALU.mult))
                link(dve.tensor_scalar(nw[:, :], nw[:, :], -0.5, 1.5, ALU.mult, ALU.add))
                link(dve.tensor_tensor(rstd[:, :], rstd[:, :], nw[:, :], ALU.mult))
                for t in range(TH):
                    n = ln * NT + f * TH + t
                    if n >= 2:
                        o = n - 2
                        dve.wait_ge(split_ready, SPLIT_AT[f"x{o // NT + 1}", o % NT // TH, o % TH] + 1)
                    dve.tensor_scalar(xn[:, n % 2, :], xres[:, f * TH + t, :], mv[:, t, 0:1], rstd[:, t:t + 1],
                                      ALU.subtract, ALU.mult).then_inc(xn_ready, 1)
                    if t >= 1:
                        low_turned((key, f, t - 1))
                low_turned((key, f, TH - 1))

            def acc(key):
                g = ACC_AT[key]
                dve.wait_ge(acc_ready, g + 1)
                return accb(g)

            def kv(f):
                for c in range(KD):
                    dve.tensor_scalar(kT[:, c, f * HALF:(f + 1) * HALF], acc(("k", f, c))[:, :], 1.0 / WSCALE,
                                      bias_cols[:, 1, c:c + 1], ALU.mult, ALU.add).then_inc(acc_free, 1)
                for t in range(TH):
                    b = acc(("v", f, t))
                    dve.scalar_tensor_tensor(out=vones[:, f * TH + t, :, 0:XD],
                                             in0=b[:, :].rearrange("p (h d) -> p h d", h=XH), scalar=1.0 / WSCALE,
                                             in1=bv_row.rearrange("p (h d) -> p h d", h=XH),
                                             op0=ALU.mult, op1=ALU.add).then_inc(acc_free, 1)

            def query(f):
                for c in range(KD):
                    dve.tensor_scalar(qT[:, c, f * HALF:(f + 1) * HALF], acc(("q", f, c))[:, :], 1.0 / WSCALE,
                                      bias_cols[:, 0, c:c + 1], ALU.mult, ALU.add).then_inc(acc_free, 1)

            units = 4 * TH

            def mask_and_max(bank, mask, slot, free, freed, exps):
                if exps is not None:
                    dve.wait_ge(exp_ready, exps)
                dve.tensor_tensor(sbuf[slot].rearrange("p (c k) -> p c k", c=4),
                                  bank[:, :].rearrange("p (c k) -> p c k", c=4),
                                  mask[:, :].unsqueeze(1).broadcast_to([P, 4, P]), ALU.add).then_inc(free, 1)
                dve.wait_ge(free, freed)
                dve.tensor_reduce(smax[:, slot, :], sbuf[slot].rearrange("p (c k) -> p c k", c=4), AX.X,
                                  ALU.max).then_inc(max_ready, 1)

            def attention(f):
                for kind, a in attention_order():
                    if kind == "scores":
                        g = ACC_AT["s", f, a]
                        m = f * units + a
                        mask_and_max(acc(("s", f, a)), mask_causal, a % 2, acc_free, g + 1,
                                     m - 1 if m >= 2 else None)
                    elif kind == "values":
                        t, half = a // 2, a % 2
                        b = acc(("pv", f, a))
                        o = b[:, 0:8 * (XD + 1)].rearrange("p (j c d) -> p j c d", j=2, c=KD)
                        n = f * TH + t
                        if n >= 2 and half == 0:
                            dve.wait_ge(split_ready, SPLIT_AT["at", (n - 2) // TH, (n - 2) % TH] + 1)
                        dve.wait_ge(acc_free, ACC_AT["pv", f, a])
                        r = rinv[:, :].rearrange("p (j c) -> p j c", j=2)
                        link(dve.reciprocal(r, o[:, :, :, XD]))
                        att = attn[n % 2].rearrange("p (c j d) -> p j c d", c=KD, j=HJ)
                        for j in range(2):
                            last = dve.tensor_tensor(att[:, 2 * half + j], o[:, j, :, 0:XD],
                                                     r[:, j].unsqueeze(2).broadcast_to([P, KD, XD]), ALU.mult)
                            if j == 0:
                                last.then_inc(att_ready, 1)
                        last.then_inc(acc_free, 1)
                    elif kind == "turn_out":
                        low_turned(("at", f, a))
                    elif kind == "project":
                        t = f * TH + a
                        dve.wait_ge(bias_added, t + 1)
                        link(dve.scalar_tensor_tensor(out=xres[:, t, :], in0=acc(("wo", f, a))[:, :],
                                                      scalar=1.0 / WSCALE, in1=xres[:, t, :], op0=ALU.mult,
                                                      op1=ALU.add))
                        dve.sem_inc(acc_free, 1)

            def spectrum(f):
                n = slice(f * HALF, (f + 1) * HALF)
                for c in range(KD):
                    b = acc(("w", f, c))
                    dve.tensor_scalar(wT[:, c, n], b[:, :], 1.0 / WSCALE, None, ALU.mult).then_inc(acc_free, 1)
                for c in range(KD):
                    dve.wait_ge(sq_ready, f * KD + c + 1)
                    last = dve.tensor_reduce(bsm[:, 1, c, :], sqT[:, c, n].rearrange("p (b n) -> p b n", b=BH),
                                             AX.X, ALU.add)
                link(last)
                link(dve.tensor_scalar(bsm[:, 1], bsm[:, 1], 1e-24, None, ALU.max))
                if f == 1:
                    dve.wait_ge(wn2_ready, KD)
                dve.reciprocal(bsm[:, 0], bsm[:, 1]).then_inc(inv_ready, 1)

            def membership(f):
                n = slice(f * HALF, (f + 1) * HALF)
                lg = acc(("lg", f))[:, 0:TH * XH].rearrange("p (t h) -> p t h", t=TH)
                link(dve.tensor_reduce(smax[:, 0, :], lg, AX.X, ALU.max))
                link(dve.tensor_tensor(pi[f], lg, smax[:, 0, :].unsqueeze(2).broadcast_to([P, TH, XH]),
                                       ALU.subtract))
                dve.sem_inc(acc_free, 1)
                dve.sem_inc(lmax_ready, 1)
                dve.wait_ge(lexp_ready, f + 1)
                link(dve.tensor_reduce(ssum[:, 0, :], pi[f], AX.X, ALU.add))
                link(dve.reciprocal(ssum[:, 0, :], ssum[:, 0, :]))
                dve.tensor_tensor(pi[f], pi[f], ssum[:, 0, :].unsqueeze(2).broadcast_to([P, TH, XH]),
                                  ALU.mult).then_inc(pi_ready, 1)
                for c in range(KD):
                    b = acc(("pb", f, c))
                    dve.tensor_reduce(bsm[:, 1, c, :], b[:, :].rearrange("p (b n) -> p b n", b=BH), AX.X, ALU.add)
                    dve.tensor_tensor(sqT[:, c, n], sqT[:, c, n], b[:, :], ALU.mult)
                    link(dve.tensor_tensor(wT[:, c, n], wT[:, c, n], b[:, :], ALU.mult))
                    dve.sem_inc(acc_free, 1)
                    last = dve.tensor_reduce(bsm[:, 2, c, :], sqT[:, c, n].rearrange("p (b n) -> p b n", b=BH),
                                             AX.X, ALU.add)
                link(last)
                link(dve.tensor_scalar(bsm[:, 1], bsm[:, 1], 1e-8, None, ALU.add))
                link(dve.reciprocal(bsm[:, 3], bsm[:, 1]))
                link(dve.tensor_tensor(bsm[:, 2], bsm[:, 2], bsm[:, 3], ALU.mult))
                link(dve.tensor_scalar(bsm[:, 2], bsm[:, 2], 1.0, -1.0 / ASCALE, ALU.add, ALU.mult))
                link(dve.reciprocal(bsm[:, 3], bsm[:, 2]))
                for c in range(KD):
                    wb = wT[:, c, n].rearrange("p (b n) -> p b n", b=BH)
                    dve.tensor_tensor(wb, wb, bsm[:, 3, c, :].unsqueeze(2).broadcast_to([P, BH, T]),
                                      ALU.mult).then_inc(z_ready, 1)
                for c in range(KD):
                    dve.wait_ge(z_hi, f * KD + c + 1)
                    dve.tensor_tensor(xt_hl[1][:, c, n], wT[:, c, n], xt_hl[0][:, c, n], ALU.subtract)\
                        .then_inc(z_lo, 1)

            def mix_out(f):
                for a in range(TH):
                    t = f * TH + a
                    dve.wait_ge(bias_added, NT + t + 1)
                    link(dve.scalar_tensor_tensor(out=xres[:, t, :], in0=acc(("wout", f, a))[:, :],
                                                  scalar=1.0 / (WSCALE * ASCALE), in1=xres[:, t, :],
                                                  op0=ALU.mult, op1=ALU.add))
                    dve.sem_inc(acc_free, 1)

            def route(f):
                z = sbuf[0].rearrange("p (t g) -> p t g", t=TH)
                if f == 0:
                    dve.wait_ge(turn_free, TURN_AT["p", 1, units - 1] + 1)
                for t in range(TH):
                    b = acc(("gl", f, t))
                    dve.tensor_scalar(z[:, t, :], b[:, 0:P], 1.0 / WSCALE, None, ALU.mult).then_inc(acc_free, 1)
                dve.wait_ge(acc_free, ACC_AT["gl", f, TH - 1] + 1)
                dve.sem_inc(rl_ready, 1)
                dve.wait_ge(prob_ready, f + 1)
                G = TH * 2 * FH

                def by8(v):
                    return v.rearrange("p (g e) -> p g e", g=G)

                def wide(v):
                    return v.unsqueeze(2).broadcast_to([P, G, E])

                pr, one, two, rest = by8(sbuf[1]), by8(pbuf[0]), by8(pbuf[1]), by8(sbuf[0])
                rampb = ramp[:, :].unsqueeze(1).broadcast_to([P, G, E])
                m1, m2, at, den = (gsm[:, i, :] for i in range(4))

                def pick(hot, values, m):
                    link(dve.tensor_reduce(m, values, AX.X, ALU.max))
                    link(dve.tensor_tensor(hot, values, wide(m), ALU.is_equal))
                    link(dve.tensor_tensor(hot, hot, rampb, ALU.mult))
                    link(dve.tensor_reduce(at, hot, AX.X, ALU.max))
                    link(dve.tensor_tensor(hot, hot, wide(at), ALU.is_equal))

                pick(one, pr, m1)
                link(dve.scalar_tensor_tensor(out=rest, in0=one, scalar=-4.0, in1=pr, op0=ALU.mult, op1=ALU.add))
                pick(two, rest, m2)
                link(dve.tensor_tensor(den, m1, m2, ALU.add))
                link(dve.tensor_scalar(den, den, 1e-9, None, ALU.max))
                link(dve.reciprocal(at, den))
                link(dve.tensor_scalar(at, at, rs_col[:, 0:1], None, ALU.mult))
                link(dve.tensor_tensor(m1, m1, at, ALU.mult))
                link(dve.tensor_tensor(m2, m2, at, ALU.mult))
                link(dve.tensor_tensor(one, one, wide(m1), ALU.mult))
                link(dve.tensor_tensor(two, two, wide(m2), ALU.mult))
                gf = gates[:, f * TH:(f + 1) * TH, :].rearrange("p t (g e) -> p (t g) e", e=E)
                link(dve.tensor_tensor(gf, one, two, ALU.add))
                dve.sem_inc(gates_ready, 1)

            def weights_low(h):
                dve.wait_ge(vw_hi, 3 * h + 1)
                dve.scalar_tensor_tensor(out=qk_hl[1].rearrange("p m k n -> p (m k n)"), in0=stage_qk, scalar=WSCALE,
                                         in1=qk_hl[0].rearrange("p m k n -> p (m k n)"),
                                         op0=ALU.mult, op1=ALU.subtract).then_inc(vw_lo, 1)
                for c in range(2):
                    dve.wait_ge(vw_hi, 3 * h + 2 + c)
                    dve.scalar_tensor_tensor(out=v_hl[1][:, c].rearrange("p k n -> p (k n)"), in0=stage_v[:, c],
                                             scalar=WSCALE, in1=v_hl[0][:, c].rearrange("p k n -> p (k n)"),
                                             op0=ALU.mult, op1=ALU.subtract).then_inc(vw_lo, 1)

            def out_weights_low(h, hl):
                for c in range(2):
                    dve.wait_ge(ow_hi, 2 * h + c + 1)
                    dve.scalar_tensor_tensor(out=hl[1][:, c * EC:(c + 1) * EC].rearrange("p e n -> p (e n)"),
                                             in0=stage_v[:, c], scalar=WSCALE,
                                             in1=hl[0][:, c * EC:(c + 1) * EC].rearrange("p e n -> p (e n)"),
                                             op0=ALU.mult, op1=ALU.subtract).then_inc(ow_lo, 1)

            def take_out(h, t):
                dve.wait_ge(acc_ready, acc_at("out", h, t) + 1)
                ins = dve.scalar_tensor_tensor(out=xres[:, t, :], in0=accb(acc_bank("out", t))[:, :],
                                               scalar=1.0 / (WSCALE * ASCALE), in1=xres[:, t, :],
                                               op0=ALU.mult, op1=ALU.add)
                ins.then_inc(acc_free, 1)

            def softmax_sums(h, f):
                dve.wait_ge(exp_ready, 2 * units + 2 * h + f + 1)
                link(dve.tensor_reduce(ssum[:, f, :], pbuf[f].rearrange("p (c k) -> p c k", c=4), AX.X, ALU.add))
                dve.reciprocal(ssum[:, f, :], ssum[:, f, :]).then_inc(rsum_ready, 1)

            def gate_context(h, t, first):
                n = h * NT + t
                if not (first and t < 2):
                    dve.wait_ge(gated_lo, n - 1)
                c = ctxT[:, t * P:(t + 1) * P].unsqueeze(1).broadcast_to([P, E, P])
                dve.scalar_tensor_tensor(out=prod[t % 2], in0=c, scalar=ASCALE,
                                         in1=gate_b[:, :, t * P:(t + 1) * P], op0=ALU.mult,
                                         op1=ALU.mult).then_inc(prod_ready, 1)

            def gated_low(h, t):
                dve.wait_ge(gated_hi, h * NT + t + 1)
                dve.tensor_tensor(gated[1][:, t], prod[t % 2], gated[0][:, t], ALU.subtract).then_inc(gated_lo, 1)

            def step(h, first=False, last=False):
                g = gates[:, :, h * E:(h + 1) * E] if isinstance(h, int) else gates[:, :, bass.ds(h * E, E)]
                link(dve.tensor_scalar(gate_h[:, :, :], g, 1.0 / WSCALE, None, ALU.mult))
                for m in range(4):
                    dve.wait_ge(acc_ready, acc_at("qk", h, m) + 1)
                    dve.tensor_scalar(qkT[:, m // 2, (m % 2) * HALF:(m % 2 + 1) * HALF],
                                      accb(acc_bank("qk", m))[:, :], 1.0 / WSCALE, None, ALU.mult)\
                        .then_inc(acc_free, 1)
                if not first:
                    out_weights_low(h - 1, o_hl)
                for c in range(2):
                    for t in range(NT):
                        dve.wait_ge(acc_ready, acc_at("xv", h, c * NT + t) + 1)
                        if c == 0 and t % TH == 0 and not first:
                            dve.wait_ge(turn_ready, turn_at("ctx", h - 1, t // TH) + 1)
                        b = accb(acc_bank("xv", c * NT + t))
                        v = v_head[:, t, :]
                        for e in range(EC):
                            scale = gate_h[:, t, c * EC + e:c * EC + e + 1]
                            part = b[:, e * P:(e + 1) * P]
                            if c == 0 and e == 0:
                                ins = dve.tensor_scalar(v, part, scale, None, ALU.mult)
                            else:
                                ins = dve.scalar_tensor_tensor(out=v, in0=part, scalar=scale, in1=v,
                                                               op0=ALU.mult, op1=ALU.add)
                            if e < EC - 1:
                                link(ins)
                        ins.then_inc(acc_free, 1)
                        if c == 0 and t in (2, 4):
                            f = t // 2 - 1
                            dve.wait_ge(split_ready, split_at(h, f) + 1)
                            mask_and_max(splitb(f), mask_batch, f, split_free, split_at(h, f) + 1,
                                         2 * units + 2 * h + f - 1)
                        if (c, t) in ((0, 6), (1, 0)):
                            softmax_sums(h, c)
                        if c == 1 and t % TH == TH - 1:
                            dve.wait_ge(acc_free, acc_at("xv", h, c * NT + t) + 1)
                            dve.sem_inc(vhead_ready, 1)
                if not last:
                    weights_low(h + 1)
                else:
                    out_weights_low(h, o_hl_last)
                dve.wait_ge(ld_gate, 16 * (h + 1))
                for t in range(NT):
                    if not first:
                        take_out(h - 1, t)
                    if t % TH == 0:
                        dve.wait_ge(turn_free, turn_at("ctx", h, t // TH) + 1)
                    gate_context(h, t, first)
                    if t >= 1:
                        gated_low(h, t - 1)
                gated_low(h, NT - 1)

            low("ctx0")
            low("wk")
            low("wv")
            dve.wait_ge(ld_bias, 64)
            dve.wait_ge(ld_bv, 16)
            dve.wait_ge(ones_ready, 1)
            dve.wait_ge(consts_ready, 1)
            kv(0)
            low("ctx1")
            low("wq")
            layernorm(0, 0, "x1")
            low("wo")
            query(0)
            kv(1)
            layernorm(1, 0, "x1")
            query(1)
            low("wqkv")
            low("wout")
            attention(0)
            attention(1)
            low("sel")
            for f in range(2):
                layernorm(f, 1, "x2")
                spectrum(f)
            for f in range(2):
                membership(f)
            for f in range(2):
                mix_out(f)
                layernorm(f, 2, "x3")
            weights_low(0)
            for f in range(2):
                route(f)

            step(0, first=True)
            LINKS = 1 + 2 * NT * (EC - 1) + 2
            with dve.Fori(1, FH - 1) as h:
                before, steps[0], steps[1] = steps[0], 0, h * LINKS + (steps[0] - LINKS)
                step(h)
                assert steps[0] == LINKS
            steps[0], steps[1] = before + (FH - 2) * LINKS, None
            step(FH - 1, last=True)
            for t in range(NT):
                take_out(FH - 1, t)

        @block.tensor
        def _(pe):
            def begin_acc(n):
                if not isinstance(n, int) or n >= ACC:
                    pe.wait_ge(acc_free, n - (ACC - 1))

            def product(bank, stat, mov, width=D):
                for k in range(KD):
                    for a, b in ((0, 0), (0, 1), (1, 0)):
                        last = pe.matmul(bank[:, 0:width], stat(a, k), mov(b, k),
                                         start=(k == 0 and (a, b) == (0, 0)), stop=(k == KD - 1 and a == 1))
                return last

            def columns(f):
                return slice(f * HALF, (f + 1) * HALF)

            def tile(t):
                return slice(t * P, (t + 1) * P)

            def project_t(key, w, src, f, c):
                g = ACC_AT[key]
                begin_acc(g)
                product(accb(g), lambda z, k: w[z][:, k, tile(c)], lambda z, k: src[z][:, k, columns(f)])\
                    .then_inc(acc_ready, 1)

            def project_n(key, w, src, t, width=D):
                g = ACC_AT[key]
                begin_acc(g)
                product(accb(g), lambda z, k: src[z][:, k, tile(t)], lambda z, k: w[z][:, k, 0:width], width)\
                    .then_inc(acc_ready, 1)

            def turn_tile(key, src):
                g = SPLIT_AT[key]
                if g >= SPLIT:
                    pe.wait_ge(split_free, g - (SPLIT - 1))
                for k in range(KD):
                    last = pe.transpose(splitb(g)[:, tile(k)], src[:, tile(k)], ident[:, :])
                last.then_inc(split_ready, 1)

            def turn_normed(f, ln):
                for t in range(TH):
                    n = ln * NT + f * TH + t
                    pe.wait_ge(xn_ready, n + 1)
                    turn_tile((f"x{ln + 1}", f, t), xn[:, n % 2, :])

            def split_tiles(key, f, t):
                pe.wait_ge(split_free, SPLIT_AT[key, f, t] + 1)

            units = 4 * TH

            def attention(f):
                for kind, a in attention_order():
                    t, j = f * TH + a // 4, a % 4
                    if kind == "scores":
                        g = ACC_AT["s", f, a]
                        begin_acc(g)
                        r = slice(XD * j, XD * (j + 1))
                        for c in range(KD):
                            last = pe.matmul(accb(g)[:, tile(c)], qT[r, c, tile(t)], kT[r, c, tile(t)],
                                             start=True, stop=True)
                        last.then_inc(acc_ready, 1)
                    elif kind == "turn":
                        g = TURN_AT["p", f, a]
                        pe.wait_ge(exp_ready, f * units + a + 1)
                        if g >= TURN:
                            pe.wait_ge(turn_free, g - (TURN - 1))
                        for c in range(KD):
                            last = pe.transpose(turnb(g)[:, tile(c)], pbuf[a % 2][:, tile(c)], ident[:, :])
                        last.then_inc(turn_ready, 1)
                    elif kind == "values":
                        t = f * TH + a // 2
                        g = ACC_AT["pv", f, a]
                        begin_acc(g)
                        pe.wait_ge(turn_free, TURN_AT["p", f, 2 * a + 1] + 1)
                        for u in range(2):
                            for c in range(KD):
                                at = (u * KD + c) * (XD + 1)
                                head = HJ * c + (2 * a + u) % 4
                                last = pe.matmul(accb(g)[:, at:at + XD + 1], ptbuf[u][:, tile(c)],
                                                 vones[:, t, head, :], start=True, stop=True)
                        last.then_inc(acc_ready, 1)
                    elif kind == "turn_out":
                        n = f * TH + a
                        pe.wait_ge(att_ready, 2 * (n + 1))
                        pe.wait_ge(acc_free, ACC_AT["pv", f, 2 * a + 1] + 1)
                        turn_tile(("at", f, a), attn[n % 2])
                    else:
                        split_tiles("at", f, a)
                        project_n(("wo", f, a), w_hl[3], xt_hl, f * TH + a)

            pe.wait_ge(consts_ready, 1)

            def keys_values(f):
                pe.wait_ge(w_lo, split_count(f"ctx{f}"))
                pe.wait_ge(w_lo, split_count("wk"))
                for c in range(KD):
                    project_t(("k", f, c), w_hl[0], ctx_hl, f, c)
                pe.wait_ge(w_lo, split_count("wv"))
                for t in range(TH):
                    project_n(("v", f, t), w_hl[1], ctx_hl, f * TH + t)

            for f in range(2):
                keys_values(f)
                turn_normed(f, 0)
                pe.wait_ge(w_lo, split_count("wq"))
                split_tiles("x1", f, TH - 1)
                for c in range(KD):
                    project_t(("q", f, c), w_hl[2], xt_hl, f, c)
            pe.wait_ge(w_lo, split_count("wo"))
            pe.wait_ge(acc_free, ACC_AT["q", 1, KD - 1] + 1)
            attention(0)
            attention(1)
            pe.wait_ge(w_lo, split_count("wqkv"))
            for f in range(2):
                turn_normed(f, 1)
                split_tiles("x2", f, TH - 1)
                for c in range(KD):
                    project_t(("w", f, c), w_hl[0], xt_hl, f, c)
            pe.wait_ge(spread_ready, 1)
            for f in range(2):
                pe.wait_ge(wn2_ready, KD * (f + 1))
                g = ACC_AT["lg", f]
                begin_acc(g)
                for t in range(TH):
                    for c in range(KD):
                        last = pe.matmul(accb(g)[:, t * XH:(t + 1) * XH], wn2[:, c, tile(f * TH + t)],
                                         head_sum[:, c, :], start=(c == 0), stop=(c == KD - 1))
                last.then_inc(acc_ready, 1)
                pe.wait_ge(pi_ready, f + 1)
                g = TURN_AT["pi", f]
                pe.wait_ge(turn_free, g - (TURN - 1))
                for t in range(TH):
                    last = pe.transpose(turnb(g)[0:XH, tile(t)], pi[f][:, t, :], ident[:, :])
                last.then_inc(turn_ready, 1)
                pe.wait_ge(turn_free, g + 1)
                for c in range(KD):
                    g = ACC_AT["pb", f, c]
                    begin_acc(g)
                    pe.matmul(accb(g)[:, :], head_spread[0:XH, c, :], piT[f][0:XH, :], start=True, stop=True)\
                        .then_inc(acc_ready, 1)
            pe.wait_ge(w_lo, split_count("wout"))
            for f in range(2):
                pe.wait_ge(z_lo, KD * (f + 1))
                for t in range(TH):
                    project_n(("wout", f, t), w_hl[1], xt_hl, f * TH + t)
                turn_normed(f, 2)
            pe.wait_ge(w_lo, split_count("sel"))
            for f in range(2):
                split_tiles("x3", f, TH - 1)
                for t in range(TH):
                    project_n(("gl", f, t), sel_hl, xt_hl, f * TH + t, P)
                pe.wait_ge(gates_ready, f + 1)
                g = TURN_AT["go", f]
                pe.wait_ge(turn_free, g - (TURN - 1))
                for t in range(TH):
                    last = pe.transpose(turnb(g)[0:FH * E, tile(t)], gates[:, f * TH + t, FH * E:2 * FH * E],
                                        ident[:, :])
                last.then_inc(turn_ready, 1)

            def output_tile(h, t, hl):
                n = acc_at("out", h, t)
                begin_acc(n)
                pe.wait_ge(gated_lo, h * NT + (t + 1))
                bank = accb(acc_bank("out", t))
                for e in range(E):
                    for a, b in ((0, 0), (0, 1), (1, 0)):
                        last = pe.matmul(bank[:, :], gated[a][:, t, e, :], hl[b][:, e, :],
                                         start=(e == 0 and (a, b) == (0, 0)), stop=(e == E - 1 and a == 1))
                last.then_inc(acc_ready, 1)

            def head_scores(h, f):
                n = split_at(h, f)
                pe.wait_ge(split_free, n - (SPLIT - 1))
                for t in range(TH):
                    q = tile(f * TH + t)
                    last = pe.matmul(splitb(f)[:, tile(t)], qkT[:, 0, q], qkT[:, 1, q], start=True, stop=True)
                last.then_inc(split_ready, 1)

            def head_turn(h, f):
                n = turn_at("p", h, f)
                pe.wait_ge(norm_ready, h * 2 + (f + 1))
                pe.wait_ge(turn_free, n - (TURN - 1))
                for t in range(TH):
                    last = pe.transpose(turnb(f)[:, tile(t)], pbuf[f][:, tile(t)], ident[:, :])
                last.then_inc(turn_ready, 1)

            def head_context(h, f):
                n = turn_at("ctx", h, f)
                pe.wait_ge(vhead_ready, h * 2 + (f + 1))
                pe.wait_ge(turn_free, n - (TURN - 1))
                for t in range(TH):
                    last = pe.matmul(turnb(f)[:, tile(t)], v_head[:, f * TH + t, :], ptbuf[f][:, tile(t)],
                                     start=True, stop=True)
                last.then_inc(turn_ready, 1)

            def step(h, first=False):
                pe.wait_ge(vw_lo, h * 3 + 1)
                for m in range(4):
                    begin_acc(acc_at("qk", h, m))
                    product(accb(acc_bank("qk", m)), lambda z, k: qk_hl[z][:, m // 2, k, :],
                            lambda z, k: xt_hl[z][:, k, columns(m % 2)]).then_inc(acc_ready, 1)
                for c in range(2):
                    pe.wait_ge(vw_lo, h * 3 + (2 + c))
                    for t in range(NT):
                        n = c * NT + t
                        begin_acc(acc_at("xv", h, n))
                        product(accb(acc_bank("xv", n)), lambda z, k: xt_hl[z][:, k, tile(t)],
                                lambda z, k: v_hl[z][:, c, k, :]).then_inc(acc_ready, 1)
                        if (c, t) in ((0, 1), (0, 3)):
                            if t == 1:
                                pe.wait_ge(acc_free, acc_at("qk", h, 3) + 1)
                            head_scores(h, t // 2)
                        if (c, t) in ((1, 1), (1, 3)):
                            head_turn(h, t // 2)
                        if (c, t) == (1, 5):
                            head_context(h, 0)
                if first:
                    head_context(h, 1)
                    return
                pe.wait_ge(ow_lo, h * 2)
                for t in range(NT):
                    output_tile(h - 1, t, o_hl)
                    if t == 1:
                        head_context(h, 1)

            step(0, first=True)
            with pe.Fori(1, FH - 1) as h:
                step(h)
            step(FH - 1)
            pe.wait_ge(ow_lo, 2 * FH)
            for t in range(NT):
                output_tile(FH - 1, t, o_hl_last)


_OUT = (N, D)


def kernel(**inputs):
    import numpy as np
    import concourse.bacc as bacc
    from concourse.bass_utils import run_bass_kernel_spmd

    a = {k: np.asarray(v) for k, v in inputs.items()}
    lay = np.ascontiguousarray
    heads = FH
    q = a["L0_ffn_q_w"].reshape(heads, P, KD, P)
    k = a["L0_ffn_k_w"].reshape(heads, P, KD, P)
    qk = np.stack([q, k], 1).transpose(0, 4, 1, 3, 2).reshape(heads, P, 2 * KD * P)
    v = a["L0_ffn_v_w"].reshape(heads, 2, EC, KD, P, P).transpose(0, 4, 1, 3, 2, 5).reshape(heads, P, KD * E * P)
    o = a["L0_ffn_o_w"].reshape(heads, E, P, D).transpose(0, 2, 1, 3).reshape(heads, P, E * D)
    arrays = {
        "x": a["x"].reshape(N, D),
        "ctx_t": a["ctx_1024"][:, :T].reshape(N, D).T,
        "wk": a["L0_xattn_Wk"], "wv": a["L0_xattn_Wv"], "wq": a["L0_xattn_Wq"], "wo": a["L0_xattn_Wo"],
        "wqkv_t": a["L0_attn_Wqkv"].T, "wout_t": a["L0_attn_Wout"].T,
        "sel_v_t": a["L0_ffn_sel_v_w"].T, "sel_o_t": a["L0_ffn_sel_o_w"].T,
        "qk_t": qk, "v_w": v, "o_w": o,
        "bq": a["L0_xattn_bq"].reshape(KD, P).T, "bk": a["L0_xattn_bk"].reshape(KD, P).T,
        "bv": a["L0_xattn_bv"], "bo": a["L0_xattn_bo"], "bout": a["L0_attn_bout"],
        "temp": a["L0_attn_temp"].reshape(XH), "route_scale": a["L0_ffn_route_scale"],
    }
    arrays = {n: lay(v) for n, v in arrays.items()}
    nc = bacc.Bacc("TRN2", target_bir_lowering=False, num_devices=1)
    args = [nc.dram_tensor(n, v.shape, mybir.dt.from_np(v.dtype), kind="ExternalInput").ap()
            for n, v in arrays.items()]
    names = list(arrays)
    byname = dict(zip(names, args))
    out = nc.dram_tensor("out", _OUT, F32, kind="ExternalOutput").ap()
    gate_dram = nc.dram_tensor("gate_dram", (FH * E, N), F32, kind="Internal").ap()
    perceiver_kernel(nc, out=out, gate_dram=gate_dram, **byname)
    r = run_bass_kernel_spmd(nc, [arrays], core_ids=[0])
    return r.results[0]["out"].reshape(B, T, D)
```

```python
from contextlib import ExitStack

import concourse.bass as bass
from concourse import mybir

F32 = mybir.dt.float32
F16 = mybir.dt.float16
ALU = mybir.AluOpType
ACT = mybir.ActivationFunctionType
AX = mybir.AxisListType

P = 128
B, T, D = 32, 32, 512
N = B * T
KD = D // P
NT = N // P
HALF = N // 2
TH = NT // 2
BH = B // 2
XH, XD = 16, 32
HJ = XH // KD
FH, E = 8, 8
EC = E // 2
WSCALE = 64.0
ASCALE = 16.0
MASKED = -1.0e30
LN_EPS = 1e-5

SLOTS = 4
UNITS = 4 * TH

ACC, SPLIT, TURN = 4, 2, 2
ACC_BODY = 4 + 2 * NT + NT


def spread(ticks, filler, first=0, last=None):
    last = len(ticks) if last is None else min(last, len(ticks))
    out, done = [], 0
    for n, tick in enumerate(ticks):
        out += tick
        due = len(filler) if n >= last - 1 else len(filler) * max(0, n + 1 - first) // (last - first)
        out += filler[done:due]
        done = max(done, due)
    return out


def norm_steps(ln, f):
    out = [("var", ln, f), ("rstd", ln, f)]
    return out + [("norm", ln, f, t) for t in range(TH)]


def attention_ticks():
    ticks = []
    for n in range(2 * UNITS + 9):
        tick = []

        def at(lag):
            return (n - lag) // UNITS, (n - lag) % UNITS

        def within(lag):
            return lag <= n < 2 * UNITS + lag

        if within(0):
            tick.append(("s", *at(0)))
        if within(1):
            tick.append(("e", *at(1)))
        if within(4) and n % 2 == 1:
            tick.append(("pv", at(4)[0], at(4)[1] // 2))
        if within(2):
            tick.append(("p", *at(2)))
        if within(6) and (n - 6) % 4 == 3:
            tick.append(("at", at(6)[0], at(6)[1] // 4))
        if within(8) and (n - 8) % 4 == 3:
            tick.append(("wo", at(8)[0], at(8)[1] // 4))
        ticks.append(tick)
    return ticks


def mix_steps(f):
    out = norm_steps(1, f)
    for c in range(KD):
        out.append(("w", f, c))
        if c >= 1:
            out.append(("nsum", f, c - 1))
    out += [("nsum", f, KD - 1), ("inv", f)]
    out += [("bias", 1, f, t) for t in range(TH)]
    out += [("lg", f), ("pi", f), ("pb", f, 0), ("pb", f, 1), ("ps", f), ("pb", f, 2), ("pb", f, 3), ("coef", f)] + [("z", f, c) for c in range(KD)] + [("zlow", f, c) for c in range(KD)]
    out += [("wout", f, t) for t in range(TH)]
    return out


def route_steps(f):
    return norm_steps(2, f) + [("gl", f, t) for t in range(TH)] + [("route", f, 0, part) for part in range(3)]


def route_out_steps(f):
    return [("route", f, 1, part) for part in range(3)] + [("go", f)]


def head0_steps():
    first = [("gate0", 0), ("qk0", 0), ("qk0", 2)] + [("xv0", c * NT + t) for c in range(2) for t in range(TH)]
    rest = [("qk0", 1), ("qk0", 3), ("hs", 0), ("gate0", 1)]
    rest += [("xv0", TH), ("hs", 1), ("xv0", TH + 1), ("xv0", TH + 2), ("he", 0), ("xv0", TH + 3), ("he", 1)]
    rest += [("xv0", NT + TH), ("hp", 0), ("xv0", NT + TH + 1), ("hp", 1), ("hc", 0)]
    rest += [("xv0", NT + TH + 2), ("xv0", NT + TH + 3), ("hc", 1)]
    rest = spread([[x] for x in rest], route_out_steps(1), 2, 11)
    return first, rest


def front_order():
    out = [("split", "ctx0"), ("split", "wk"), ("k", 0, 0), ("k", 0, 1), ("split", "wv"), ("k", 0, 2), ("k", 0, 3)]
    out += [("var", 0, 0), ("rstd", 0, 0), ("split", "wq"), ("v", 0, 0), ("v", 0, 1)]
    out += [("norm", 0, 0, 0), ("v", 0, 2), ("norm", 0, 0, 1), ("v", 0, 3), ("norm", 0, 0, 2), ("norm", 0, 0, 3)]
    out += [("bias", 0, 0, t) for t in range(TH)] + [("var", 0, 1), ("rstd", 0, 1), ("split", "ctx1")]
    out += [("q", 0, c) for c in range(KD)]
    ticks = attention_ticks()
    kv1 = [("k", 1, c) for c in range(KD)] + [("v", 1, t) for t in range(TH)]
    ln1 = norm_steps(0, 1)[2:] + [("bias", 0, 1, t) for t in range(TH)]
    early = [("split", "wo")] + kv1 + ln1 + [("q", 1, c) for c in range(KD)] + [("split", "wqkv"), ("split", "wout")]
    mix0 = [("spread",)] + mix_steps(0)
    cut = UNITS + 9
    out += spread(ticks[:UNITS], early)
    out += spread(ticks[UNITS:cut], [])
    out += spread(ticks[cut:], mix0[:MIX_CUT], MIX_START)
    first, rest = head0_steps()
    weights0 = [("ew", part) for part in range(3)]
    chain0 = mix0[MIX_CUT:] + [("split", "sel")] + route_steps(0)
    at = len(chain0) - EW_AT
    chain0 = chain0[:at] + weights0 + chain0[at:]
    chain1 = mix_steps(1)
    out += spread([[x] for x in chain0], chain1[:CHAIN_CUT])
    second = [[x] for x in chain1[CHAIN_CUT:] + route_steps(1)]
    second[:8] = [a + b for a, b in zip(second[:8], [[x] for x in route_out_steps(0)] + [[]] * 4)]
    out += spread(second, first, FILL_START, FILL_END)
    return place_halves(out) + rest


def place_halves(steps):
    out, highs, lows = [], [], []

    def flush(queue, n=0):
        while len(queue) > n:
            key, _ = queue.pop(0)
            if queue is highs:
                flush(lows)
                out.append(("high", *key))
                lows.append((key, len(steps_done)))
            else:
                out.append(("low", *key))

    steps_done = []
    for x in steps:
        steps_done.append(x)
        now = len(steps_done)
        if x[0] in ("q", "w", "gl", "wo", "qk0", "xv0"):
            flush(highs)
            flush(lows)
        if lows and now - lows[0][1] >= LOW_LAG:
            flush(lows)
        if x[0] == "at":
            flush(highs)
        out.append(x)
        if x[0] == "norm":
            flush(highs)
            highs.append(((f"x{x[1] + 1}", *x[2:]), now))
        elif x[0] == "at":
            highs.append((x, now))
            flush(highs)
        elif highs and now - highs[0][1] >= HIGH_LAG:
            flush(highs)
    flush(highs)
    flush(lows)
    return out


HIGH_LAG = 1
LOW_LAG = 3
EW_AT = 3
MIX_START = 0
MIX_CUT = 30
CHAIN_CUT = 22
FILL_START = 0
FILL_END = 40
FRONT = front_order()
_ACC = [x for x in FRONT if x[0] in ("k", "v", "q", "s", "pv", "wo", "w", "lg", "ps", "pb", "wout", "gl", "qk0", "xv0")]
_SPLIT = [(f"x{x[1] + 1}", *x[2:]) if x[0] == "norm" else x for x in FRONT if x[0] in ("norm", "at")]
_TURN = [x for x in FRONT if x[0] in ("p", "pi", "go")]
ACC_AT = {k: n for n, k in enumerate(_ACC)}
SPLIT_AT = {k: n for n, k in enumerate(_SPLIT)}
TURN_AT = {k: n for n, k in enumerate(_TURN)}
NORM_AT = {x[1:]: n for n, x in enumerate(y for y in FRONT if y[0] == "norm")}
RSTD_AT = {x[1:]: n for n, x in enumerate(y for y in FRONT if y[0] == "rstd")}
VAR_AT = {x[1:]: n for n, x in enumerate(y for y in FRONT if y[0] == "var")}
assert len(_SPLIT) % SPLIT == 0 and len(_TURN) % TURN == 0 and ACC_BODY % ACC == 0


def acc_at(kind, h, n):
    off = {"qk": 0, "xv": 4, "out": 4 + 2 * NT}[kind] + n
    if kind == "out":
        h = h + 1
        if isinstance(h, int) and h == FH:
            return len(_ACC) + (FH - 1) * ACC_BODY + n
    elif isinstance(h, int) and h == 0:
        return ACC_AT[kind + "0", n]
    return h * ACC_BODY + (len(_ACC) - ACC_BODY + off)


def acc_bank(kind, n):
    off = {"qk": 0, "xv": 4, "out": 4 + 2 * NT}[kind] + n
    return (len(_ACC) + off) % ACC


def split_at(h, f):
    return h * 2 + (len(_SPLIT) + f)


def turn_at(kind, h, f):
    return h * 4 + (len(_TURN) + {"p": 0, "ctx": 2}[kind] + f)


def perceiver_kernel(nc, x, ctx_t, wk, wv, wq, wo, wqkv_t, wout_t, sel_v_t, sel_o_t,
                     qk_t, v_w, o_w, bq, bk, bv, bo, bout, temp, route_scale, out, gate_dram):
    ctx = ExitStack()
    with ctx:
        def sb(name, shape, dt=F32):
            return ctx.enter_context(nc.sbuf_tensor(name, shape, dt))

        def sem(name):
            return ctx.enter_context(nc.semaphore(name))

        KB = 256
        r_stage = sb("r_stage", [P, 16 * KB])
        r_split = sb("r_split", [P, 16 * KB])
        r_qk = sb("r_qk", [P, 32 * KB])
        r_mid = sb("r_mid", [P, 32 * KB])
        r_w = sb("r_w", [P, 32 * KB])
        r_v = sb("r_v", [P, NT * XH * (XD + 1)])
        r_s = sb("r_s", [P, 4 * KB])
        r_p = sb("r_p", [P, 4 * KB])
        r_pt = sb("r_pt", [P, 4 * KB])
        r_att = sb("r_att", [P, 4 * KB])

        xres = sb("xres", [P, NT, D])
        xt_split = sb("xt_split", [P, 16 * KB])
        xn = sb("xn", [P, 2, D])
        bo_row = sb("bo_row", [P, D])
        ident = sb("ident", [P, P])
        mask_causal = sb("mask_causal", [P, P])
        mask_batch = sb("mask_batch", [P, P])
        head_sum = sb("head_sum", [P, KD, XH])
        bias_cols = sb("bias_cols", [P, 2, KD])
        temp_row = sb("temp_row", [P, XH])
        rs_col = sb("rs_col", [P, 1])
        ramp = sb("ramp", [P, E])
        stats = sb("stats", [P, 2, TH, 6])
        mv = sb("mv", [P, 2, TH, 2])
        var = sb("var", [P, 2, TH])
        rstd = sb("rstd", [P, 2, TH])
        nw = sb("nw", [P, 2, TH])
        shift = sb("shift", [P, 2, TH])
        lsum = sb("lsum", [P, 2, 2, TH])
        pi_sum = sb("pi_sum", [XH, 2, BH])
        bv_row = sb("bv_row", [P, D])
        smax = sb("smax", [P, SLOTS, 4])
        ssum = sb("ssum", [P, 2, 4])
        rinv = sb("rinv", [P, 2, 8])
        gsm = sb("gsm", [P, 5, TH * 2 * FH])
        bsm = sb("bsm", [P, 2, 4, KD, BH])
        gate_h = sb("gate_h", [P, NT, E])

        def half_view(region, off, shape, names, **kw):
            size = 1
            for s in shape:
                size *= s
            return region[:, off * KB:].bitcast(F16)[:, 0:size].rearrange(names, **kw)

        def words(region, off, size):
            return region[:, off:off + size]

        ctx_stage = r_stage[:, :].rearrange("p (k n) -> p k n", k=KD)
        ctx_hl = [half_view(r_split, 8 * s, (KD, N), "p (k n) -> p k n", k=KD) for s in range(2)]
        wstage4 = [words(r_mid, 8 * KB * s, 8 * KB).rearrange("p (k n) -> p k n", k=KD) for s in range(4)]
        sel_stage = words(r_pt, 0, KD * P).rearrange("p (k n) -> p k n", k=KD)
        w_hl = [[half_view(r_w, 8 * s + 4 * z, (KD, D), "p (k n) -> p k n", k=KD) for z in range(2)]
                for s in range(4)]
        sel_hl = [half_view(r_w, 16 + 4 * z, (KD, P), "p (k n) -> p k n", k=KD) for z in range(2)]
        xt_hl = [half_view(xt_split, 8 * s, (KD, N), "p (k n) -> p k n", k=KD) for s in range(2)]
        qT, kT, wn2 = [], [], []
        for f in range(2):
            qT.append(words(r_qk, 16 * KB * f, 8 * KB).rearrange("p (c n) -> p c n", c=KD))
            kT.append(words(r_qk, (16 * f + 8) * KB, 8 * KB).rearrange("p (c n) -> p c n", c=KD))
            wn2.append(qT[f])
        vones = r_v[:, :].rearrange("p (t h d) -> p t h d", t=NT, h=XH)

        def slots(region, n):
            return ([words(region, 2 * KB * s, D) for s in range(2)]
                    + [words(r_stage, (4 * n + 2 * s) * KB, D) for s in range(2)])

        sbuf, pbuf, ptbuf, attn = slots(r_s, 0), slots(r_p, 1), slots(r_pt, 2), slots(r_att, 3)
        wT = [words(r_mid, 16 * KB * f, 8 * KB).rearrange("p (c n) -> p c n", c=KD) for f in range(2)]
        sqT = [words(r_mid, (16 * f + 8) * KB, 8 * KB).rearrange("p (c n) -> p c n", c=KD) for f in range(2)]
        head_spread = words(r_qk, 8 * KB, KD * P).rearrange("p (c j) -> p c j", c=KD)
        piT = [words(r_qk, (10 + 2 * f) * KB, D) for f in range(2)]
        pi = [words(r_qk, 14 * KB + 64 * f, TH * XH).rearrange("p (t h) -> p t h", t=TH) for f in range(2)]
        route_buf = [words(r_qk, (24 + 2 * i) * KB, D) for i in range(4)]
        gates = words(r_att, 0, NT * 2 * FH * E).rearrange("p (t g) -> p t g", t=NT)
        goT = r_pt[0:FH * E, :]
        stage_v = r_stage[:, :].rearrange("p (c n) -> p c n", c=2)
        v_hl = [half_view(r_split, 8 * z, (2, KD, EC * P), "p (c k n) -> p c k n", c=2, k=KD) for z in range(2)]
        o_hl = [half_view(r_w, 8 * z, (E, D), "p (e n) -> p e n", e=E) for z in range(2)]
        o_hl_last = [half_view(r_split, 8 * z, (E, D), "p (e n) -> p e n", e=E) for z in range(2)]
        prod = [words(r_w, (16 + 4 * s) * KB, E * P).rearrange("p (e n) -> p e n", e=E) for s in range(2)]
        ctxT = words(r_w, 24 * KB, N)
        v_head = words(r_w, 28 * KB, NT * P).rearrange("p (t d) -> p t d", t=NT)
        stage_qk = words(r_v, 0, 4 * KB)
        qk_hl = [half_view(r_v, 4 + 2 * z, (2, KD, P), "p (m k n) -> p m k n", m=2, k=KD) for z in range(2)]
        qkT = words(r_v, 8 * KB, 8 * KB).rearrange("p (m n) -> p m n", m=2)
        gate_b = r_qk[:, :].rearrange("p (e n) -> p e n", e=E)
        gated = [half_view(r_mid, 16 * z, (NT, E, P), "p (t e n) -> p t e n", t=NT, e=E) for z in range(2)]

        psum = [ctx.enter_context(nc.psum_tensor(f"bank{i}", [P, 512], F32)) for i in range(8)]

        def accb(n):
            return psum[n % ACC]

        def splitb(n):
            return psum[ACC + n % SPLIT]

        def turnb(n):
            return psum[ACC + SPLIT + n % TURN]

        SPLITS = ["ctx0", "wk", "wv", "ctx1", "wq", "wo", "wqkv", "wout", "sel"]
        POOL_SPLITS = ["wo", "wqkv", "wout", "sel"]

        ld_ctx = [sem(f"ld_ctx{f}") for f in range(2)]
        ld_w = [sem(f"ld_w{i}") for i in range(7)]
        ld_x = [sem(f"ld_x{t}") for t in range(NT)]
        ld_bias, ld_bv, ld_bo, ld_bout = sem("ld_bias"), sem("ld_bv"), sem("ld_bo"), sem("ld_bout")
        ld_exp, ld_qk, ld_gate = sem("ld_exp"), sem("ld_qk"), sem("ld_gate")
        gate_stored, out_stored = sem("gate_stored"), sem("out_stored")
        cst, consts_ready, ones_ready, spread_ready = sem("cst"), sem("consts_ready"), sem("ones_ready"), sem("spread_ready")
        headsum_ready = sem("headsum_ready")
        acc_ready, acc_free = sem("acc_ready"), sem("acc_free")
        split_ready, split_hi, split_free = sem("split_ready"), sem("split_hi"), sem("split_free")
        turn_ready, turn_free = sem("turn_ready"), sem("turn_free")
        w_hi = {n: sem(f"hi_{n}") for n in SPLITS}
        w_lo = {n: sem(f"lo_{n}") for n in SPLITS}
        w_scaled = sem("w_scaled")
        var_ready, std_ready, xn_ready = sem("var_ready"), sem("std_ready"), sem("xn_ready")
        rstd_ready = sem("rstd_ready")
        bias_added = [sem("bo_added"), sem("bout_added")]
        max_ready, sub_ready, exp_ready, att_ready = sem("max_ready"), sem("sub_ready"), sem("exp_ready"), sem("att_ready")
        rsum_ready, norm_ready = sem("rsum_ready"), sem("norm_ready")
        sq_ready, inv_ready = sem("sq_ready"), sem("inv_ready")
        wn2_first, wn2_last = sem("wn2_first"), sem("wn2_last")
        lexp_ready, pi_ready, pisum_ready, coef_ready = (sem("lexp_ready"), sem("pi_ready"), sem("pisum_ready"),
                                                         sem("coef_ready"))
        z_ready, z_hi, z_lo = sem("z_ready"), sem("z_hi"), sem("z_lo")
        rl_ready, prob_ready = sem("rl_ready"), sem("prob_ready")
        gates_v_ready, gates_o_ready = sem("gates_v_ready"), sem("gates_o_ready")
        vw_hi, vw_lo, ow_hi, ow_lo = sem("vw_hi"), sem("vw_lo"), sem("ow_hi"), sem("ow_lo")
        prod_ready, gated_hi, gated_lo = sem("prod_ready"), sem("gated_hi"), sem("gated_lo")
        dve_step, pool_step = sem("dve_step"), sem("pool_step")

        def split_operands(name):
            if name == "ctx0" or name == "ctx1":
                f = int(name[3])
                n = slice(f * HALF, (f + 1) * HALF)
                return ctx_stage[:, :, n], [c[:, :, n] for c in ctx_hl], 1.0, ld_ctx[f], 16
            i = ["wk", "wv", "wq", "wo", "wqkv", "wout", "sel"].index(name)
            if name == "sel":
                return sel_stage, sel_hl, WSCALE, ld_w[6], 32
            src = wstage4[i if i < 4 else i - 2]
            return src, w_hl[i if i < 4 else i - 4], WSCALE, ld_w[i], 16

        block = ctx.enter_context(nc.Block())

        @block.sync
        def _(sp):
            ctx_v = ctx_t.rearrange("(k p) n -> p k n", p=P)

            def weight(w):
                return w.rearrange("(k p) n -> p k n", p=P)

            sp.dma_start(ctx_stage[:, :, 0:HALF], ctx_v[:, :, 0:HALF]).then_inc(ld_ctx[0], 16)
            sp.dma_start(wstage4[1], weight(wv)).then_inc(ld_w[1], 16)
            sp.dma_start(wstage4[2], weight(wq)).then_inc(ld_w[2], 16)
            sp.dma_start(ctx_stage[:, :, HALF:N], ctx_v[:, :, HALF:N]).then_inc(ld_ctx[1], 16)
            sp.dma_start(wstage4[3], weight(wo)).then_inc(ld_w[3], 16)
            sp.wait_ge(w_lo["wq"], 1)
            sp.dma_start(wstage4[2], weight(wqkv_t)).then_inc(ld_w[4], 16)
            sp.wait_ge(w_lo["wo"], 1)
            sp.dma_start(wstage4[3], weight(wout_t)).then_inc(ld_w[5], 16)
            sp.wait_ge(bias_added[0], NT)
            sp.dma_start(bo_row[:, :], bout.partition_broadcast(P)).then_inc(ld_bout, 16)
            sp.wait_ge(split_ready, SPLIT_AT["at", 1, TH - 1] + 1)
            sp.dma_start(sel_stage[:, :, 0:FH * E], weight(sel_v_t)).then_inc(ld_w[6], 16)
            sp.dma_start(sel_stage[:, :, FH * E:P], weight(sel_o_t)).then_inc(ld_w[6], 16)
            sp.dma_start(stage_qk, qk_t[0]).then_inc(ld_qk, 16)
            sp.dma_start(r_stage[:, :], v_w[0]).then_inc(ld_exp, 16)
            sp.wait_ge(vw_lo, 3)
            sp.dma_start(r_stage[:, :], v_w[1]).then_inc(ld_exp, 16)
            sp.dma_start(stage_qk, qk_t[1]).then_inc(ld_qk, 16)
            sp.wait_ge(turn_free, TURN_AT["go", 1] + 1)
            sp.dma_start(gate_dram, goT).then_inc(gate_stored, 16)
            sp.wait_ge(gate_stored, 16)
            sp.dma_start(gate_b, gate_dram[0:E, :].partition_broadcast(P)).then_inc(ld_gate, 16)

            def step(h, last=False):
                sp.wait_ge(vw_lo, h * 3 + 3)
                sp.dma_start(r_stage[:, :], o_w[bass.ds(h - 1, 1)][0]).then_inc(ld_exp, 16)
                sp.wait_ge(prod_ready, h * NT)
                sp.dma_start(gate_b, gate_dram[bass.ds(h * E, E), :].partition_broadcast(P)).then_inc(ld_gate, 16)
                sp.wait_ge(ow_lo, h * 2)
                if not last:
                    sp.dma_start(r_stage[:, :], v_w[bass.ds(h + 1, 1)][0]).then_inc(ld_exp, 16)
                    sp.dma_start(stage_qk, qk_t[bass.ds(h + 1, 1)][0]).then_inc(ld_qk, 16)
                else:
                    sp.dma_start(r_stage[:, :], o_w[h]).then_inc(ld_exp, 16)

            with sp.Fori(1, FH - 1) as h:
                step(h)
            step(FH - 1, last=True)
            out_v = out.rearrange("(t p) d -> t p d", p=P)
            for t in range(NT):
                sp.wait_ge(acc_free, acc_at("out", FH - 1, t) + 1)
                sp.dma_start(out_v[t], xres[:, t, :]).then_inc(out_stored, 16)
            sp.wait_ge(out_stored, 16 * NT)

        @block.gpsimd
        def _(pool):
            steps = [0]

            def link(ins):
                steps[0] += 1
                ins.then_inc(pool_step, 1)
                pool.wait_ge(pool_step, steps[0])

            def select(view, pattern, base, mult, op, fill):
                return pool.affine_select(out=view, in_=view, pattern=pattern, compare_op=op, fill=fill,
                                          base=base, channel_multiplier=mult)

            link(pool.memset(ident[:, :], 0.0))
            link(pool.memset(mask_causal[:, :], 0.0))
            link(pool.memset(mask_batch[:, :], 0.0))
            link(select(ident[:, :], [[-1, P]], 0, 1, ALU.not_equal, 1.0))
            pool.memset(vones[:, :, :, XD:XD + 1], 1.0).then_inc(ones_ready, 1)
            mc = mask_causal[:, :].rearrange("p (b j) -> p b j", b=P // T)
            mb = mask_batch[:, :].rearrange("p (b j) -> p b j", b=P // T)
            link(select(mc, [[-T, P // T], [-1, T]], 0, 1, ALU.is_ge, MASKED))
            link(select(mc, [[T, P // T], [0, T]], T - 1, -1, ALU.is_ge, MASKED))
            link(select(mb, [[-T, P // T], [0, T]], 0, 1, ALU.is_ge, MASKED))
            link(select(mb, [[T, P // T], [0, T]], T - 1, -1, ALU.is_ge, MASKED))
            link(pool.memset(head_sum[:, :, :], 1.0))
            link(select(head_sum[:, :, :], [[P, KD], [-XD, XH]], 0, 1, ALU.is_ge, 0.0))
            link(select(head_sum[:, :, :], [[-P, KD], [XD, XH]], XD - 1, -1, ALU.is_ge, 0.0))
            for e in range(E):
                last = pool.memset(ramp[:, e:e + 1], float(E - e))
            link(last)
            pool.wait_ge(ld_bias, 16 * 4)
            pool.tensor_tensor(head_sum[:, :, :], head_sum[:, :, :],
                               temp_row[:, :].unsqueeze(1).broadcast_to([P, KD, XH]), ALU.mult)\
                .then_inc(consts_ready, 1)

            def low(name):
                if name not in POOL_SPLITS:
                    return
                src, hl, scale, load, count = split_operands(name)
                pool.wait_ge(w_scaled, POOL_SPLITS.index(name) + 1)
                pool.tensor_tensor(hl[1], src, hl[0], ALU.subtract).then_inc(w_lo[name], 1)

            def bias(block_n, f, t):
                pool.wait_ge([ld_bo, ld_bout][block_n], 16)
                pool.wait_ge(xn_ready, NORM_AT[block_n, f, t] + 1)
                pool.tensor_tensor(xres[:, f * TH + t, :], xres[:, f * TH + t, :], bo_row[:, :], ALU.add)\
                    .then_inc(bias_added[block_n], 1)

            def subtract_max(count, slot):
                pool.wait_ge(max_ready, count)
                s = sbuf[slot].rearrange("p (c k) -> p c k", c=4)
                pool.tensor_tensor(s, s, smax[:, slot, :].unsqueeze(2).broadcast_to([P, 4, P]),
                                   ALU.subtract).then_inc(sub_ready, 1)

            def heads_rows():
                pool.wait_ge(acc_ready, ACC_AT["s", 0, UNITS - 1] + 1)
                link(pool.memset(head_spread[0:XH], 1.0))
                link(select(head_spread[0:XH], [[P, KD], [1, P]], 0, -XD, ALU.is_ge, 0.0))
                select(head_spread[0:XH], [[-P, KD], [-1, P]], XD - 1, XD, ALU.is_ge, 0.0).then_inc(spread_ready, 1)

            def over_norms(f):
                pool.wait_ge(inv_ready, f + 1)
                for c in range(KD // 2, KD):
                    pool.tensor_tensor(wn2[f][:, c, :].rearrange("p (b n) -> p b n", b=BH),
                                       sqT[f][:, c, :].rearrange("p (b n) -> p b n", b=BH),
                                       bsm[:, f, 0, c, :].unsqueeze(2).broadcast_to([P, BH, T]),
                                       ALU.mult).then_inc(wn2_last, 1)

            def weigh(f, c):
                pool.wait_ge(coef_ready, f + 1)
                wb = wT[f][:, c, :].rearrange("p (b n) -> p b n", b=BH)
                pool.tensor_tensor(wb, wb, bsm[:, f, 3, c, :].unsqueeze(2).broadcast_to([P, BH, T]),
                                   ALU.mult).then_inc(z_ready, 1)

            def normalise(h, f):
                pool.wait_ge(rsum_ready, h * 2 + (f + 1))
                p = pbuf[f].rearrange("p (c k) -> p c k", c=4)
                pool.tensor_tensor(p, p, ssum[:, f, :].unsqueeze(2).broadcast_to([P, 4, P]),
                                   ALU.mult).then_inc(norm_ready, 1)

            def scores(f, n):
                m = f * UNITS + n
                subtract_max(m + 1, m % SLOTS)

            do = {"split": low, "bias": bias, "s": scores, "spread": heads_rows, "inv": over_norms,
                  "z": weigh, "hs": lambda f: subtract_max(2 * UNITS + f + 1, f), "he": lambda f: normalise(0, f)}
            for kind, *a in FRONT:
                if kind in do:
                    do[kind](*a)
            with pool.Fori(1, FH) as h:
                for f in range(2):
                    subtract_max(h * 2 + (2 * UNITS + f + 1), f)
                for f in range(2):
                    normalise(h, f)

        @block.scalar
        def _(act):
            act.dma_start(wstage4[0], wk.rearrange("(k p) n -> p k n", p=P)).then_inc(ld_w[0], 16)
            x_v = x.rearrange("(t p) d -> t p d", p=P)
            for t in range(TH):
                act.dma_start(xres[:, t, :], x_v[t]).then_inc(ld_x[t], 16)
            act.dma_start(bias_cols[:, 0, :], bq).then_inc(ld_bias, 16)
            act.dma_start(bias_cols[:, 1, :], bk).then_inc(ld_bias, 16)
            act.dma_start(temp_row[:, :], temp.partition_broadcast(P)).then_inc(ld_bias, 16)
            act.dma_start(rs_col[:, :], route_scale.partition_broadcast(P)).then_inc(ld_bias, 16)
            act.dma_start(bv_row[:, :], bv.partition_broadcast(P)).then_inc(ld_bv, 16)
            act.dma_start(bo_row[:, :], bo.partition_broadcast(P)).then_inc(ld_bo, 16)
            for t in range(TH, NT):
                act.dma_start(xres[:, t, :], x_v[t]).then_inc(ld_x[t], 16)

            def high(name):
                src, hl, scale, load, count = split_operands(name)
                act.wait_ge(load, count)
                if name == "wqkv":
                    act.wait_ge(acc_ready, ACC_AT["k", 1, KD - 1] + 1)
                if name == "wout":
                    act.wait_ge(acc_ready, ACC_AT["v", 1, TH - 1] + 1)
                if name == "sel":
                    act.wait_ge(acc_ready, ACC_AT["q", 1, KD - 1] + 1)
                act.activation(hl[0], src, ACT.Copy, scale=scale).then_inc(w_hi[name], 1)
                if name in POOL_SPLITS:
                    act.wait_ge(w_hi[name], 1)
                    act.activation(src, src, ACT.Copy, scale=scale).then_inc(w_scaled, 1)

            def high_turned(key, f, a):
                g = SPLIT_AT[key, f, a]
                t = f * TH + a
                act.wait_ge(split_ready, g + 1)
                act.activation(xt_hl[0][:, :, t * P:(t + 1) * P],
                               splitb(g)[:, :].rearrange("p (k n) -> p k n", k=KD), ACT.Copy)\
                    .then_inc(split_hi, 1)

            def std(ln, f):
                act.wait_ge(var_ready, VAR_AT[ln, f] + 1)
                act.activation(rstd[:, f, :], var[:, f, :], ACT.Sqrt).then_inc(std_ready, 1)

            def norm(ln, f, t):
                n = NORM_AT[ln, f, t]
                act.wait_ge(rstd_ready, RSTD_AT[ln, f] + 1)
                if n >= 2:
                    o = next(k for k, v in NORM_AT.items() if v == n - 2)
                    act.wait_ge(split_ready, SPLIT_AT[f"x{o[0] + 1}", o[1], o[2]] + 1)
                act.activation(xn[:, n % 2, :], xres[:, f * TH + t, :], ACT.Identity, scale=rstd[:, f, t:t + 1],
                               bias=shift[:, f, t:t + 1]).then_inc(xn_ready, 1)

            def exp_scores(f, n):
                m = f * UNITS + n
                act.wait_ge(sub_ready, m + 1)
                if m >= SLOTS:
                    act.wait_ge(turn_ready, TURN_AT["p", (m - SLOTS) // UNITS, (m - SLOTS) % UNITS] + 1)
                act.activation(pbuf[m % SLOTS], sbuf[m % SLOTS], ACT.Exp, scale=float(XD) ** -0.5)\
                    .then_inc(exp_ready, 1)

            def take_turned(f, n):
                g = TURN_AT["p", f, n]
                m = f * UNITS + n
                act.wait_ge(turn_ready, g + 1)
                if m >= SLOTS:
                    u = (m - SLOTS) // 2
                    act.wait_ge(acc_ready, ACC_AT["pv", u // (UNITS // 2), u % (UNITS // 2)] + 1)
                act.copy(ptbuf[m % SLOTS], turnb(g)[:, :]).then_inc(turn_free, 1)

            def squares(f, c):
                act.wait_ge(acc_free, ACC_AT["w", f, c] + 1)
                if (f, c) == (1, 0):
                    act.wait_ge(w_lo["wout"], 1)
                act.activation(sqT[f][:, c, :], wT[f][:, c, :], ACT.Square).then_inc(sq_ready, 1)

            def exp_logits(f):
                act.wait_ge(acc_free, ACC_AT["lg", f] + 1)
                act.activation(pi[f], pi[f], ACT.Exp).then_inc(lexp_ready, 1)

            def take_pi(f):
                g = TURN_AT["pi", f]
                act.wait_ge(turn_ready, g + 1)
                act.copy(piT[f][0:XH], turnb(g)[0:XH, :]).then_inc(turn_free, 1)

            def high_z(f, c):
                act.wait_ge(z_ready, f * KD + c + 1)
                act.activation(xt_hl[0][:, c, f * HALF:(f + 1) * HALF], wT[f][:, c, :], ACT.Copy)\
                    .then_inc(z_hi, 1)

            def probabilities(f, m, part):
                if (m, part) != (0, 0):
                    return
                act.wait_ge(rl_ready, f + 1)
                act.activation(route_buf[1], route_buf[0], ACT.Sigmoid).then_inc(prob_ready, 1)

            def take_gates(f):
                g = TURN_AT["go", f]
                act.wait_ge(w_lo["sel"], 1)
                act.wait_ge(turn_ready, g + 1)
                act.copy(goT[:, f * HALF:(f + 1) * HALF], turnb(g)[0:FH * E, :]).then_inc(turn_free, 1)

            def weights_high(h, part):
                if part == 0:
                    act.wait_ge(ld_qk, h * 16 + 16)
                    act.activation(qk_hl[0], stage_qk.rearrange("p (m k n) -> p m k n", m=2, k=KD), ACT.Copy,
                                   scale=WSCALE).then_inc(vw_hi, 1)
                    return
                act.wait_ge(ld_exp, 16 if isinstance(h, int) and h == 0 else h * 32)
                c = part - 1
                act.activation(v_hl[0][:, c], stage_v[:, c].rearrange("p (k n) -> p k n", k=KD), ACT.Copy,
                               scale=WSCALE).then_inc(vw_hi, 1)

            def out_weights_high(h, hl, c):
                act.wait_ge(ld_exp, h * 32 + 48 if not (isinstance(h, int) and h == FH - 1) else 32 * FH)
                act.activation(hl[0][:, c * EC:(c + 1) * EC],
                               stage_v[:, c].rearrange("p (e n) -> p e n", e=EC), ACT.Copy,
                               scale=WSCALE).then_inc(ow_hi, 1)

            def exp_head(h, f):
                act.wait_ge(sub_ready, h * 2 + (2 * UNITS + f + 1))
                first = isinstance(h, int) and h == 0
                act.wait_ge(turn_ready, TURN_AT["p", 1, UNITS - 1] + 1 if first else turn_at("p", h - 1, f) + 1)
                act.activation(pbuf[f], sbuf[f], ACT.Exp, scale=float(P) ** -0.5).then_inc(exp_ready, 1)

            def take_head(h, f):
                if isinstance(h, int) and h == 0:
                    act.wait_ge(gate_stored, 16)
                act.wait_ge(turn_ready, turn_at("p", h, f) + 1)
                act.copy(ptbuf[f], turnb(f)[:, :]).then_inc(turn_free, 1)

            def take_context(h, f):
                act.wait_ge(turn_ready, turn_at("ctx", h, f) + 1)
                if not (isinstance(h, int) and h == 0):
                    act.wait_ge(prod_ready, h * NT)
                act.copy(ctxT[:, f * HALF:(f + 1) * HALF], turnb(f)[:, :]).then_inc(turn_free, 1)

            def gated_high(h, t):
                act.wait_ge(prod_ready, h * NT + (t + 1))
                if not (isinstance(h, int) and h == 0):
                    act.wait_ge(acc_ready, acc_at("out", h - 1, t) + 1)
                act.activation(gated[0][:, t], prod[t % 2], ACT.Copy).then_inc(gated_hi, 1)

            def gating(h, last=False):
                for t in range(NT):
                    if t % TH == 2 % TH and t < TH:
                        take_context(h, 1)
                    gated_high(h, t)
                    if t == 1:
                        act.wait_ge(acc_ready, acc_at("xv", h, 2 * NT - 1) + 1)
                    if t in (1, 3, 5):
                        if not last:
                            weights_high(h + 1, t // 2)
                        elif t > 1:
                            out_weights_high(h, o_hl_last, t // 2 - 1)

            def step(h, last=False):
                act.wait_ge(acc_ready, acc_at("out", h - 2, NT - 1) + 1)
                for f in range(2):
                    exp_head(h, f)
                for c in range(2):
                    out_weights_high(h - 1, o_hl, c)
                for f in range(2):
                    take_head(h, f)
                take_context(h, 0)
                gating(h, last)

            do = {"split": high, "var": std, "norm": norm, "high": high_turned, "e": exp_scores, "p": take_turned, "w": squares,
                  "lg": exp_logits, "pi": take_pi, "z": high_z, "route": probabilities, "go": take_gates,
                  "ew": lambda part: weights_high(0, part),
                  "hs": lambda f: exp_head(0, f), "hp": lambda f: take_head(0, f)}
            for kind, *a in FRONT:
                if kind in do:
                    do[kind](*a)
            take_context(0, 0)
            gating(0)
            with act.Fori(1, FH - 1) as h:
                step(h)
            step(FH - 1, last=True)

        @block.vector
        def _(dve):
            steps = [0, None]

            def link(ins):
                steps[0] += 1
                ins.then_inc(dve_step, 1)
                dve.wait_ge(dve_step, steps[0] if steps[1] is None else steps[1] + steps[0])

            def low(name):
                if name in POOL_SPLITS:
                    return
                src, hl, scale, load, count = split_operands(name)
                dve.wait_ge(w_hi[name], 1)
                dve.scalar_tensor_tensor(out=hl[1], in0=src, scalar=scale, in1=hl[0], op0=ALU.mult,
                                         op1=ALU.subtract).then_inc(w_lo[name], 1)

            def low_turned(key, f, a):
                g = SPLIT_AT[key, f, a]
                t = f * TH + a
                dve.wait_ge(split_hi, g + 1)
                dve.tensor_tensor(xt_hl[1][:, :, t * P:(t + 1) * P],
                                  splitb(g)[:, :].rearrange("p (k n) -> p k n", k=KD),
                                  xt_hl[0][:, :, t * P:(t + 1) * P], ALU.subtract).then_inc(split_free, 1)

            def variance(ln, f):
                if ln:
                    dve.wait_ge(xn_ready, NORM_AT[ln - 1, f, TH - 1] + 1)
                    statistics(["wo", "wout"][ln - 1], f, TH - 1)
                else:
                    for t in range(TH):
                        dve.wait_ge(ld_x[f * TH + t], 16)
                        dve.bn_stats(stats[:, f, t, :], xres[:, f * TH + t, :]).then_inc(dve_step, 1)
                        steps[0] += 1
                dve.wait_ge(dve_step, steps[0])
                for t in range(TH):
                    last = dve.bn_aggr(mv[:, f, t, :], stats[:, f, t, :])
                link(last)
                dve.tensor_scalar(var[:, f, :], mv[:, f, :, 1], LN_EPS, None, ALU.add).then_inc(var_ready, 1)

            def inverse_std(ln, f):
                r, n = rstd[:, f, :], nw[:, f, :]
                dve.wait_ge(std_ready, VAR_AT[ln, f] + 1)
                link(dve.reciprocal(r, r))
                link(dve.tensor_tensor(n, r, r, ALU.mult))
                link(dve.tensor_tensor(n, n, var[:, f, :], ALU.mult))
                link(dve.tensor_scalar(n, n, -0.5, 1.5, ALU.mult, ALU.add))
                link(dve.tensor_tensor(r, r, n, ALU.mult))
                dve.scalar_tensor_tensor(out=shift[:, f, :], in0=mv[:, f, :, 0], scalar=-1.0, in1=r,
                                         op0=ALU.mult, op1=ALU.mult).then_inc(rstd_ready, 1)

            def acc(*key):
                g = ACC_AT[key]
                dve.wait_ge(acc_ready, g + 1)
                return accb(g)

            def keys(f, c):
                if f == c == 0:
                    dve.wait_ge(ld_bias, 64)
                dve.tensor_scalar(kT[f][:, c, :], acc("k", f, c)[:, :], 1.0 / WSCALE,
                                  bias_cols[:, 1, c:c + 1], ALU.mult, ALU.add).then_inc(acc_free, 1)

            def values(f, t):
                if f == t == 0:
                    dve.wait_ge(ld_bv, 16)
                    dve.wait_ge(ones_ready, 1)
                dve.scalar_tensor_tensor(out=vones[:, f * TH + t, :, 0:XD],
                                         in0=acc("v", f, t)[:, :].rearrange("p (h d) -> p h d", h=XH),
                                         scalar=1.0 / WSCALE, in1=bv_row[:, :].rearrange("p (h d) -> p h d", h=XH),
                                         op0=ALU.mult, op1=ALU.add).then_inc(acc_free, 1)

            def queries(f, c):
                dve.tensor_scalar(qT[f][:, c, :], acc("q", f, c)[:, :], 1.0 / WSCALE,
                                  bias_cols[:, 0, c:c + 1], ALU.mult, ALU.add).then_inc(acc_free, 1)

            def mask_and_max(bank, mask, slot, free, freed, exps):
                if exps is not None:
                    dve.wait_ge(exp_ready, exps)
                dve.tensor_tensor(sbuf[slot].rearrange("p (c k) -> p c k", c=4),
                                  bank[:, :].rearrange("p (c k) -> p c k", c=4),
                                  mask[:, :].unsqueeze(1).broadcast_to([P, 4, P]), ALU.add).then_inc(free, 1)
                dve.wait_ge(free, freed)
                dve.tensor_reduce(smax[:, slot, :], sbuf[slot].rearrange("p (c k) -> p c k", c=4), AX.X,
                                  ALU.max).then_inc(max_ready, 1)

            def scores(f, n):
                m = f * UNITS + n
                if m == 0:
                    dve.wait_ge(consts_ready, 1)
                mask_and_max(acc("s", f, n), mask_causal, m % SLOTS, acc_free, ACC_AT["s", f, n] + 1,
                             m - SLOTS + 1 if m >= SLOTS else None)

            def attended(f, a):
                t, half = a // 2, a % 2
                b = acc("pv", f, a)
                o = b[:, 0:8 * (XD + 1)].rearrange("p (j c d) -> p j c d", j=2, c=KD)
                n = f * TH + t
                if n >= SLOTS and half == 0:
                    dve.wait_ge(split_ready, SPLIT_AT["at", (n - SLOTS) // TH, (n - SLOTS) % TH] + 1)
                r = rinv[:, a % 2, :].rearrange("p (j c) -> p j c", j=2)
                dve.wait_ge(acc_free, ACC_AT["pv", f, a])
                link(dve.reciprocal(r, o[:, :, :, XD]))
                att = attn[n % SLOTS].rearrange("p (c j d) -> p j c d", c=KD, j=HJ)
                for j in range(2):
                    ins = dve.tensor_tensor(att[:, 2 * half + j], o[:, j, :, 0:XD],
                                            r[:, j].unsqueeze(2).broadcast_to([P, KD, XD]), ALU.mult)
                    ins.then_inc(att_ready if j == 0 else acc_free, 1)

            def residual(kind, f, a):
                t = f * TH + a
                dve.wait_ge(bias_added[0 if kind == "wo" else 1], t + 1)
                scale = 1.0 / WSCALE if kind == "wo" else 1.0 / (WSCALE * ASCALE)
                dve.scalar_tensor_tensor(out=xres[:, t, :], in0=acc(kind, f, a)[:, :], scalar=scale,
                                         in1=xres[:, t, :], op0=ALU.mult, op1=ALU.add).then_inc(acc_free, 1)
                if a >= 1:
                    statistics(kind, f, a - 1)

            def statistics(kind, f, a):
                dve.wait_ge(acc_free, ACC_AT[kind, f, a] + 1)
                dve.bn_stats(stats[:, f, a, :], xres[:, f * TH + a, :]).then_inc(dve_step, 1)
                steps[0] += 1

            def spectrum(f, c):
                dve.tensor_scalar(wT[f][:, c, :], acc("w", f, c)[:, :], 1.0 / WSCALE, None, ALU.mult)\
                    .then_inc(acc_free, 1)

            def squares_sum(f, c):
                dve.wait_ge(sq_ready, f * KD + c + 1)
                link(dve.tensor_reduce(bsm[:, f, 1, c, :], sqT[f][:, c, :].rearrange("p (b n) -> p b n", b=BH),
                                       AX.X, ALU.add))

            def inverse_norms(f):
                link(dve.tensor_scalar(bsm[:, f, 1], bsm[:, f, 1], 1e-24, None, ALU.max))
                dve.reciprocal(bsm[:, f, 0], bsm[:, f, 1]).then_inc(inv_ready, 1)
                dve.wait_ge(inv_ready, f + 1)
                for c in range(KD // 2):
                    dve.tensor_tensor(wn2[f][:, c, :].rearrange("p (b n) -> p b n", b=BH),
                                      sqT[f][:, c, :].rearrange("p (b n) -> p b n", b=BH),
                                      bsm[:, f, 0, c, :].unsqueeze(2).broadcast_to([P, BH, T]),
                                      ALU.mult).then_inc(wn2_first, 1)

            def logits(f):
                lg = acc("lg", f)[:, 0:TH * XH].rearrange("p (t h) -> p t h", t=TH)
                link(dve.tensor_reduce(lsum[:, f, 0, :], lg, AX.X, ALU.max))
                dve.tensor_tensor(pi[f], lg, lsum[:, f, 0, :].unsqueeze(2).broadcast_to([P, TH, XH]),
                                  ALU.subtract).then_inc(acc_free, 1)

            def membership(f):
                dve.wait_ge(lexp_ready, f + 1)
                link(dve.tensor_reduce(lsum[:, f, 1, :], pi[f], AX.X, ALU.add))
                link(dve.reciprocal(lsum[:, f, 1, :], lsum[:, f, 1, :]))
                dve.tensor_tensor(pi[f], pi[f], lsum[:, f, 1, :].unsqueeze(2).broadcast_to([P, TH, XH]),
                                  ALU.mult).then_inc(pi_ready, 1)
                dve.wait_ge(turn_free, TURN_AT["pi", f] + 1)
                dve.tensor_reduce(pi_sum[:, f, :], piT[f][0:XH].rearrange("p (b n) -> p b n", b=BH), AX.X,
                                  ALU.add).then_inc(pisum_ready, 1)

            def weighted(f, c):
                b = acc("pb", f, c)
                steps[0] += 1
                dve.tensor_tensor(sqT[f][:, c, :], sqT[f][:, c, :], b[:, :], ALU.mult).then_inc(dve_step, 1)
                dve.tensor_tensor(wT[f][:, c, :], wT[f][:, c, :], b[:, :], ALU.mult).then_inc(acc_free, 1)
                dve.wait_ge(dve_step, steps[0])
                link(dve.tensor_reduce(bsm[:, f, 2, c, :], sqT[f][:, c, :].rearrange("p (b n) -> p b n", b=BH),
                                       AX.X, ALU.add))

            def pi_sums(f):
                b = acc("ps", f)[:, 0:KD * BH].rearrange("p (c b) -> p c b", c=KD)
                dve.tensor_scalar(bsm[:, f, 1], b, 1e-8, None, ALU.add).then_inc(acc_free, 1)
                dve.wait_ge(acc_free, ACC_AT["ps", f] + 1)
                link(dve.reciprocal(bsm[:, f, 0], bsm[:, f, 1]))

            def coefficients(f):
                link(dve.tensor_tensor(bsm[:, f, 2], bsm[:, f, 2], bsm[:, f, 0], ALU.mult))
                link(dve.tensor_scalar(bsm[:, f, 2], bsm[:, f, 2], 1.0, -1.0 / ASCALE, ALU.add, ALU.mult))
                dve.reciprocal(bsm[:, f, 3], bsm[:, f, 2]).then_inc(coef_ready, 1)

            def low_z(f, c):
                n = slice(f * HALF, (f + 1) * HALF)
                dve.wait_ge(z_hi, f * KD + c + 1)
                dve.tensor_tensor(xt_hl[1][:, c, n], wT[f][:, c, :], xt_hl[0][:, c, n], ALU.subtract)\
                    .then_inc(z_lo, 1)

            def router_logits(f, t):
                if f == 1 and t == 0:
                    dve.wait_ge(gates_v_ready, 1)
                    dve.wait_ge(gates_o_ready, 1)
                z = route_buf[0].rearrange("p (t g) -> p t g", t=TH)
                dve.tensor_scalar(z[:, t, :], acc("gl", f, t)[:, 0:P], 1.0 / WSCALE, None, ALU.mult)\
                    .then_inc(acc_free, 1)
                if t == TH - 1:
                    dve.wait_ge(acc_free, ACC_AT["gl", f, t] + 1)
                    dve.sem_inc(rl_ready, 1)

            def route(f, m, part):
                if (m, part) == (0, 0):
                    dve.wait_ge(prob_ready, f + 1)
                shape = [P, TH, FH, E]
                rest, pr, one, two = (b.rearrange("p (t m h e) -> p t m h e", t=TH, m=2, h=FH)[:, :, m]
                                      for b in route_buf)
                rampb = ramp[:, :].unsqueeze(1).unsqueeze(1).broadcast_to(shape)
                m1, m2, at, den = (gsm[:, i, m * TH * FH:(m + 1) * TH * FH].rearrange("p (t h) -> p t h", t=TH)
                                   for i in range(4))

                def wide(v):
                    return v.unsqueeze(3).broadcast_to(shape)

                def pick(hot, values, top):
                    link(dve.tensor_reduce(top, values, AX.X, ALU.max))
                    link(dve.tensor_tensor(hot, values, wide(top), ALU.is_equal))
                    link(dve.tensor_tensor(hot, hot, rampb, ALU.mult))
                    link(dve.tensor_reduce(at, hot, AX.X, ALU.max))
                    link(dve.tensor_tensor(hot, hot, wide(at), ALU.is_equal))

                if part == 0:
                    pick(one, pr, m1)
                    link(dve.scalar_tensor_tensor(out=rest, in0=one, scalar=-4.0, in1=pr, op0=ALU.mult,
                                                  op1=ALU.add))
                elif part == 1:
                    pick(two, rest, m2)
                    link(dve.tensor_tensor(den, m1, m2, ALU.add))
                    link(dve.tensor_scalar(den, den, 1e-9, None, ALU.max))
                    link(dve.reciprocal(at, den))
                    link(dve.tensor_scalar(at, at, rs_col[:, 0:1], None, ALU.mult))
                else:
                    link(dve.tensor_tensor(m1, m1, at, ALU.mult))
                    link(dve.tensor_tensor(m2, m2, at, ALU.mult))
                    link(dve.tensor_tensor(one, one, wide(m1), ALU.mult))
                    link(dve.tensor_tensor(two, two, wide(m2), ALU.mult))
                    out = gates[:, f * TH:(f + 1) * TH, m * FH * E:(m + 1) * FH * E]
                    dve.tensor_tensor(out.rearrange("p t (h e) -> p t h e", e=E), one, two, ALU.add)\
                        .then_inc([gates_v_ready, gates_o_ready][m], 1)

            def first_gates(f):
                dve.wait_ge(gates_v_ready, f + 1)
                n = slice(f * TH, (f + 1) * TH)
                link(dve.tensor_scalar(gate_h[:, n, :], gates[:, n, 0:E], 1.0 / WSCALE, None, ALU.mult))

            def weights_low(h, part):
                dve.wait_ge(vw_hi, h * 3 + (part + 1))
                if part == 0:
                    dve.scalar_tensor_tensor(out=qk_hl[1].rearrange("p m k n -> p (m k n)"), in0=stage_qk,
                                             scalar=WSCALE, in1=qk_hl[0].rearrange("p m k n -> p (m k n)"),
                                             op0=ALU.mult, op1=ALU.subtract).then_inc(vw_lo, 1)
                    return
                c = part - 1
                dve.scalar_tensor_tensor(out=v_hl[1][:, c].rearrange("p k n -> p (k n)"), in0=stage_v[:, c],
                                         scalar=WSCALE, in1=v_hl[0][:, c].rearrange("p k n -> p (k n)"),
                                         op0=ALU.mult, op1=ALU.subtract).then_inc(vw_lo, 1)

            def out_weights_low(h, hl, c):
                dve.wait_ge(ow_hi, h * 2 + (c + 1))
                dve.scalar_tensor_tensor(out=hl[1][:, c * EC:(c + 1) * EC].rearrange("p e n -> p (e n)"),
                                         in0=stage_v[:, c], scalar=WSCALE,
                                         in1=hl[0][:, c * EC:(c + 1) * EC].rearrange("p e n -> p (e n)"),
                                         op0=ALU.mult, op1=ALU.subtract).then_inc(ow_lo, 1)

            def take_out(h, t):
                dve.wait_ge(acc_ready, acc_at("out", h, t) + 1)
                dve.scalar_tensor_tensor(out=xres[:, t, :], in0=accb(acc_bank("out", t))[:, :],
                                         scalar=1.0 / (WSCALE * ASCALE), in1=xres[:, t, :],
                                         op0=ALU.mult, op1=ALU.add).then_inc(acc_free, 1)

            def bank_of(kind, h, n):
                return accb(ACC_AT[kind + "0", n] if isinstance(h, int) and h == 0 else acc_bank(kind, n))

            def take_qk(h, m):
                dve.wait_ge(acc_ready, acc_at("qk", h, m) + 1)
                dve.tensor_scalar(qkT[:, m // 2, (m % 2) * HALF:(m % 2 + 1) * HALF],
                                  bank_of("qk", h, m)[:, :], 1.0 / WSCALE, None, ALU.mult).then_inc(acc_free, 1)

            def take_values(h, n):
                c, t = n // NT, n % NT
                dve.wait_ge(acc_ready, acc_at("xv", h, n) + 1)
                b = bank_of("xv", h, n)
                v = v_head[:, t, :]
                for e in range(EC):
                    scale = gate_h[:, t, c * EC + e:c * EC + e + 1]
                    part = b[:, e * P:(e + 1) * P]
                    if c == 0 and e == 0:
                        ins = dve.tensor_scalar(v, part, scale, None, ALU.mult)
                    else:
                        ins = dve.scalar_tensor_tensor(out=v, in0=part, scalar=scale, in1=v,
                                                       op0=ALU.mult, op1=ALU.add)
                    if e < EC - 1:
                        link(ins)
                ins.then_inc(acc_free, 1)

            def head_scores(h, f):
                dve.wait_ge(split_ready, split_at(h, f) + 1)
                mask_and_max(splitb(f), mask_batch, f, split_free, split_at(h, f) + 1,
                             h * 2 + (2 * UNITS + f - 1))

            def softmax_sums(h, f):
                dve.wait_ge(exp_ready, h * 2 + (2 * UNITS + f + 1))
                link(dve.tensor_reduce(ssum[:, f, :], pbuf[f].rearrange("p (c k) -> p c k", c=4), AX.X, ALU.add))
                dve.reciprocal(ssum[:, f, :], ssum[:, f, :]).then_inc(rsum_ready, 1)

            def gate_context(h, t, first):
                if not (first and t < 2):
                    dve.wait_ge(gated_lo, h * NT + (t - 1))
                c = ctxT[:, t * P:(t + 1) * P].unsqueeze(1).broadcast_to([P, E, P])
                dve.scalar_tensor_tensor(out=prod[t % 2], in0=c, scalar=ASCALE,
                                         in1=gate_b[:, :, t * P:(t + 1) * P], op0=ALU.mult,
                                         op1=ALU.mult).then_inc(prod_ready, 1)

            def gated_low(h, t):
                dve.wait_ge(gated_hi, h * NT + (t + 1))
                dve.tensor_tensor(gated[1][:, t], prod[t % 2], gated[0][:, t], ALU.subtract).then_inc(gated_lo, 1)

            def gating(h, first=False, last=False):
                dve.wait_ge(ld_gate, h * 16 + 16)
                for t in range(NT):
                    if not first:
                        take_out(h - 1, t)
                    if t % TH == 0:
                        dve.wait_ge(turn_free, turn_at("ctx", h, t // TH) + 1)
                    gate_context(h, t, first)
                    if t >= 1:
                        gated_low(h, t - 1)
                    if t in (1, 3, 5):
                        if not last:
                            weights_low(h + 1, t // 2)
                        elif t > 1:
                            out_weights_low(h, o_hl_last, t // 2 - 1)
                gated_low(h, NT - 1)

            def step(h, last=False):
                g = gates[:, :, h * E:(h + 1) * E] if isinstance(h, int) else gates[:, :, bass.ds(h * E, E)]
                link(dve.tensor_scalar(gate_h[:, :, :], g, 1.0 / WSCALE, None, ALU.mult))
                for m in range(4):
                    take_qk(h, m)
                for c in range(2):
                    for t in range(NT):
                        if c == 0 and t % TH == 0:
                            dve.wait_ge(turn_ready, turn_at("ctx", h - 1, t // TH) + 1)
                        take_values(h, c * NT + t)
                        if c == 0 and t in (2, 4):
                            head_scores(h, t // 2 - 1)
                        if c == 0 and t in (5, 7):
                            out_weights_low(h - 1, o_hl, t // 2 - 2)
                        if (c, t) in ((0, 6), (1, 0)):
                            softmax_sums(h, c)
                gating(h, last=last)

            do = {"split": low, "var": variance, "rstd": inverse_std, "low": low_turned, "k": keys, "v": values,
                  "q": queries, "s": scores, "pv": attended, "wo": lambda f, t: residual("wo", f, t),
                  "w": spectrum, "nsum": squares_sum, "inv": inverse_norms, "lg": logits, "pi": membership,
                  "pb": weighted, "ps": pi_sums, "coef": coefficients, "zlow": low_z,
                  "wout": lambda f, t: residual("wout", f, t), "gl": router_logits, "route": route,
                  "ew": lambda part: weights_low(0, part), "gate0": first_gates,
                  "qk0": lambda m: take_qk(0, m), "xv0": lambda n: take_values(0, n),
                  "hs": lambda f: head_scores(0, f), "he": lambda f: softmax_sums(0, f)}
            for kind, *a in FRONT:
                if kind in do:
                    do[kind](*a)
            gating(0, first=True)
            LINKS = 1 + 2 * NT * (EC - 1) + 2
            with dve.Fori(1, FH - 1) as h:
                before, steps[0], steps[1] = steps[0], 0, h * LINKS + (steps[0] - LINKS)
                step(h)
                assert steps[0] == LINKS
            steps[0], steps[1] = before + (FH - 2) * LINKS, None
            step(FH - 1, last=True)
            for t in range(NT):
                take_out(FH - 1, t)

        @block.tensor
        def _(pe):
            def begin_acc(n):
                if not isinstance(n, int) or n >= ACC:
                    pe.wait_ge(acc_free, n - (ACC - 1))

            def product(bank, stat, mov, width=D):
                for k in range(KD):
                    for a, b in ((0, 0), (0, 1), (1, 0)):
                        last = pe.matmul(bank[:, 0:width], stat(a, k), mov(b, k),
                                         start=(k == 0 and (a, b) == (0, 0)), stop=(k == KD - 1 and a == 1))
                return last

            def columns(f):
                return slice(f * HALF, (f + 1) * HALF)

            def tile(t):
                return slice(t * P, (t + 1) * P)

            def begin(*key):
                g = ACC_AT[key]
                begin_acc(g)
                return accb(g)

            def project_t(key, w, src, f, c):
                product(begin(*key), lambda z, k: w[z][:, k, tile(c)], lambda z, k: src[z][:, k, columns(f)])\
                    .then_inc(acc_ready, 1)

            def project_n(key, w, src, t, width=D):
                product(begin(*key), lambda z, k: src[z][:, k, tile(t)], lambda z, k: w[z][:, k, 0:width], width)\
                    .then_inc(acc_ready, 1)

            def split_tiles(key, f, t):
                pe.wait_ge(split_free, SPLIT_AT[key, f, t] + 1)

            def keys(f, c):
                if c == 0:
                    pe.wait_ge(w_lo[f"ctx{f}"], 1)
                    pe.wait_ge(w_lo["wk"], 1)
                project_t(("k", f, c), w_hl[0], ctx_hl, f, c)

            def values(f, t):
                if t == 0:
                    pe.wait_ge(w_lo["wv"], 1)
                project_n(("v", f, t), w_hl[1], ctx_hl, f * TH + t)

            def queries(f, c):
                if c == 0:
                    pe.wait_ge(w_lo["wq"], 1)
                    split_tiles("x1", f, TH - 1)
                project_t(("q", f, c), w_hl[2], xt_hl, f, c)

            def turn_tile(key, src):
                g = SPLIT_AT[key]
                if g >= SPLIT:
                    pe.wait_ge(split_free, g - (SPLIT - 1))
                for k in range(KD):
                    last = pe.transpose(splitb(g)[:, tile(k)], src[:, tile(k)], ident[:, :])
                last.then_inc(split_ready, 1)

            def turn_normed(ln, f, t):
                n = NORM_AT[ln, f, t]
                if n == 0:
                    pe.wait_ge(consts_ready, 1)
                pe.wait_ge(xn_ready, n + 1)
                turn_tile((f"x{ln + 1}", f, t), xn[:, n % 2, :])

            def scores(f, n):
                if n == 0:
                    pe.wait_ge(acc_free, ACC_AT["q", f, KD - 1] + 1)
                bank = begin("s", f, n)
                t, j = n // 4, n % 4
                r = slice(XD * j, XD * (j + 1))
                for c in range(KD):
                    last = pe.matmul(bank[:, tile(c)], qT[f][r, c, tile(t)], kT[f][r, c, tile(t)],
                                     start=True, stop=True)
                last.then_inc(acc_ready, 1)

            def turn_probs(f, n):
                g = TURN_AT["p", f, n]
                m = f * UNITS + n
                pe.wait_ge(exp_ready, m + 1)
                if g >= TURN:
                    pe.wait_ge(turn_free, g - (TURN - 1))
                for c in range(KD):
                    last = pe.transpose(turnb(g)[:, tile(c)], pbuf[m % SLOTS][:, tile(c)], ident[:, :])
                last.then_inc(turn_ready, 1)

            def attend(f, a):
                t = f * TH + a // 2
                bank = begin("pv", f, a)
                pe.wait_ge(turn_free, TURN_AT["p", f, 2 * a + 1] + 1)
                for u in range(2):
                    for c in range(KD):
                        at = (u * KD + c) * (XD + 1)
                        n = 2 * a + u
                        head = HJ * c + n % 4
                        last = pe.matmul(bank[:, at:at + XD + 1], ptbuf[(f * UNITS + n) % SLOTS][:, tile(c)],
                                         vones[:, t, head, :], start=True, stop=True)
                last.then_inc(acc_ready, 1)

            def turn_attended(f, a):
                n = f * TH + a
                pe.wait_ge(att_ready, 2 * (n + 1))
                pe.wait_ge(acc_free, ACC_AT["pv", f, 2 * a + 1] + 1)
                turn_tile(("at", f, a), attn[n % SLOTS])

            def project_attended(f, a):
                if f == a == 0:
                    pe.wait_ge(w_lo["wo"], 1)
                split_tiles("at", f, a)
                project_n(("wo", f, a), w_hl[3], xt_hl, f * TH + a)

            def spectrum(f, c):
                if c == 0:
                    pe.wait_ge(w_lo["wqkv"], 1)
                    split_tiles("x2", f, TH - 1)
                project_t(("w", f, c), w_hl[0], xt_hl, f, c)

            def logits(f):
                bank = begin("lg", f)
                pe.wait_ge(wn2_first, KD // 2 * (f + 1))
                pe.wait_ge(wn2_last, KD // 2 * (f + 1))
                for t in range(TH):
                    for c in range(KD):
                        last = pe.matmul(bank[:, t * XH:(t + 1) * XH], wn2[f][:, c, tile(t)],
                                         head_sum[:, c, :], start=(c == 0), stop=(c == KD - 1))
                last.then_inc(acc_ready, 1)

            def turn_pi(f):
                g = TURN_AT["pi", f]
                pe.wait_ge(pi_ready, f + 1)
                pe.wait_ge(turn_free, g - (TURN - 1))
                for t in range(TH):
                    last = pe.transpose(turnb(g)[0:XH, tile(t)], pi[f][:, t, :], ident[:, :])
                last.then_inc(turn_ready, 1)

            def spread_pi(f, c):
                if c == 0:
                    pe.wait_ge(spread_ready, 1)
                    pe.wait_ge(turn_free, TURN_AT["pi", f] + 1)
                pe.matmul(begin("pb", f, c)[:, :], head_spread[0:XH, c, :], piT[f][0:XH, :],
                          start=True, stop=True).then_inc(acc_ready, 1)

            def spread_sums(f):
                bank = begin("ps", f)
                pe.wait_ge(pisum_ready, f + 1)
                for c in range(KD):
                    last = pe.matmul(bank[:, c * BH:(c + 1) * BH], head_spread[0:XH, c, :], pi_sum[:, f, :],
                                     start=True, stop=True)
                last.then_inc(acc_ready, 1)

            def mix_out(f, t):
                if t == 0:
                    pe.wait_ge(w_lo["wout"], 1)
                    pe.wait_ge(z_lo, KD * (f + 1))
                project_n(("wout", f, t), w_hl[1], xt_hl, f * TH + t)

            def router_logits(f, t):
                if t == 0:
                    pe.wait_ge(w_lo["sel"], 1)
                    split_tiles("x3", f, TH - 1)
                project_n(("gl", f, t), sel_hl, xt_hl, f * TH + t, P)

            def turn_gates(f):
                g = TURN_AT["go", f]
                pe.wait_ge(gates_o_ready, f + 1)
                pe.wait_ge(turn_free, g - (TURN - 1))
                for t in range(TH):
                    last = pe.transpose(turnb(g)[0:FH * E, tile(t)], gates[:, f * TH + t, FH * E:2 * FH * E],
                                        ident[:, :])
                last.then_inc(turn_ready, 1)

            def bank_of(kind, h, n):
                return accb(ACC_AT[kind + "0", n] if isinstance(h, int) and h == 0 else acc_bank(kind, n))

            def head_qk(h, m):
                begin_acc(acc_at("qk", h, m))
                product(bank_of("qk", h, m), lambda z, k: qk_hl[z][:, m // 2, k, :],
                        lambda z, k: xt_hl[z][:, k, columns(m % 2)]).then_inc(acc_ready, 1)

            def head_values(h, n):
                c, t = n // NT, n % NT
                begin_acc(acc_at("xv", h, n))
                product(bank_of("xv", h, n), lambda z, k: xt_hl[z][:, k, tile(t)],
                        lambda z, k: v_hl[z][:, c, k, :]).then_inc(acc_ready, 1)

            def head_scores(h, f):
                n = split_at(h, f)
                pe.wait_ge(acc_free, acc_at("qk", h, 3) + 1)
                pe.wait_ge(split_free, n - (SPLIT - 1))
                for t in range(TH):
                    q = tile(f * TH + t)
                    last = pe.matmul(splitb(f)[:, tile(t)], qkT[:, 0, q], qkT[:, 1, q], start=True, stop=True)
                last.then_inc(split_ready, 1)

            def head_turn(h, f):
                n = turn_at("p", h, f)
                pe.wait_ge(norm_ready, h * 2 + (f + 1))
                pe.wait_ge(turn_free, n - (TURN - 1))
                for t in range(TH):
                    last = pe.transpose(turnb(f)[:, tile(t)], pbuf[f][:, tile(t)], ident[:, :])
                last.then_inc(turn_ready, 1)

            def head_context(h, f):
                n = turn_at("ctx", h, f)
                pe.wait_ge(acc_free, acc_at("xv", h, NT + TH * (f + 1) - 1) + 1)
                pe.wait_ge(turn_free, n - (TURN - 1))
                for t in range(TH):
                    last = pe.matmul(turnb(f)[:, tile(t)], v_head[:, f * TH + t, :], ptbuf[f][:, tile(t)],
                                     start=True, stop=True)
                last.then_inc(turn_ready, 1)

            def output_tile(h, t, hl):
                begin_acc(acc_at("out", h, t))
                pe.wait_ge(gated_lo, h * NT + (t + 1))
                bank = accb(acc_bank("out", t))
                for e in range(E):
                    for a, b in ((0, 0), (0, 1), (1, 0)):
                        last = pe.matmul(bank[:, :], gated[a][:, t, e, :], hl[b][:, e, :],
                                         start=(e == 0 and (a, b) == (0, 0)), stop=(e == E - 1 and a == 1))
                last.then_inc(acc_ready, 1)

            def step(h):
                pe.wait_ge(vw_lo, h * 3 + 1)
                for m in range(4):
                    head_qk(h, m)
                for c in range(2):
                    pe.wait_ge(vw_lo, h * 3 + (2 + c))
                    for t in range(NT):
                        head_values(h, c * NT + t)
                        if (c, t) in ((0, 1), (0, 3)):
                            head_scores(h, t // 2)
                        if (c, t) in ((1, 1), (1, 3)):
                            head_turn(h, t // 2)
                        if (c, t) == (1, 5):
                            head_context(h, 0)
                pe.wait_ge(ow_lo, h * 2)
                for t in range(NT):
                    output_tile(h - 1, t, o_hl)
                    if t == 1:
                        head_context(h, 1)

            def experts_ready(part):
                pe.wait_ge(vw_lo, part + 1)

            do = {"k": keys, "v": values, "q": queries, "norm": turn_normed, "s": scores, "p": turn_probs,
                  "pv": attend, "at": turn_attended, "wo": project_attended, "w": spectrum, "lg": logits,
                  "pi": turn_pi, "pb": spread_pi, "ps": spread_sums, "wout": mix_out, "gl": router_logits,
                  "go": turn_gates, "ew": experts_ready, "qk0": lambda m: head_qk(0, m),
                  "xv0": lambda n: head_values(0, n), "hs": lambda f: head_scores(0, f),
                  "hp": lambda f: head_turn(0, f), "hc": lambda f: head_context(0, f)}
            for kind, *a in FRONT:
                if kind in do:
                    do[kind](*a)
            with pe.Fori(1, FH - 1) as h:
                step(h)
            step(FH - 1)
            pe.wait_ge(ow_lo, 2 * FH)
            for t in range(NT):
                output_tile(FH - 1, t, o_hl_last)


_OUT = (N, D)


def kernel(**inputs):
    import numpy as np
    import concourse.bacc as bacc
    from concourse.bass_utils import run_bass_kernel_spmd

    a = {k: np.asarray(v) for k, v in inputs.items()}
    lay = np.ascontiguousarray
    heads = FH
    q = a["L0_ffn_q_w"].reshape(heads, P, KD, P)
    k = a["L0_ffn_k_w"].reshape(heads, P, KD, P)
    qk = np.stack([q, k], 1).transpose(0, 4, 1, 3, 2).reshape(heads, P, 2 * KD * P)
    v = a["L0_ffn_v_w"].reshape(heads, 2, EC, KD, P, P).transpose(0, 4, 1, 3, 2, 5).reshape(heads, P, KD * E * P)
    o = a["L0_ffn_o_w"].reshape(heads, E, P, D).transpose(0, 2, 1, 3).reshape(heads, P, E * D)
    arrays = {
        "x": a["x"].reshape(N, D),
        "ctx_t": a["ctx_1024"][:, :T].reshape(N, D).T,
        "wk": a["L0_xattn_Wk"], "wv": a["L0_xattn_Wv"], "wq": a["L0_xattn_Wq"], "wo": a["L0_xattn_Wo"],
        "wqkv_t": a["L0_attn_Wqkv"].T, "wout_t": a["L0_attn_Wout"].T,
        "sel_v_t": a["L0_ffn_sel_v_w"].T, "sel_o_t": a["L0_ffn_sel_o_w"].T,
        "qk_t": qk, "v_w": v, "o_w": o,
        "bq": a["L0_xattn_bq"].reshape(KD, P).T, "bk": a["L0_xattn_bk"].reshape(KD, P).T,
        "bv": a["L0_xattn_bv"], "bo": a["L0_xattn_bo"], "bout": a["L0_attn_bout"],
        "temp": a["L0_attn_temp"].reshape(XH), "route_scale": a["L0_ffn_route_scale"],
    }
    arrays = {n: lay(v) for n, v in arrays.items()}
    nc = bacc.Bacc("TRN2", target_bir_lowering=False, num_devices=1)
    args = [nc.dram_tensor(n, v.shape, mybir.dt.from_np(v.dtype), kind="ExternalInput").ap()
            for n, v in arrays.items()]
    names = list(arrays)
    byname = dict(zip(names, args))
    out = nc.dram_tensor("out", _OUT, F32, kind="ExternalOutput").ap()
    gate_dram = nc.dram_tensor("gate_dram", (FH * E, N), F32, kind="Internal").ap()
    perceiver_kernel(nc, out=out, gate_dram=gate_dram, **byname)
    r = run_bass_kernel_spmd(nc, [arrays], core_ids=[0])
    return r.results[0]["out"].reshape(B, T, D)
```

```python
from contextlib import ExitStack

import concourse.bass as bass
from concourse import mybir

F32 = mybir.dt.float32
F16 = mybir.dt.float16
ALU = mybir.AluOpType
ACT = mybir.ActivationFunctionType
AX = mybir.AxisListType

P = 128
B, T, D = 32, 32, 512
N = B * T
KD = D // P
NT = N // P
HALF = N // 2
TH = NT // 2
BH = B // 2
XH, XD = 16, 32
HJ = XH // KD
FH, E = 8, 8
EC = E // 2
WSCALE = 64.0
ASCALE = 16.0
MASKED = -1.0e30
LN_EPS = 1e-5

SLOTS = 4
UNITS = 4 * TH

ACC, SPLIT, TURN = 4, 2, 2
ACC_BODY = 4 + 2 * NT + NT




def norm_steps(ln, f):
    out = [("var", ln, f), ("rstd", ln, f)]
    return out + [("norm", ln, f, t) for t in range(TH)]


def attention_ticks():
    ticks = []
    for n in range(2 * UNITS + 9):
        tick = []

        def at(lag):
            return (n - lag) // UNITS, (n - lag) % UNITS

        def within(lag):
            return lag <= n < 2 * UNITS + lag

        if within(0):
            tick.append(("s", *at(0)))
        if within(1):
            tick.append(("e", *at(1)))
        if within(4) and n % 2 == 1:
            tick.append(("pv", at(4)[0], at(4)[1] // 2))
        if within(2):
            tick.append(("p", *at(2)))
        if within(6) and (n - 6) % 4 == 3:
            tick.append(("at", at(6)[0], at(6)[1] // 4))
        if within(8) and (n - 8) % 4 == 3:
            tick.append(("wo", at(8)[0], at(8)[1] // 4))
        ticks.append(tick)
    return ticks


def mix_steps(f):
    out = norm_steps(1, f)
    for c in range(KD):
        out.append(("w", f, c))
        if c >= 1:
            out.append(("nsum", f, c - 1))
    out += [("nsum", f, KD - 1), ("inv", f)]
    out += [("bias", 1, f, t) for t in range(TH)]
    out += [("lg", f), ("pi", f), ("pb", f, 0), ("pb", f, 1), ("ps", f), ("pb", f, 2), ("pb", f, 3), ("coef", f)]
    out += [("z", f, c) for c in range(KD)] + [("zlow", f, c) for c in range(KD)]
    out += [("wout", f, t) for t in range(TH)]
    return out


def route_steps(f):
    return norm_steps(2, f) + [("gl", f, t) for t in range(TH)] + [("route", f, 0, part) for part in range(3)]


def route_out_steps(f):
    return [("route", f, 1, part) for part in range(3)] + [("go", f)]


def head0_steps():
    first = [("gate0", 0), ("qk0", 0), ("qk0", 2)] + [("xv0", c * NT + t) for c in range(2) for t in range(TH)]
    rest = [("qk0", 1), ("qk0", 3), ("hs", 0), ("gate0", 1)]
    rest += [("xv0", TH), ("hs", 1), ("xv0", TH + 1), ("xv0", TH + 2), ("he", 0), ("xv0", TH + 3), ("he", 1)]
    rest += [("xv0", NT + TH), ("hp", 0), ("xv0", NT + TH + 1), ("w1", 0), ("hp", 1), ("hc", 0)]
    rest += [("xv0", NT + TH + 2), ("w1", 1), ("xv0", NT + TH + 3), ("w1", 2), ("hc", 1)]
    return first, rest


def streams():
    first, rest = head0_steps()
    early = [("split", "wo")] + [("k", 1, c) for c in range(KD)] + [("v", 1, t) for t in range(TH)]
    early += norm_steps(0, 1)[2:] + [("bias", 0, 1, t) for t in range(TH)]
    early += [("q", 1, c) for c in range(KD)] + [("split", "wqkv"), ("split", "wout")]
    chain = [mix_steps(f) + [("split", "sel")] * (f == 0) + route_steps(f) + route_out_steps(f) for f in range(2)]
    return {"T": attention_ticks(), "E": [[x] for x in early], "A": [[("spread",)]] + [[x] for x in chain[0]],
            "B": [[x] for x in chain[1]], "F": [[("ew", part)] for part in range(3)] + [[x] for x in first + rest]}


def front_order():
    out = [("split", name, part) for part in range(2) for name in ("ctx0", "wk")]
    out += [("k", 0, 0), ("k", 0, 1), ("split", "wv"), ("k", 0, 2), ("k", 0, 3)]
    out += [("var", 0, 0), ("rstd", 0, 0), ("split", "wq"), ("v", 0, 0), ("v", 0, 1)]
    out += [("norm", 0, 0, 0), ("v", 0, 2), ("norm", 0, 0, 1), ("v", 0, 3), ("norm", 0, 0, 2), ("norm", 0, 0, 3)]
    out += [("bias", 0, 0, t) for t in range(TH)] + [("var", 0, 1), ("rstd", 0, 1), ("split", "ctx1")]
    out += [("q", 0, c) for c in range(KD)]
    parts = streams()
    for word in MERGE.split():
        for _ in range(int(word[:-1])):
            out += parts[word[-1]].pop(0)
    assert not any(parts.values())
    return place_halves(out)


def place_halves(steps):
    out, highs, lows = [], [], []

    def take_lows():
        while lows:
            out.append(("low", *lows.pop(0)[0]))

    def take_highs():
        while highs:
            key = highs.pop(0)[0]
            take_lows()
            out.append(("high", *key))
            lows.append((key, now))

    for now, step in enumerate(steps):
        if step[0] in ("q", "w", "gl", "wo", "qk0", "xv0"):
            take_highs()
            take_lows()
        if lows and now - lows[0][1] >= LOW_LAG:
            take_lows()
        if step[0] == "at":
            take_highs()
        out.append(step)
        if step[0] == "norm":
            take_highs()
            highs.append(((f"x{step[1] + 1}", *step[2:]), now))
        elif step[0] == "at":
            highs.append((step, now))
            take_highs()
        elif highs and now - highs[0][1] >= HIGH_LAG:
            take_highs()
    take_highs()
    take_lows()
    return out


HIGH_LAG = 1
LOW_LAG = 3
MERGE = ("2E 1T 1E 1T 1E 1T 2E 1T 2E 2T 6E 6T 2E 2T 7E 11T 1A 2T 2A 1T 4A 3T 1A 2T 5A 2T 5A 2T 3A 1T "
         "2A 1T 1A 1T 1B 1A 1B 2A 4B 9A 1B 2A 1B 1A 1B 1A 2F 5A 6B 2A 5B 5A 1F 1A 1B 1A 6B 2F 1B 2F 6B "
         "1F 1B 1A 1F 1B 1A 4B 1F 1B 1A 2F 2B 1F 2B 1F 5B 2F 3B 1F 2B 1F 1A 8F 1T 1B 10F")
FRONT = front_order()
_ACC = [x for x in FRONT if x[0] in ("k", "v", "q", "s", "pv", "wo", "w", "lg", "ps", "pb", "wout", "gl",
                                     "qk0", "xv0")]
_SPLIT = [(f"x{x[1] + 1}", *x[2:]) if x[0] == "norm" else x for x in FRONT if x[0] in ("norm", "at")]
_TURN = [x for x in FRONT if x[0] in ("p", "pi", "go")]
ACC_AT = {k: n for n, k in enumerate(_ACC)}
SPLIT_AT = {k: n for n, k in enumerate(_SPLIT)}
TURN_AT = {k: n for n, k in enumerate(_TURN)}
NORM_AT = {x[1:]: n for n, x in enumerate(y for y in FRONT if y[0] == "norm")}
RSTD_AT = {x[1:]: n for n, x in enumerate(y for y in FRONT if y[0] == "rstd")}
VAR_AT = {x[1:]: n for n, x in enumerate(y for y in FRONT if y[0] == "var")}
assert len(_SPLIT) % SPLIT == 0 and len(_TURN) % TURN == 0 and ACC_BODY % ACC == 0


def is_head(h, n):
    return isinstance(h, int) and h == n


def acc_at(kind, h, n):
    off = {"qk": 0, "xv": 4, "out": 4 + 2 * NT}[kind] + n
    if kind == "out":
        h = h + 1
        if is_head(h, FH):
            return len(_ACC) + (FH - 1) * ACC_BODY + n
    elif is_head(h, 0):
        return ACC_AT[kind + "0", n]
    return h * ACC_BODY + (len(_ACC) - ACC_BODY + off)


def acc_bank(kind, n):
    off = {"qk": 0, "xv": 4, "out": 4 + 2 * NT}[kind] + n
    return (len(_ACC) + off) % ACC


def split_at(h, f):
    return h * 2 + (len(_SPLIT) + f)


def turn_at(kind, h, f):
    return h * 4 + (len(_TURN) + {"p": 0, "ctx": 2}[kind] + f)


def perceiver_kernel(nc, x, ctx_t, wk, wv, wq, wo, wqkv_t, wout_t, sel_v_t, sel_o_t,
                     qk_t, v_w, o_w, bq, bk, bv, bo, bout, temp, route_scale, out, gate_dram):
    ctx = ExitStack()
    with ctx:
        def sb(name, shape, dt=F32):
            return ctx.enter_context(nc.sbuf_tensor(name, shape, dt))

        def sem(name):
            return ctx.enter_context(nc.semaphore(name))

        KB = 256
        r_stage = sb("r_stage", [P, 16 * KB])
        r_split = sb("r_split", [P, 16 * KB])
        r_qk = sb("r_qk", [P, 32 * KB])
        r_mid = sb("r_mid", [P, 32 * KB])
        r_w = sb("r_w", [P, 32 * KB])
        r_v = sb("r_v", [P, NT * XH * (XD + 1)])
        r_s = sb("r_s", [P, 4 * KB])
        r_p = sb("r_p", [P, 4 * KB])
        r_pt = sb("r_pt", [P, 4 * KB])
        r_att = sb("r_att", [P, 4 * KB])

        xres = sb("xres", [P, NT, D])
        xt_split = sb("xt_split", [P, 16 * KB])
        xn = sb("xn", [P, 2, D])
        bo_row = sb("bo_row", [P, D])
        ident = sb("ident", [P, P])
        mask_causal = sb("mask_causal", [P, P])
        mask_batch = sb("mask_batch", [P, P])
        head_sum = sb("head_sum", [P, KD, XH])
        bias_cols = sb("bias_cols", [P, 2, KD])
        temp_row = sb("temp_row", [P, XH])
        rs_col = sb("rs_col", [P, 1])
        ramp = sb("ramp", [P, E])
        stats = sb("stats", [P, 2, TH, 6])
        mv = sb("mv", [P, 2, TH, 2])
        var = sb("var", [P, 2, TH])
        rstd = sb("rstd", [P, 2, TH])
        nw = sb("nw", [P, 2, TH])
        shift = sb("shift", [P, 2, TH])
        lsum = sb("lsum", [P, 2, 2, TH])
        pi_sum = sb("pi_sum", [XH, 2, BH])
        bv_row = sb("bv_row", [P, D])
        smax = sb("smax", [P, SLOTS, 4])
        ssum = sb("ssum", [P, 2, 4])
        rinv = sb("rinv", [P, 2, 8])
        gsm = sb("gsm", [P, 5, TH * 2 * FH])
        bsm = sb("bsm", [P, 2, 4, KD, BH])
        gate_h = sb("gate_h", [P, NT, E])

        def half_view(region, off, shape, names, **kw):
            size = 1
            for s in shape:
                size *= s
            return region[:, off * KB:].bitcast(F16)[:, 0:size].rearrange(names, **kw)

        def words(region, off, size):
            return region[:, off:off + size]

        ctx_stage = r_stage[:, :].rearrange("p (k n) -> p k n", k=KD)
        ctx_hl = [half_view(r_split, 8 * s, (KD, N), "p (k n) -> p k n", k=KD) for s in range(2)]
        wstage4 = [words(r_mid, 8 * KB * s, 8 * KB).rearrange("p (k n) -> p k n", k=KD) for s in range(4)]
        sel_stage = words(r_pt, 0, KD * P).rearrange("p (k n) -> p k n", k=KD)
        w_hl = [[half_view(r_w, 8 * s + 4 * z, (KD, D), "p (k n) -> p k n", k=KD) for z in range(2)]
                for s in range(4)]
        sel_hl = [half_view(r_w, 16 + 4 * z, (KD, P), "p (k n) -> p k n", k=KD) for z in range(2)]
        xt_hl = [half_view(xt_split, 8 * s, (KD, N), "p (k n) -> p k n", k=KD) for s in range(2)]
        qT, kT, wn2 = [], [], []
        for f in range(2):
            qT.append(words(r_qk, 16 * KB * f, 8 * KB).rearrange("p (c n) -> p c n", c=KD))
            kT.append(words(r_qk, (16 * f + 8) * KB, 8 * KB).rearrange("p (c n) -> p c n", c=KD))
            wn2.append(qT[f])
        vones = r_v[:, :].rearrange("p (t h d) -> p t h d", t=NT, h=XH)

        def slots(region, n):
            return ([words(region, 2 * KB * s, D) for s in range(2)]
                    + [words(r_stage, (4 * n + 2 * s) * KB, D) for s in range(2)])

        sbuf, pbuf, ptbuf, attn = slots(r_s, 0), slots(r_p, 1), slots(r_pt, 2), slots(r_att, 3)
        wT = [words(r_mid, 16 * KB * f, 8 * KB).rearrange("p (c n) -> p c n", c=KD) for f in range(2)]
        sqT = [words(r_mid, (16 * f + 8) * KB, 8 * KB).rearrange("p (c n) -> p c n", c=KD) for f in range(2)]
        head_spread = words(r_qk, 8 * KB, KD * P).rearrange("p (c j) -> p c j", c=KD)
        piT = [words(r_qk, (10 + 2 * f) * KB, D) for f in range(2)]
        pi = [words(r_qk, 14 * KB + 64 * f, TH * XH).rearrange("p (t h) -> p t h", t=TH) for f in range(2)]
        route_buf = [words(r_qk, (24 + 2 * i) * KB, D) for i in range(4)]
        gates = words(r_att, 0, NT * 2 * FH * E).rearrange("p (t g) -> p t g", t=NT)
        goT = r_pt[0:FH * E, :]
        stage_v = r_stage[:, :].rearrange("p (c n) -> p c n", c=2)
        v_hl = [half_view(r_split, 8 * z, (2, KD, EC * P), "p (c k n) -> p c k n", c=2, k=KD) for z in range(2)]
        o_hl = [half_view(r_w, 8 * z, (E, D), "p (e n) -> p e n", e=E) for z in range(2)]
        o_hl_last = [half_view(r_split, 8 * z, (E, D), "p (e n) -> p e n", e=E) for z in range(2)]
        prod = [words(r_w, (16 + 4 * s) * KB, E * P).rearrange("p (e n) -> p e n", e=E) for s in range(2)]
        ctxT = words(r_w, 24 * KB, N)
        v_head = words(r_w, 28 * KB, NT * P).rearrange("p (t d) -> p t d", t=NT)
        stage_qk = words(r_v, 0, 4 * KB)
        qk_hl = [half_view(r_v, 4 + 2 * z, (2, KD, P), "p (m k n) -> p m k n", m=2, k=KD) for z in range(2)]
        qkT = words(r_v, 8 * KB, 8 * KB).rearrange("p (m n) -> p m n", m=2)
        gate_b = r_qk[:, :].rearrange("p (e n) -> p e n", e=E)
        gated = [half_view(r_mid, 16 * z, (NT, E, P), "p (t e n) -> p t e n", t=NT, e=E) for z in range(2)]

        psum = [ctx.enter_context(nc.psum_tensor(f"bank{i}", [P, 512], F32)) for i in range(8)]

        def accb(n):
            return psum[n % ACC]

        def splitb(n):
            return psum[ACC + n % SPLIT]

        def turnb(n):
            return psum[ACC + SPLIT + n % TURN]

        SPLITS = ["ctx0", "wk", "wv", "ctx1", "wq", "wo", "wqkv", "wout", "sel"]
        POOL_SPLITS = ["wo", "wqkv", "wout", "sel"]

        ld_ctx = [sem(f"ld_ctx{f}") for f in range(2)]
        ld_rest = {"ctx0": sem("ld_ctx0_rest"), "wk": sem("ld_wk_rest")}
        ld_w = [sem(f"ld_w{i}") for i in range(7)]
        ld_x = [sem(f"ld_x{f}") for f in range(2)]
        ld_bias, ld_bv, ld_bo, ld_bout = sem("ld_bias"), sem("ld_bv"), sem("ld_bo"), sem("ld_bout")
        ld_exp, ld_qk, ld_gate = sem("ld_exp"), sem("ld_qk"), sem("ld_gate")
        gate_stored, out_stored = sem("gate_stored"), sem("out_stored")
        consts_ready, ones_ready, spread_ready = sem("consts_ready"), sem("ones_ready"), sem("spread_ready")
        acc_ready, acc_free = sem("acc_ready"), sem("acc_free")
        split_ready, split_hi, split_free = sem("split_ready"), sem("split_hi"), sem("split_free")
        turn_ready, turn_free = sem("turn_ready"), sem("turn_free")
        w_hi = {n: sem(f"hi_{n}") for n in SPLITS}
        w_lo = {n: sem(f"lo_{n}") for n in SPLITS}
        w_scaled = sem("w_scaled")
        var_ready, std_ready, xn_ready = sem("var_ready"), sem("std_ready"), sem("xn_ready")
        rstd_ready = sem("rstd_ready")
        bias_added = [sem("bo_added"), sem("bout_added")]
        max_ready, sub_ready = sem("max_ready"), sem("sub_ready")
        exp_ready, att_ready = sem("exp_ready"), sem("att_ready")
        rsum_ready, norm_ready = sem("rsum_ready"), sem("norm_ready")
        sq_ready, inv_ready = sem("sq_ready"), sem("inv_ready")
        wn2_first, wn2_last = sem("wn2_first"), sem("wn2_last")
        lexp_ready, pi_ready, pisum_ready, coef_ready = (sem("lexp_ready"), sem("pi_ready"), sem("pisum_ready"),
                                                         sem("coef_ready"))
        z_ready, z_hi, z_lo = sem("z_ready"), sem("z_hi"), sem("z_lo")
        rl_ready, prob_ready = sem("rl_ready"), sem("prob_ready")
        gates_v_ready, gates_o_ready = sem("gates_v_ready"), sem("gates_o_ready")
        vw_hi, vw_lo, ow_hi, ow_lo = sem("vw_hi"), sem("vw_lo"), sem("ow_hi"), sem("ow_lo")
        prod_ready, gated_hi, gated_lo = sem("prod_ready"), sem("gated_hi"), sem("gated_lo")
        dve_step, pool_step = sem("dve_step"), sem("pool_step")

        PARTS = {"ctx0": 2, "wk": 2}

        def part_of(name, n):
            rows = KD // PARTS.get(name, 1)
            return slice(n * rows, (n + 1) * rows)

        def split_operands(name):
            if name == "ctx0" or name == "ctx1":
                f = int(name[3])
                n = slice(f * HALF, (f + 1) * HALF)
                return ctx_stage[:, :, n], [c[:, :, n] for c in ctx_hl], 1.0, ld_ctx[f], 16
            i = ["wk", "wv", "wq", "wo", "wqkv", "wout", "sel"].index(name)
            if name == "sel":
                return sel_stage, sel_hl, WSCALE, ld_w[6], 32
            src = wstage4[i if i < 4 else i - 2]
            return src, w_hl[i if i < 4 else i - 4], WSCALE, ld_w[i], 16

        block = ctx.enter_context(nc.Block())

        @block.sync
        def _(sp):
            ctx_v = ctx_t.rearrange("(k p) n -> p k n", p=P)

            def weight(w):
                return w.rearrange("(k p) n -> p k n", p=P)

            for n, load in enumerate((ld_ctx[0], ld_rest["ctx0"])):
                k = part_of("ctx0", n)
                sp.dma_start(ctx_stage[:, k, 0:HALF], ctx_v[:, k, 0:HALF]).then_inc(load, 16)
            x_v = x.rearrange("(t p) d -> p t d", p=P)
            sp.dma_start(wstage4[1], weight(wv)).then_inc(ld_w[1], 16)
            sp.dma_start(bias_cols[:, 0, :], bq).then_inc(ld_bias, 16)
            sp.dma_start(bias_cols[:, 1, :], bk).then_inc(ld_bias, 16)
            sp.dma_start(temp_row[:, :], temp.partition_broadcast(P)).then_inc(ld_bias, 16)
            sp.dma_start(rs_col[:, :], route_scale.partition_broadcast(P)).then_inc(ld_bias, 16)
            sp.dma_start(xres[:, 0:TH, :], x_v[:, 0:TH, :]).then_inc(ld_x[0], 16)
            sp.dma_start(wstage4[2], weight(wq)).then_inc(ld_w[2], 16)
            sp.dma_start(bv_row[:, :], bv.partition_broadcast(P)).then_inc(ld_bv, 16)
            sp.dma_start(bo_row[:, :], bo.partition_broadcast(P)).then_inc(ld_bo, 16)
            sp.dma_start(xres[:, TH:NT, :], x_v[:, TH:NT, :]).then_inc(ld_x[1], 16)
            sp.dma_start(ctx_stage[:, :, HALF:N], ctx_v[:, :, HALF:N]).then_inc(ld_ctx[1], 16)
            sp.dma_start(wstage4[3], weight(wo)).then_inc(ld_w[3], 16)
            sp.wait_ge(w_lo["wq"], 1)
            sp.dma_start(wstage4[2], weight(wqkv_t)).then_inc(ld_w[4], 16)
            sp.wait_ge(w_lo["wo"], 1)
            sp.dma_start(wstage4[3], weight(wout_t)).then_inc(ld_w[5], 16)
            sp.wait_ge(bias_added[0], NT)
            sp.dma_start(bo_row[:, :], bout.partition_broadcast(P)).then_inc(ld_bout, 16)
            sp.wait_ge(split_ready, SPLIT_AT["at", 1, TH - 1] + 1)
            sp.dma_start(sel_stage[:, :, 0:FH * E], weight(sel_v_t)).then_inc(ld_w[6], 16)
            sp.dma_start(sel_stage[:, :, FH * E:P], weight(sel_o_t)).then_inc(ld_w[6], 16)
            sp.dma_start(stage_qk, qk_t[0]).then_inc(ld_qk, 16)
            sp.dma_start(r_stage[:, :], v_w[0]).then_inc(ld_exp, 16)
            sp.wait_ge(vw_lo, 3)
            sp.dma_start(r_stage[:, :], v_w[1]).then_inc(ld_exp, 16)
            sp.dma_start(stage_qk, qk_t[1]).then_inc(ld_qk, 16)
            sp.wait_ge(turn_free, TURN_AT["go", 1] + 1)
            sp.dma_start(gate_dram, goT).then_inc(gate_stored, 16)
            sp.wait_ge(gate_stored, 16)
            sp.dma_start(gate_b, gate_dram[0:E, :].partition_broadcast(P)).then_inc(ld_gate, 16)

            def step(h, last=False):
                sp.wait_ge(vw_lo, h * 3 + 3)
                sp.dma_start(r_stage[:, :], o_w[bass.ds(h - 1, 1)][0]).then_inc(ld_exp, 16)
                sp.wait_ge(prod_ready, h * NT)
                sp.dma_start(gate_b, gate_dram[bass.ds(h * E, E), :].partition_broadcast(P)).then_inc(ld_gate, 16)
                sp.wait_ge(ow_lo, h * 2)
                if not last:
                    sp.dma_start(r_stage[:, :], v_w[bass.ds(h + 1, 1)][0]).then_inc(ld_exp, 16)
                    sp.dma_start(stage_qk, qk_t[bass.ds(h + 1, 1)][0]).then_inc(ld_qk, 16)
                else:
                    sp.dma_start(r_stage[:, :], o_w[h]).then_inc(ld_exp, 16)

            with sp.Fori(1, FH - 1) as h:
                step(h)
            step(FH - 1, last=True)
            out_v = out.rearrange("(t p) d -> t p d", p=P)
            for t in range(NT):
                sp.wait_ge(acc_free, acc_at("out", FH - 1, t) + 1)
                sp.dma_start(out_v[t], xres[:, t, :]).then_inc(out_stored, 16)
            sp.wait_ge(out_stored, 16 * NT)

        @block.gpsimd
        def _(pool):
            steps = [0]

            def link(ins):
                steps[0] += 1
                ins.then_inc(pool_step, 1)
                pool.wait_ge(pool_step, steps[0])

            def select(view, pattern, base, mult, op, fill):
                return pool.affine_select(out=view, in_=view, pattern=pattern, compare_op=op, fill=fill,
                                          base=base, channel_multiplier=mult)

            link(pool.memset(ident[:, :], 0.0))
            link(pool.memset(mask_causal[:, :], 0.0))
            link(pool.memset(mask_batch[:, :], 0.0))
            link(select(ident[:, :], [[-1, P]], 0, 1, ALU.not_equal, 1.0))
            pool.memset(vones[:, :, :, XD:XD + 1], 1.0).then_inc(ones_ready, 1)
            mc = mask_causal[:, :].rearrange("p (b j) -> p b j", b=P // T)
            mb = mask_batch[:, :].rearrange("p (b j) -> p b j", b=P // T)
            link(select(mc, [[-T, P // T], [-1, T]], 0, 1, ALU.is_ge, MASKED))
            link(select(mc, [[T, P // T], [0, T]], T - 1, -1, ALU.is_ge, MASKED))
            link(select(mb, [[-T, P // T], [0, T]], 0, 1, ALU.is_ge, MASKED))
            link(select(mb, [[T, P // T], [0, T]], T - 1, -1, ALU.is_ge, MASKED))
            link(pool.memset(head_sum[:, :, :], 1.0))
            link(select(head_sum[:, :, :], [[P, KD], [-XD, XH]], 0, 1, ALU.is_ge, 0.0))
            link(select(head_sum[:, :, :], [[-P, KD], [XD, XH]], XD - 1, -1, ALU.is_ge, 0.0))
            for e in range(E):
                last = pool.memset(ramp[:, e:e + 1], float(E - e))
            link(last)
            pool.wait_ge(ld_bias, 16 * 4)
            pool.tensor_tensor(head_sum[:, :, :], head_sum[:, :, :],
                               temp_row[:, :].unsqueeze(1).broadcast_to([P, KD, XH]), ALU.mult)\
                .then_inc(consts_ready, 1)

            def low(name, part=0):
                if name not in POOL_SPLITS:
                    return
                src, hl, scale, load, count = split_operands(name)
                pool.wait_ge(w_scaled, POOL_SPLITS.index(name) + 1)
                pool.tensor_tensor(hl[1], src, hl[0], ALU.subtract).then_inc(w_lo[name], 1)

            def value_weights_low(part):
                if part == 0:
                    return
                c = part - 1
                pool.wait_ge(w_scaled, len(POOL_SPLITS) + part)
                pool.wait_ge(vw_lo, part)
                pool.tensor_tensor(v_hl[1][:, c].rearrange("p k n -> p (k n)"), stage_v[:, c],
                                   v_hl[0][:, c].rearrange("p k n -> p (k n)"), ALU.subtract).then_inc(vw_lo, 1)

            def bias(block_n, f, t):
                pool.wait_ge([ld_bo, ld_bout][block_n], 16)
                pool.wait_ge(xn_ready, NORM_AT[block_n, f, t] + 1)
                pool.tensor_tensor(xres[:, f * TH + t, :], xres[:, f * TH + t, :], bo_row[:, :], ALU.add)\
                    .then_inc(bias_added[block_n], 1)

            def subtract_max(count, slot):
                pool.wait_ge(max_ready, count)
                s = sbuf[slot].rearrange("p (c k) -> p c k", c=4)
                pool.tensor_tensor(s, s, smax[:, slot, :].unsqueeze(2).broadcast_to([P, 4, P]),
                                   ALU.subtract).then_inc(sub_ready, 1)

            def heads_rows():
                pool.wait_ge(acc_ready, ACC_AT["s", 0, UNITS - 1] + 1)
                link(pool.memset(head_spread[0:XH], 1.0))
                link(select(head_spread[0:XH], [[P, KD], [1, P]], 0, -XD, ALU.is_ge, 0.0))
                select(head_spread[0:XH], [[-P, KD], [-1, P]], XD - 1, XD, ALU.is_ge, 0.0).then_inc(spread_ready, 1)

            def over_norms(f):
                pool.wait_ge(inv_ready, f + 1)
                for c in range(KD // 2, KD):
                    pool.tensor_tensor(wn2[f][:, c, :].rearrange("p (b n) -> p b n", b=BH),
                                       sqT[f][:, c, :].rearrange("p (b n) -> p b n", b=BH),
                                       bsm[:, f, 0, c, :].unsqueeze(2).broadcast_to([P, BH, T]),
                                       ALU.mult).then_inc(wn2_last, 1)

            def weigh(f, c):
                pool.wait_ge(coef_ready, f + 1)
                wb = wT[f][:, c, :].rearrange("p (b n) -> p b n", b=BH)
                pool.tensor_tensor(wb, wb, bsm[:, f, 3, c, :].unsqueeze(2).broadcast_to([P, BH, T]),
                                   ALU.mult).then_inc(z_ready, 1)

            def normalise(h, f):
                pool.wait_ge(rsum_ready, h * 2 + (f + 1))
                p = pbuf[f].rearrange("p (c k) -> p c k", c=4)
                pool.tensor_tensor(p, p, ssum[:, f, :].unsqueeze(2).broadcast_to([P, 4, P]),
                                   ALU.mult).then_inc(norm_ready, 1)

            def scores(f, n):
                m = f * UNITS + n
                subtract_max(m + 1, m % SLOTS)

            do = {"split": low, "bias": bias, "s": scores, "spread": heads_rows, "inv": over_norms,
                  "z": weigh, "ew": value_weights_low,
                  "hs": lambda f: subtract_max(2 * UNITS + f + 1, f), "he": lambda f: normalise(0, f)}
            for kind, *a in FRONT:
                if kind in do:
                    do[kind](*a)
            with pool.Fori(1, FH) as h:
                for f in range(2):
                    subtract_max(h * 2 + (2 * UNITS + f + 1), f)
                for f in range(2):
                    normalise(h, f)

        @block.scalar
        def _(act):
            for n, load in enumerate((ld_w[0], ld_rest["wk"])):
                k = part_of("wk", n)
                act.dma_start(wstage4[0][:, k], wk.rearrange("(k p) n -> p k n", p=P)[:, k]).then_inc(load, 16)

            def high(name, part=0):
                src, hl, scale, load, count = split_operands(name)
                act.wait_ge(ld_rest[name] if part else load, count)
                if name == "wqkv":
                    act.wait_ge(acc_ready, ACC_AT["k", 1, KD - 1] + 1)
                if name == "wout":
                    act.wait_ge(acc_ready, ACC_AT["v", 1, TH - 1] + 1)
                if name == "sel":
                    act.wait_ge(acc_ready, ACC_AT["q", 1, KD - 1] + 1)
                k = part_of(name, part)
                act.activation(hl[0][:, k], src[:, k], ACT.Copy, scale=scale).then_inc(w_hi[name], 1)
                if name in POOL_SPLITS:
                    act.wait_ge(w_hi[name], 1)
                    act.activation(src, src, ACT.Copy, scale=scale).then_inc(w_scaled, 1)

            def high_turned(key, f, a):
                g = SPLIT_AT[key, f, a]
                t = f * TH + a
                act.wait_ge(split_ready, g + 1)
                act.activation(xt_hl[0][:, :, t * P:(t + 1) * P],
                               splitb(g)[:, :].rearrange("p (k n) -> p k n", k=KD), ACT.Copy)\
                    .then_inc(split_hi, 1)

            def std(ln, f):
                act.wait_ge(var_ready, VAR_AT[ln, f] + 1)
                act.activation(rstd[:, f, :], var[:, f, :], ACT.Sqrt).then_inc(std_ready, 1)

            def norm(ln, f, t):
                n = NORM_AT[ln, f, t]
                act.wait_ge(rstd_ready, RSTD_AT[ln, f] + 1)
                if n >= 2:
                    o = next(k for k, v in NORM_AT.items() if v == n - 2)
                    act.wait_ge(split_ready, SPLIT_AT[f"x{o[0] + 1}", o[1], o[2]] + 1)
                act.activation(xn[:, n % 2, :], xres[:, f * TH + t, :], ACT.Identity, scale=rstd[:, f, t:t + 1],
                               bias=shift[:, f, t:t + 1]).then_inc(xn_ready, 1)

            def exp_scores(f, n):
                m = f * UNITS + n
                act.wait_ge(sub_ready, m + 1)
                if m >= SLOTS:
                    act.wait_ge(turn_ready, TURN_AT["p", (m - SLOTS) // UNITS, (m - SLOTS) % UNITS] + 1)
                act.activation(pbuf[m % SLOTS], sbuf[m % SLOTS], ACT.Exp, scale=float(XD) ** -0.5)\
                    .then_inc(exp_ready, 1)

            def take_turned(f, n):
                g = TURN_AT["p", f, n]
                m = f * UNITS + n
                act.wait_ge(turn_ready, g + 1)
                if m >= SLOTS:
                    u = (m - SLOTS) // 2
                    act.wait_ge(acc_ready, ACC_AT["pv", u // (UNITS // 2), u % (UNITS // 2)] + 1)
                act.copy(ptbuf[m % SLOTS], turnb(g)[:, :]).then_inc(turn_free, 1)

            def squares(f, c):
                act.wait_ge(acc_free, ACC_AT["w", f, c] + 1)
                if (f, c) == (1, 0):
                    act.wait_ge(w_lo["wout"], 1)
                act.activation(sqT[f][:, c, :], wT[f][:, c, :], ACT.Square).then_inc(sq_ready, 1)

            def exp_logits(f):
                act.wait_ge(acc_free, ACC_AT["lg", f] + 1)
                act.activation(pi[f], pi[f], ACT.Exp).then_inc(lexp_ready, 1)

            def take_pi(f):
                g = TURN_AT["pi", f]
                act.wait_ge(turn_ready, g + 1)
                act.copy(piT[f][0:XH], turnb(g)[0:XH, :]).then_inc(turn_free, 1)

            def high_z(f, c):
                act.wait_ge(z_ready, f * KD + c + 1)
                act.activation(xt_hl[0][:, c, f * HALF:(f + 1) * HALF], wT[f][:, c, :], ACT.Copy)\
                    .then_inc(z_hi, 1)

            def probabilities(f, m, part):
                if (m, part) != (0, 0):
                    return
                act.wait_ge(rl_ready, f + 1)
                act.activation(route_buf[1], route_buf[0], ACT.Sigmoid).then_inc(prob_ready, 1)

            def take_gates(f):
                g = TURN_AT["go", f]
                act.wait_ge(w_lo["sel"], 1)
                act.wait_ge(turn_ready, g + 1)
                act.copy(goT[:, f * HALF:(f + 1) * HALF], turnb(g)[0:FH * E, :]).then_inc(turn_free, 1)

            def weights_high(h, part):
                if part == 0:
                    act.wait_ge(ld_qk, h * 16 + 16)
                    act.activation(qk_hl[0], stage_qk.rearrange("p (m k n) -> p m k n", m=2, k=KD), ACT.Copy,
                                   scale=WSCALE).then_inc(vw_hi, 1)
                    return
                act.wait_ge(ld_exp, 16 if is_head(h, 0) else h * 32)
                c = part - 1
                act.activation(v_hl[0][:, c], stage_v[:, c].rearrange("p (k n) -> p k n", k=KD), ACT.Copy,
                               scale=WSCALE).then_inc(vw_hi, 1)
                if is_head(h, 0):
                    act.wait_ge(vw_hi, part + 1)
                    act.activation(stage_v[:, c], stage_v[:, c], ACT.Copy, scale=WSCALE).then_inc(w_scaled, 1)

            def second_weights(part):
                act.wait_ge(acc_ready, [ACC_AT["qk0", 3], ACC_AT["xv0", NT - 1], ACC_AT["xv0", 2 * NT - 1]][part] + 1)
                weights_high(1, part)

            def out_weights_high(h, hl, c):
                act.wait_ge(ld_exp, h * 32 + 48 if not is_head(h, FH - 1) else 32 * FH)
                act.activation(hl[0][:, c * EC:(c + 1) * EC],
                               stage_v[:, c].rearrange("p (e n) -> p e n", e=EC), ACT.Copy,
                               scale=WSCALE).then_inc(ow_hi, 1)

            def exp_head(h, f):
                act.wait_ge(sub_ready, h * 2 + (2 * UNITS + f + 1))
                first = is_head(h, 0)
                act.wait_ge(turn_ready, TURN_AT["p", 1, UNITS - 1] + 1 if first else turn_at("p", h - 1, f) + 1)
                act.activation(pbuf[f], sbuf[f], ACT.Exp, scale=float(P) ** -0.5).then_inc(exp_ready, 1)

            def take_head(h, f):
                if is_head(h, 0):
                    act.wait_ge(gate_stored, 16)
                act.wait_ge(turn_ready, turn_at("p", h, f) + 1)
                act.copy(ptbuf[f], turnb(f)[:, :]).then_inc(turn_free, 1)

            def take_context(h, f):
                act.wait_ge(turn_ready, turn_at("ctx", h, f) + 1)
                if not is_head(h, 0):
                    act.wait_ge(prod_ready, h * NT)
                act.copy(ctxT[:, f * HALF:(f + 1) * HALF], turnb(f)[:, :]).then_inc(turn_free, 1)

            def gated_high(h, t):
                act.wait_ge(prod_ready, h * NT + (t + 1))
                if not is_head(h, 0):
                    act.wait_ge(acc_ready, acc_at("out", h - 1, t) + 1)
                act.activation(gated[0][:, t], prod[t % 2], ACT.Copy).then_inc(gated_hi, 1)

            def gating(h, first=False, last=False):
                for t in range(NT):
                    if t % TH == 2 % TH and t < TH:
                        take_context(h, 1)
                    gated_high(h, t)
                    if first:
                        continue
                    if t == 1:
                        act.wait_ge(acc_ready, acc_at("xv", h, 2 * NT - 1) + 1)
                    if t in (1, 3, 5):
                        if not last:
                            weights_high(h + 1, t // 2)
                        elif t > 1:
                            out_weights_high(h, o_hl_last, t // 2 - 1)

            def step(h, last=False):
                act.wait_ge(acc_ready, acc_at("out", h - 2, NT - 1) + 1)
                for f in range(2):
                    exp_head(h, f)
                for c in range(2):
                    out_weights_high(h - 1, o_hl, c)
                for f in range(2):
                    take_head(h, f)
                take_context(h, 0)
                gating(h, last=last)

            do = {"split": high, "var": std, "norm": norm, "high": high_turned, "e": exp_scores,
                  "p": take_turned, "w": squares,
                  "lg": exp_logits, "pi": take_pi, "z": high_z, "route": probabilities, "go": take_gates,
                  "ew": lambda part: weights_high(0, part), "w1": second_weights,
                  "hs": lambda f: exp_head(0, f), "hp": lambda f: take_head(0, f)}
            for kind, *a in FRONT:
                if kind in do:
                    do[kind](*a)
            take_context(0, 0)
            gating(0, first=True)
            with act.Fori(1, FH - 1) as h:
                step(h)
            step(FH - 1, last=True)

        @block.vector
        def _(dve):
            steps = [0, None]

            def link(ins):
                steps[0] += 1
                ins.then_inc(dve_step, 1)
                dve.wait_ge(dve_step, steps[0] if steps[1] is None else steps[1] + steps[0])

            def low(name, part=0):
                if name in POOL_SPLITS:
                    return
                src, hl, scale, load, count = split_operands(name)
                k = part_of(name, part)
                dve.wait_ge(w_hi[name], part + 1)
                dve.scalar_tensor_tensor(out=hl[1][:, k], in0=src[:, k], scalar=scale, in1=hl[0][:, k], op0=ALU.mult,
                                         op1=ALU.subtract).then_inc(w_lo[name], 1)

            def low_turned(key, f, a):
                g = SPLIT_AT[key, f, a]
                t = f * TH + a
                dve.wait_ge(split_hi, g + 1)
                dve.tensor_tensor(xt_hl[1][:, :, t * P:(t + 1) * P],
                                  splitb(g)[:, :].rearrange("p (k n) -> p k n", k=KD),
                                  xt_hl[0][:, :, t * P:(t + 1) * P], ALU.subtract).then_inc(split_free, 1)

            def variance(ln, f):
                if ln:
                    dve.wait_ge(xn_ready, NORM_AT[ln - 1, f, TH - 1] + 1)
                    statistics(["wo", "wout"][ln - 1], f, TH - 1)
                else:
                    dve.wait_ge(ld_x[f], 16)
                    for t in range(TH):
                        dve.bn_stats(stats[:, f, t, :], xres[:, f * TH + t, :]).then_inc(dve_step, 1)
                        steps[0] += 1
                dve.wait_ge(dve_step, steps[0])
                for t in range(TH):
                    last = dve.bn_aggr(mv[:, f, t, :], stats[:, f, t, :])
                link(last)
                dve.tensor_scalar(var[:, f, :], mv[:, f, :, 1], LN_EPS, None, ALU.add).then_inc(var_ready, 1)

            def inverse_std(ln, f):
                r, n = rstd[:, f, :], nw[:, f, :]
                dve.wait_ge(std_ready, VAR_AT[ln, f] + 1)
                link(dve.reciprocal(r, r))
                link(dve.tensor_tensor(n, r, r, ALU.mult))
                link(dve.tensor_tensor(n, n, var[:, f, :], ALU.mult))
                link(dve.tensor_scalar(n, n, -0.5, 1.5, ALU.mult, ALU.add))
                link(dve.tensor_tensor(r, r, n, ALU.mult))
                dve.scalar_tensor_tensor(out=shift[:, f, :], in0=mv[:, f, :, 0], scalar=-1.0, in1=r,
                                         op0=ALU.mult, op1=ALU.mult).then_inc(rstd_ready, 1)

            def acc(*key):
                g = ACC_AT[key]
                dve.wait_ge(acc_ready, g + 1)
                return accb(g)

            def keys(f, c):
                if f == c == 0:
                    dve.wait_ge(ld_bias, 64)
                dve.tensor_scalar(kT[f][:, c, :], acc("k", f, c)[:, :], 1.0 / WSCALE,
                                  bias_cols[:, 1, c:c + 1], ALU.mult, ALU.add).then_inc(acc_free, 1)

            def values(f, t):
                if f == t == 0:
                    dve.wait_ge(ld_bv, 16)
                    dve.wait_ge(ones_ready, 1)
                dve.scalar_tensor_tensor(out=vones[:, f * TH + t, :, 0:XD],
                                         in0=acc("v", f, t)[:, :].rearrange("p (h d) -> p h d", h=XH),
                                         scalar=1.0 / WSCALE, in1=bv_row[:, :].rearrange("p (h d) -> p h d", h=XH),
                                         op0=ALU.mult, op1=ALU.add).then_inc(acc_free, 1)

            def queries(f, c):
                dve.tensor_scalar(qT[f][:, c, :], acc("q", f, c)[:, :], 1.0 / WSCALE,
                                  bias_cols[:, 0, c:c + 1], ALU.mult, ALU.add).then_inc(acc_free, 1)

            def mask_and_max(bank, mask, slot, free, freed, exps):
                if exps is not None:
                    dve.wait_ge(exp_ready, exps)
                dve.tensor_tensor(sbuf[slot].rearrange("p (c k) -> p c k", c=4),
                                  bank[:, :].rearrange("p (c k) -> p c k", c=4),
                                  mask[:, :].unsqueeze(1).broadcast_to([P, 4, P]), ALU.add).then_inc(free, 1)
                dve.wait_ge(free, freed)
                dve.tensor_reduce(smax[:, slot, :], sbuf[slot].rearrange("p (c k) -> p c k", c=4), AX.X,
                                  ALU.max).then_inc(max_ready, 1)

            def scores(f, n):
                m = f * UNITS + n
                if m == 0:
                    dve.wait_ge(consts_ready, 1)
                mask_and_max(acc("s", f, n), mask_causal, m % SLOTS, acc_free, ACC_AT["s", f, n] + 1,
                             m - SLOTS + 1 if m >= SLOTS else None)

            def attended(f, a):
                t, half = a // 2, a % 2
                b = acc("pv", f, a)
                o = b[:, 0:8 * (XD + 1)].rearrange("p (j c d) -> p j c d", j=2, c=KD)
                n = f * TH + t
                if n >= SLOTS and half == 0:
                    dve.wait_ge(split_ready, SPLIT_AT["at", (n - SLOTS) // TH, (n - SLOTS) % TH] + 1)
                r = rinv[:, a % 2, :].rearrange("p (j c) -> p j c", j=2)
                dve.wait_ge(acc_free, ACC_AT["pv", f, a])
                link(dve.reciprocal(r, o[:, :, :, XD]))
                att = attn[n % SLOTS].rearrange("p (c j d) -> p j c d", c=KD, j=HJ)
                for j in range(2):
                    ins = dve.tensor_tensor(att[:, 2 * half + j], o[:, j, :, 0:XD],
                                            r[:, j].unsqueeze(2).broadcast_to([P, KD, XD]), ALU.mult)
                    ins.then_inc(att_ready if j == 0 else acc_free, 1)

            def residual(kind, f, a):
                t = f * TH + a
                dve.wait_ge(bias_added[0 if kind == "wo" else 1], t + 1)
                scale = 1.0 / WSCALE if kind == "wo" else 1.0 / (WSCALE * ASCALE)
                dve.scalar_tensor_tensor(out=xres[:, t, :], in0=acc(kind, f, a)[:, :], scalar=scale,
                                         in1=xres[:, t, :], op0=ALU.mult, op1=ALU.add).then_inc(acc_free, 1)
                if a >= 1:
                    statistics(kind, f, a - 1)

            def statistics(kind, f, a):
                dve.wait_ge(acc_free, ACC_AT[kind, f, a] + 1)
                dve.bn_stats(stats[:, f, a, :], xres[:, f * TH + a, :]).then_inc(dve_step, 1)
                steps[0] += 1

            def spectrum(f, c):
                dve.tensor_scalar(wT[f][:, c, :], acc("w", f, c)[:, :], 1.0 / WSCALE, None, ALU.mult)\
                    .then_inc(acc_free, 1)

            def squares_sum(f, c):
                dve.wait_ge(sq_ready, f * KD + c + 1)
                link(dve.tensor_reduce(bsm[:, f, 1, c, :], sqT[f][:, c, :].rearrange("p (b n) -> p b n", b=BH),
                                       AX.X, ALU.add))

            def inverse_norms(f):
                link(dve.tensor_scalar(bsm[:, f, 1], bsm[:, f, 1], 1e-24, None, ALU.max))
                dve.reciprocal(bsm[:, f, 0], bsm[:, f, 1]).then_inc(inv_ready, 1)
                dve.wait_ge(inv_ready, f + 1)
                for c in range(KD // 2):
                    dve.tensor_tensor(wn2[f][:, c, :].rearrange("p (b n) -> p b n", b=BH),
                                      sqT[f][:, c, :].rearrange("p (b n) -> p b n", b=BH),
                                      bsm[:, f, 0, c, :].unsqueeze(2).broadcast_to([P, BH, T]),
                                      ALU.mult).then_inc(wn2_first, 1)

            def logits(f):
                lg = acc("lg", f)[:, 0:TH * XH].rearrange("p (t h) -> p t h", t=TH)
                link(dve.tensor_reduce(lsum[:, f, 0, :], lg, AX.X, ALU.max))
                dve.tensor_tensor(pi[f], lg, lsum[:, f, 0, :].unsqueeze(2).broadcast_to([P, TH, XH]),
                                  ALU.subtract).then_inc(acc_free, 1)

            def membership(f):
                dve.wait_ge(lexp_ready, f + 1)
                link(dve.tensor_reduce(lsum[:, f, 1, :], pi[f], AX.X, ALU.add))
                link(dve.reciprocal(lsum[:, f, 1, :], lsum[:, f, 1, :]))
                dve.tensor_tensor(pi[f], pi[f], lsum[:, f, 1, :].unsqueeze(2).broadcast_to([P, TH, XH]),
                                  ALU.mult).then_inc(pi_ready, 1)
                dve.wait_ge(turn_free, TURN_AT["pi", f] + 1)
                dve.tensor_reduce(pi_sum[:, f, :], piT[f][0:XH].rearrange("p (b n) -> p b n", b=BH), AX.X,
                                  ALU.add).then_inc(pisum_ready, 1)

            def weighted(f, c):
                b = acc("pb", f, c)
                steps[0] += 1
                dve.tensor_tensor(sqT[f][:, c, :], sqT[f][:, c, :], b[:, :], ALU.mult).then_inc(dve_step, 1)
                dve.tensor_tensor(wT[f][:, c, :], wT[f][:, c, :], b[:, :], ALU.mult).then_inc(acc_free, 1)
                dve.wait_ge(dve_step, steps[0])
                link(dve.tensor_reduce(bsm[:, f, 2, c, :], sqT[f][:, c, :].rearrange("p (b n) -> p b n", b=BH),
                                       AX.X, ALU.add))

            def pi_sums(f):
                b = acc("ps", f)[:, 0:KD * BH].rearrange("p (c b) -> p c b", c=KD)
                dve.tensor_scalar(bsm[:, f, 1], b, 1e-8, None, ALU.add).then_inc(acc_free, 1)
                dve.wait_ge(acc_free, ACC_AT["ps", f] + 1)
                link(dve.reciprocal(bsm[:, f, 0], bsm[:, f, 1]))

            def coefficients(f):
                link(dve.tensor_tensor(bsm[:, f, 2], bsm[:, f, 2], bsm[:, f, 0], ALU.mult))
                link(dve.tensor_scalar(bsm[:, f, 2], bsm[:, f, 2], 1.0, -1.0 / ASCALE, ALU.add, ALU.mult))
                dve.reciprocal(bsm[:, f, 3], bsm[:, f, 2]).then_inc(coef_ready, 1)

            def low_z(f, c):
                n = slice(f * HALF, (f + 1) * HALF)
                dve.wait_ge(z_hi, f * KD + c + 1)
                dve.tensor_tensor(xt_hl[1][:, c, n], wT[f][:, c, :], xt_hl[0][:, c, n], ALU.subtract)\
                    .then_inc(z_lo, 1)

            def router_logits(f, t):
                if f == 1 and t == 0:
                    dve.wait_ge(gates_v_ready, 1)
                    dve.wait_ge(gates_o_ready, 1)
                z = route_buf[0].rearrange("p (t g) -> p t g", t=TH)
                dve.tensor_scalar(z[:, t, :], acc("gl", f, t)[:, 0:P], 1.0 / WSCALE, None, ALU.mult)\
                    .then_inc(acc_free, 1)
                if t == TH - 1:
                    dve.wait_ge(acc_free, ACC_AT["gl", f, t] + 1)
                    dve.sem_inc(rl_ready, 1)

            def route(f, m, part):
                if (m, part) == (0, 0):
                    dve.wait_ge(prob_ready, f + 1)
                shape = [P, TH, FH, E]
                rest, pr, one, two = (b.rearrange("p (t m h e) -> p t m h e", t=TH, m=2, h=FH)[:, :, m]
                                      for b in route_buf)
                rampb = ramp[:, :].unsqueeze(1).unsqueeze(1).broadcast_to(shape)
                m1, m2, at, den = (gsm[:, i, m * TH * FH:(m + 1) * TH * FH].rearrange("p (t h) -> p t h", t=TH)
                                   for i in range(4))

                def wide(v):
                    return v.unsqueeze(3).broadcast_to(shape)

                def pick(hot, values, top):
                    link(dve.tensor_reduce(top, values, AX.X, ALU.max))
                    link(dve.tensor_tensor(hot, values, wide(top), ALU.is_equal))
                    link(dve.tensor_tensor(hot, hot, rampb, ALU.mult))
                    link(dve.tensor_reduce(at, hot, AX.X, ALU.max))
                    link(dve.tensor_tensor(hot, hot, wide(at), ALU.is_equal))

                if part == 0:
                    pick(one, pr, m1)
                    link(dve.scalar_tensor_tensor(out=rest, in0=one, scalar=-4.0, in1=pr, op0=ALU.mult,
                                                  op1=ALU.add))
                elif part == 1:
                    pick(two, rest, m2)
                    link(dve.tensor_tensor(den, m1, m2, ALU.add))
                    link(dve.tensor_scalar(den, den, 1e-9, None, ALU.max))
                    link(dve.reciprocal(at, den))
                    link(dve.tensor_scalar(at, at, rs_col[:, 0:1], None, ALU.mult))
                else:
                    link(dve.tensor_tensor(m1, m1, at, ALU.mult))
                    link(dve.tensor_tensor(m2, m2, at, ALU.mult))
                    link(dve.tensor_tensor(one, one, wide(m1), ALU.mult))
                    link(dve.tensor_tensor(two, two, wide(m2), ALU.mult))
                    out = gates[:, f * TH:(f + 1) * TH, m * FH * E:(m + 1) * FH * E]
                    dve.tensor_tensor(out.rearrange("p t (h e) -> p t h e", e=E), one, two, ALU.add)\
                        .then_inc([gates_v_ready, gates_o_ready][m], 1)

            def first_gates(f):
                dve.wait_ge(gates_v_ready, f + 1)
                n = slice(f * TH, (f + 1) * TH)
                link(dve.tensor_scalar(gate_h[:, n, :], gates[:, n, 0:E], 1.0 / WSCALE, None, ALU.mult))

            def weights_low(h, part):
                dve.wait_ge(vw_hi, h * 3 + (part + 1))
                if part == 0:
                    dve.scalar_tensor_tensor(out=qk_hl[1].rearrange("p m k n -> p (m k n)"), in0=stage_qk,
                                             scalar=WSCALE, in1=qk_hl[0].rearrange("p m k n -> p (m k n)"),
                                             op0=ALU.mult, op1=ALU.subtract).then_inc(vw_lo, 1)
                    return
                c = part - 1
                dve.scalar_tensor_tensor(out=v_hl[1][:, c].rearrange("p k n -> p (k n)"), in0=stage_v[:, c],
                                         scalar=WSCALE, in1=v_hl[0][:, c].rearrange("p k n -> p (k n)"),
                                         op0=ALU.mult, op1=ALU.subtract).then_inc(vw_lo, 1)

            def out_weights_low(h, hl, c):
                dve.wait_ge(ow_hi, h * 2 + (c + 1))
                dve.scalar_tensor_tensor(out=hl[1][:, c * EC:(c + 1) * EC].rearrange("p e n -> p (e n)"),
                                         in0=stage_v[:, c], scalar=WSCALE,
                                         in1=hl[0][:, c * EC:(c + 1) * EC].rearrange("p e n -> p (e n)"),
                                         op0=ALU.mult, op1=ALU.subtract).then_inc(ow_lo, 1)

            def take_out(h, t):
                dve.wait_ge(acc_ready, acc_at("out", h, t) + 1)
                dve.scalar_tensor_tensor(out=xres[:, t, :], in0=accb(acc_bank("out", t))[:, :],
                                         scalar=1.0 / (WSCALE * ASCALE), in1=xres[:, t, :],
                                         op0=ALU.mult, op1=ALU.add).then_inc(acc_free, 1)

            def bank_of(kind, h, n):
                return accb(ACC_AT[kind + "0", n] if is_head(h, 0) else acc_bank(kind, n))

            def take_qk(h, m):
                dve.wait_ge(acc_ready, acc_at("qk", h, m) + 1)
                dve.tensor_scalar(qkT[:, m // 2, (m % 2) * HALF:(m % 2 + 1) * HALF],
                                  bank_of("qk", h, m)[:, :], 1.0 / WSCALE, None, ALU.mult).then_inc(acc_free, 1)

            def take_values(h, n):
                c, t = n // NT, n % NT
                dve.wait_ge(acc_ready, acc_at("xv", h, n) + 1)
                b = bank_of("xv", h, n)
                v = v_head[:, t, :]
                for e in range(EC):
                    scale = gate_h[:, t, c * EC + e:c * EC + e + 1]
                    part = b[:, e * P:(e + 1) * P]
                    if c == 0 and e == 0:
                        ins = dve.tensor_scalar(v, part, scale, None, ALU.mult)
                    else:
                        ins = dve.scalar_tensor_tensor(out=v, in0=part, scalar=scale, in1=v,
                                                       op0=ALU.mult, op1=ALU.add)
                    if e < EC - 1:
                        link(ins)
                ins.then_inc(acc_free, 1)

            def head_scores(h, f):
                dve.wait_ge(split_ready, split_at(h, f) + 1)
                mask_and_max(splitb(f), mask_batch, f, split_free, split_at(h, f) + 1,
                             h * 2 + (2 * UNITS + f - 1))

            def softmax_sums(h, f):
                dve.wait_ge(exp_ready, h * 2 + (2 * UNITS + f + 1))
                link(dve.tensor_reduce(ssum[:, f, :], pbuf[f].rearrange("p (c k) -> p c k", c=4), AX.X, ALU.add))
                dve.reciprocal(ssum[:, f, :], ssum[:, f, :]).then_inc(rsum_ready, 1)

            def gate_context(h, t, first):
                if not (first and t < 2):
                    dve.wait_ge(gated_lo, h * NT + (t - 1))
                c = ctxT[:, t * P:(t + 1) * P].unsqueeze(1).broadcast_to([P, E, P])
                dve.scalar_tensor_tensor(out=prod[t % 2], in0=c, scalar=ASCALE,
                                         in1=gate_b[:, :, t * P:(t + 1) * P], op0=ALU.mult,
                                         op1=ALU.mult).then_inc(prod_ready, 1)

            def gated_low(h, t):
                dve.wait_ge(gated_hi, h * NT + (t + 1))
                dve.tensor_tensor(gated[1][:, t], prod[t % 2], gated[0][:, t], ALU.subtract).then_inc(gated_lo, 1)

            def gate_tile(h, t):
                if t == 0:
                    dve.wait_ge(ld_gate, h * 16 + 16)
                if t % TH == 0:
                    dve.wait_ge(turn_free, turn_at("ctx", h, t // TH) + 1)
                gate_context(h, t, is_head(h, 0))
                if t >= 1:
                    gated_low(h, t - 1)
                if t == NT - 1:
                    gated_low(h, t)

            def gating(h, last=False):
                for t in range(NT):
                    take_out(h - 1, t)
                    gate_tile(h, t)
                    if t in (1, 3, 5):
                        if not last:
                            weights_low(h + 1, t // 2)
                        elif t > 1:
                            out_weights_low(h, o_hl_last, t // 2 - 1)

            def step(h, first=False, last=False):
                dve.wait_ge(acc_free, acc_at("xv", h - 1, 2 * NT - 1) + 1)
                g = gates[:, :, h * E:(h + 1) * E] if isinstance(h, int) else gates[:, :, bass.ds(h * E, E)]
                link(dve.tensor_scalar(gate_h[:, :, :], g, 1.0 / WSCALE, None, ALU.mult))
                for m in range(4):
                    take_qk(h, m)
                    if first:
                        gate_tile(0, m)
                for c in range(2):
                    for t in range(NT):
                        if c == 0 and t % TH == 0:
                            dve.wait_ge(turn_ready, turn_at("ctx", h - 1, t // TH) + 1)
                        take_values(h, c * NT + t)
                        if first and c == 0 and t < NT - 4:
                            gate_tile(0, 4 + t)
                        if c == 0 and t in (2, 4):
                            head_scores(h, t // 2 - 1)
                        if (c, t) in (((1, 3), (1, 5)) if first else ((0, 5), (0, 7))):
                            out_weights_low(h - 1, o_hl, (t - 3) // 2 if first else (t - 5) // 2)
                        if (c, t) in ((0, 6), (1, 0)):
                            softmax_sums(h, c)
                gating(h, last=last)

            do = {"split": low, "var": variance, "rstd": inverse_std, "low": low_turned, "k": keys, "v": values,
                  "q": queries, "s": scores, "pv": attended, "wo": lambda f, t: residual("wo", f, t),
                  "w": spectrum, "nsum": squares_sum, "inv": inverse_norms, "lg": logits, "pi": membership,
                  "pb": weighted, "ps": pi_sums, "coef": coefficients, "zlow": low_z,
                  "wout": lambda f, t: residual("wout", f, t), "gl": router_logits, "route": route,
                  "ew": lambda part: weights_low(0, part) if part == 0 else None,
                  "w1": lambda part: weights_low(1, part), "gate0": first_gates,
                  "qk0": lambda m: take_qk(0, m), "xv0": lambda n: take_values(0, n),
                  "hs": lambda f: head_scores(0, f), "he": lambda f: softmax_sums(0, f)}
            for kind, *a in FRONT:
                if kind in do:
                    do[kind](*a)
            step(1, first=True)
            LINKS = 1 + 2 * NT * (EC - 1) + 2
            with dve.Fori(2, FH - 1) as h:
                before, steps[0], steps[1] = steps[0], 0, h * LINKS + (steps[0] - 2 * LINKS)
                step(h)
                assert steps[0] == LINKS
            steps[0], steps[1] = before + (FH - 3) * LINKS, None
            step(FH - 1, last=True)
            for t in range(NT):
                take_out(FH - 1, t)

        @block.tensor
        def _(pe):
            def begin_acc(n):
                if not isinstance(n, int) or n >= ACC:
                    pe.wait_ge(acc_free, n - (ACC - 1))

            def product(bank, stat, mov, width=D, parts=None):
                for k in range(KD):
                    if parts and k % (KD // 2) == 0:
                        pe.wait_ge(w_lo[parts[0]], k // (KD // 2) + 1)
                        pe.wait_ge(w_lo[parts[1]], k // (KD // 2) + 1)
                    for a, b in ((0, 0), (0, 1), (1, 0)):
                        last = pe.matmul(bank[:, 0:width], stat(a, k), mov(b, k),
                                         start=(k == 0 and (a, b) == (0, 0)), stop=(k == KD - 1 and a == 1))
                return last

            def columns(f):
                return slice(f * HALF, (f + 1) * HALF)

            def tile(t):
                return slice(t * P, (t + 1) * P)

            def begin(*key):
                g = ACC_AT[key]
                begin_acc(g)
                return accb(g)

            def project_t(key, w, src, f, c, parts=None):
                product(begin(*key), lambda z, k: w[z][:, k, tile(c)], lambda z, k: src[z][:, k, columns(f)],
                        parts=parts).then_inc(acc_ready, 1)

            def project_n(key, w, src, t, width=D):
                product(begin(*key), lambda z, k: src[z][:, k, tile(t)], lambda z, k: w[z][:, k, 0:width], width)\
                    .then_inc(acc_ready, 1)

            def split_tiles(key, f, t):
                pe.wait_ge(split_free, SPLIT_AT[key, f, t] + 1)

            def keys(f, c):
                if (f, c) == (1, 0):
                    pe.wait_ge(w_lo["ctx1"], 1)
                project_t(("k", f, c), w_hl[0], ctx_hl, f, c, ("ctx0", "wk") if f == c == 0 else None)

            def values(f, t):
                if t == 0:
                    pe.wait_ge(w_lo["wv"], 1)
                project_n(("v", f, t), w_hl[1], ctx_hl, f * TH + t)

            def queries(f, c):
                if c == 0:
                    pe.wait_ge(w_lo["wq"], 1)
                    split_tiles("x1", f, TH - 1)
                project_t(("q", f, c), w_hl[2], xt_hl, f, c)

            def turn_tile(key, src):
                g = SPLIT_AT[key]
                if g >= SPLIT:
                    pe.wait_ge(split_free, g - (SPLIT - 1))
                for k in range(KD):
                    last = pe.transpose(splitb(g)[:, tile(k)], src[:, tile(k)], ident[:, :])
                last.then_inc(split_ready, 1)

            def turn_normed(ln, f, t):
                n = NORM_AT[ln, f, t]
                if n == 0:
                    pe.wait_ge(consts_ready, 1)
                pe.wait_ge(xn_ready, n + 1)
                turn_tile((f"x{ln + 1}", f, t), xn[:, n % 2, :])

            def scores(f, n):
                if n == 0:
                    pe.wait_ge(acc_free, ACC_AT["q", f, KD - 1] + 1)
                bank = begin("s", f, n)
                t, j = n // 4, n % 4
                r = slice(XD * j, XD * (j + 1))
                for c in range(KD):
                    last = pe.matmul(bank[:, tile(c)], qT[f][r, c, tile(t)], kT[f][r, c, tile(t)],
                                     start=True, stop=True)
                last.then_inc(acc_ready, 1)

            def turn_probs(f, n):
                g = TURN_AT["p", f, n]
                m = f * UNITS + n
                pe.wait_ge(exp_ready, m + 1)
                if g >= TURN:
                    pe.wait_ge(turn_free, g - (TURN - 1))
                for c in range(KD):
                    last = pe.transpose(turnb(g)[:, tile(c)], pbuf[m % SLOTS][:, tile(c)], ident[:, :])
                last.then_inc(turn_ready, 1)

            def attend(f, a):
                t = f * TH + a // 2
                bank = begin("pv", f, a)
                pe.wait_ge(turn_free, TURN_AT["p", f, 2 * a + 1] + 1)
                for u in range(2):
                    for c in range(KD):
                        at = (u * KD + c) * (XD + 1)
                        n = 2 * a + u
                        head = HJ * c + n % 4
                        last = pe.matmul(bank[:, at:at + XD + 1], ptbuf[(f * UNITS + n) % SLOTS][:, tile(c)],
                                         vones[:, t, head, :], start=True, stop=True)
                last.then_inc(acc_ready, 1)

            def turn_attended(f, a):
                n = f * TH + a
                pe.wait_ge(att_ready, 2 * (n + 1))
                pe.wait_ge(acc_free, ACC_AT["pv", f, 2 * a + 1] + 1)
                turn_tile(("at", f, a), attn[n % SLOTS])

            def project_attended(f, a):
                if f == a == 0:
                    pe.wait_ge(w_lo["wo"], 1)
                split_tiles("at", f, a)
                project_n(("wo", f, a), w_hl[3], xt_hl, f * TH + a)

            def spectrum(f, c):
                if c == 0:
                    pe.wait_ge(w_lo["wqkv"], 1)
                    split_tiles("x2", f, TH - 1)
                project_t(("w", f, c), w_hl[0], xt_hl, f, c)

            def logits(f):
                bank = begin("lg", f)
                pe.wait_ge(wn2_first, KD // 2 * (f + 1))
                pe.wait_ge(wn2_last, KD // 2 * (f + 1))
                for t in range(TH):
                    for c in range(KD):
                        last = pe.matmul(bank[:, t * XH:(t + 1) * XH], wn2[f][:, c, tile(t)],
                                         head_sum[:, c, :], start=(c == 0), stop=(c == KD - 1))
                last.then_inc(acc_ready, 1)

            def turn_pi(f):
                g = TURN_AT["pi", f]
                pe.wait_ge(pi_ready, f + 1)
                pe.wait_ge(turn_free, g - (TURN - 1))
                for t in range(TH):
                    last = pe.transpose(turnb(g)[0:XH, tile(t)], pi[f][:, t, :], ident[:, :])
                last.then_inc(turn_ready, 1)

            def spread_pi(f, c):
                if c == 0:
                    pe.wait_ge(spread_ready, 1)
                    pe.wait_ge(turn_free, TURN_AT["pi", f] + 1)
                pe.matmul(begin("pb", f, c)[:, :], head_spread[0:XH, c, :], piT[f][0:XH, :],
                          start=True, stop=True).then_inc(acc_ready, 1)

            def spread_sums(f):
                bank = begin("ps", f)
                pe.wait_ge(pisum_ready, f + 1)
                for c in range(KD):
                    last = pe.matmul(bank[:, c * BH:(c + 1) * BH], head_spread[0:XH, c, :], pi_sum[:, f, :],
                                     start=True, stop=True)
                last.then_inc(acc_ready, 1)

            def mix_out(f, t):
                if t == 0:
                    pe.wait_ge(w_lo["wout"], 1)
                    pe.wait_ge(z_lo, KD * (f + 1))
                project_n(("wout", f, t), w_hl[1], xt_hl, f * TH + t)

            def router_logits(f, t):
                if t == 0:
                    pe.wait_ge(w_lo["sel"], 1)
                    split_tiles("x3", f, TH - 1)
                project_n(("gl", f, t), sel_hl, xt_hl, f * TH + t, P)

            def turn_gates(f):
                g = TURN_AT["go", f]
                pe.wait_ge(gates_o_ready, f + 1)
                pe.wait_ge(turn_free, g - (TURN - 1))
                for t in range(TH):
                    last = pe.transpose(turnb(g)[0:FH * E, tile(t)], gates[:, f * TH + t, FH * E:2 * FH * E],
                                        ident[:, :])
                last.then_inc(turn_ready, 1)

            def bank_of(kind, h, n):
                return accb(ACC_AT[kind + "0", n] if is_head(h, 0) else acc_bank(kind, n))

            def head_qk(h, m):
                begin_acc(acc_at("qk", h, m))
                product(bank_of("qk", h, m), lambda z, k: qk_hl[z][:, m // 2, k, :],
                        lambda z, k: xt_hl[z][:, k, columns(m % 2)]).then_inc(acc_ready, 1)

            def head_values(h, n):
                c, t = n // NT, n % NT
                begin_acc(acc_at("xv", h, n))
                product(bank_of("xv", h, n), lambda z, k: xt_hl[z][:, k, tile(t)],
                        lambda z, k: v_hl[z][:, c, k, :]).then_inc(acc_ready, 1)

            def head_scores(h, f):
                n = split_at(h, f)
                pe.wait_ge(acc_free, acc_at("qk", h, 3) + 1)
                pe.wait_ge(split_free, n - (SPLIT - 1))
                for t in range(TH):
                    q = tile(f * TH + t)
                    last = pe.matmul(splitb(f)[:, tile(t)], qkT[:, 0, q], qkT[:, 1, q], start=True, stop=True)
                last.then_inc(split_ready, 1)

            def head_turn(h, f):
                n = turn_at("p", h, f)
                pe.wait_ge(norm_ready, h * 2 + (f + 1))
                pe.wait_ge(turn_free, n - (TURN - 1))
                for t in range(TH):
                    last = pe.transpose(turnb(f)[:, tile(t)], pbuf[f][:, tile(t)], ident[:, :])
                last.then_inc(turn_ready, 1)

            def head_context(h, f):
                n = turn_at("ctx", h, f)
                pe.wait_ge(acc_free, acc_at("xv", h, NT + TH * (f + 1) - 1) + 1)
                pe.wait_ge(turn_free, n - (TURN - 1))
                for t in range(TH):
                    last = pe.matmul(turnb(f)[:, tile(t)], v_head[:, f * TH + t, :], ptbuf[f][:, tile(t)],
                                     start=True, stop=True)
                last.then_inc(turn_ready, 1)

            def output_tile(h, t, hl):
                begin_acc(acc_at("out", h, t))
                pe.wait_ge(gated_lo, h * NT + (t + 1))
                bank = accb(acc_bank("out", t))
                for e in range(E):
                    for a, b in ((0, 0), (0, 1), (1, 0)):
                        last = pe.matmul(bank[:, :], gated[a][:, t, e, :], hl[b][:, e, :],
                                         start=(e == 0 and (a, b) == (0, 0)), stop=(e == E - 1 and a == 1))
                last.then_inc(acc_ready, 1)

            def step(h):
                pe.wait_ge(vw_lo, h * 3 + 1)
                for m in range(4):
                    head_qk(h, m)
                for c in range(2):
                    pe.wait_ge(vw_lo, h * 3 + (2 + c))
                    for t in range(NT):
                        head_values(h, c * NT + t)
                        if (c, t) in ((0, 1), (0, 3)):
                            head_scores(h, t // 2)
                        if (c, t) in ((1, 1), (1, 3)):
                            head_turn(h, t // 2)
                        if (c, t) == (1, 5):
                            head_context(h, 0)
                pe.wait_ge(ow_lo, h * 2)
                for t in range(NT):
                    output_tile(h - 1, t, o_hl)
                    if t == 1:
                        head_context(h, 1)

            def experts_ready(part):
                pe.wait_ge(vw_lo, part + 1)

            do = {"k": keys, "v": values, "q": queries, "norm": turn_normed, "s": scores, "p": turn_probs,
                  "pv": attend, "at": turn_attended, "wo": project_attended, "w": spectrum, "lg": logits,
                  "pi": turn_pi, "pb": spread_pi, "ps": spread_sums, "wout": mix_out, "gl": router_logits,
                  "go": turn_gates, "ew": experts_ready, "qk0": lambda m: head_qk(0, m),
                  "xv0": lambda n: head_values(0, n), "hs": lambda f: head_scores(0, f),
                  "hp": lambda f: head_turn(0, f), "hc": lambda f: head_context(0, f)}
            for kind, *a in FRONT:
                if kind in do:
                    do[kind](*a)
            with pe.Fori(1, FH - 1) as h:
                step(h)
            step(FH - 1)
            pe.wait_ge(ow_lo, 2 * FH)
            for t in range(NT):
                output_tile(FH - 1, t, o_hl_last)


_OUT = (N, D)


def kernel(**inputs):
    import numpy as np
    import concourse.bacc as bacc
    from concourse.bass_utils import run_bass_kernel_spmd

    a = {k: np.asarray(v) for k, v in inputs.items()}
    lay = np.ascontiguousarray
    heads = FH
    q = a["L0_ffn_q_w"].reshape(heads, P, KD, P)
    k = a["L0_ffn_k_w"].reshape(heads, P, KD, P)
    qk = np.stack([q, k], 1).transpose(0, 4, 1, 3, 2).reshape(heads, P, 2 * KD * P)
    v = a["L0_ffn_v_w"].reshape(heads, 2, EC, KD, P, P).transpose(0, 4, 1, 3, 2, 5).reshape(heads, P, KD * E * P)
    o = a["L0_ffn_o_w"].reshape(heads, E, P, D).transpose(0, 2, 1, 3).reshape(heads, P, E * D)
    arrays = {
        "x": a["x"].reshape(N, D),
        "ctx_t": a["ctx_1024"][:, :T].reshape(N, D).T,
        "wk": a["L0_xattn_Wk"], "wv": a["L0_xattn_Wv"], "wq": a["L0_xattn_Wq"], "wo": a["L0_xattn_Wo"],
        "wqkv_t": a["L0_attn_Wqkv"].T, "wout_t": a["L0_attn_Wout"].T,
        "sel_v_t": a["L0_ffn_sel_v_w"].T, "sel_o_t": a["L0_ffn_sel_o_w"].T,
        "qk_t": qk, "v_w": v, "o_w": o,
        "bq": a["L0_xattn_bq"].reshape(KD, P).T, "bk": a["L0_xattn_bk"].reshape(KD, P).T,
        "bv": a["L0_xattn_bv"], "bo": a["L0_xattn_bo"], "bout": a["L0_attn_bout"],
        "temp": a["L0_attn_temp"].reshape(XH), "route_scale": a["L0_ffn_route_scale"],
    }
    arrays = {n: lay(v) for n, v in arrays.items()}
    nc = bacc.Bacc("TRN2", target_bir_lowering=False, num_devices=1)
    args = [nc.dram_tensor(n, v.shape, mybir.dt.from_np(v.dtype), kind="ExternalInput").ap()
            for n, v in arrays.items()]
    names = list(arrays)
    byname = dict(zip(names, args))
    out = nc.dram_tensor("out", _OUT, F32, kind="ExternalOutput").ap()
    gate_dram = nc.dram_tensor("gate_dram", (FH * E, N), F32, kind="Internal").ap()
    perceiver_kernel(nc, out=out, gate_dram=gate_dram, **byname)
    r = run_bass_kernel_spmd(nc, [arrays], core_ids=[0])
    return r.results[0]["out"].reshape(B, T, D)
```
